# Optimizing a Trainium2 kernel written in Bass

```python
import numpy as np
import jax
import jax.numpy as jnp

def _softmax(x, axis=-1):
    return jax.nn.softmax(x, axis=axis)

def _gelu(x):
    return jax.nn.gelu(x, approximate=True)

def _silu(x):
    return jax.nn.silu(x)

def _sigmoid(x):
    return jax.nn.sigmoid(x)

def _layernorm(x, axis=-1, eps=1e-05):
    m = jnp.mean(x, axis=axis, keepdims=True)
    v = jnp.var(x, axis=axis, keepdims=True)
    return (x - m) / jnp.sqrt(v + eps)

def _scatter_add(tgt, idx, src, axis=0):
    return tgt.at[idx].add(src)

def _segment_sum(src, seg, n):
    return jax.ops.segment_sum(src, seg, n)
kernel_name = 'mk_decoder_postln_d1_seqx_r2_f0848a'

def setup_inputs(seed: int=0):
    np.random.seed(seed)
    _w = jnp.asarray

    def _rec_inputs():
        import jax
        import jax.numpy as jnp
        _rk = jax.random.key(seed)
        x = -0.0003929 + 0.9999 * jax.random.normal(jax.random.fold_in(_rk, 1), (16, 256, 2048), jnp.float32)
        _lenS = 256 - jax.random.randint(jax.random.fold_in(_rk, 7), (16,), 0, max(1, 256 // 4) + 1, jnp.int32)
        _lenS2 = 256 - jax.random.randint(jax.random.fold_in(_rk, 8), (16,), 0, max(1, 256 // 4) + 1, jnp.int32)
        _ctx_4096P = jax.random.normal(jax.random.fold_in(_rk, 11), (16, 16, 2048), jnp.float32)
        _ctx_4096c = jax.random.dirichlet(jax.random.fold_in(_rk, 511), 0.3 * jnp.ones((16,), jnp.float32), (16, 256))
        _ctx_4096t = jnp.einsum('bsk,bkd->bsd', _ctx_4096c, _ctx_4096P)
        _ctx_4096t = _ctx_4096t * jax.lax.rsqrt(jnp.mean(jnp.square(_ctx_4096t)) + 1e-12) * 0.953939
        ctx_4096 = 2.81802e-05 + 1.00001 * (_ctx_4096t + 0.3 * jax.random.normal(jax.random.fold_in(_rk, 611), (16, 256, 2048), jnp.float32))
        return (x, ctx_4096)
    x, ctx_4096 = _rec_inputs()

    def _L0_attn_setup():
        import jax, jax.numpy as jnp
        import numpy as np
        HDC_DIM = 2048
        N_HEADS = 4
        HEAD_DIM = HDC_DIM // N_HEADS

        def _ste_sign(w):
            alpha = jnp.mean(jnp.abs(w), axis=-1, keepdims=True)
            hard = alpha * jnp.sign(w)
            hard = jnp.where(hard == 0, alpha, hard)
            return jax.lax.stop_gradient(hard - w) + w
        key = jax.random.key(seed)
        kx, kq, kk, kv = jax.random.split(key, 4)
        B, T = (4, 1024)
        x = jax.random.normal(kx, (B, T, HDC_DIM), dtype=jnp.float32)
        bv_q = jax.random.normal(kq, (N_HEADS, HEAD_DIM), dtype=jnp.float32) * 0.02
        bv_k = jax.random.normal(kk, (N_HEADS, HEAD_DIM), dtype=jnp.float32) * 0.02
        bv_v = jax.random.normal(kv, (N_HEADS, HEAD_DIM), dtype=jnp.float32) * 0.02
        return {'x': x, 'bv_q': bv_q, 'bv_k': bv_k, 'bv_v': bv_v}
    _L0_attn_all = _L0_attn_setup()
    _L0_attn_in = {k: v for k, v in _L0_attn_all.items() if k in ('bv_q', 'bv_k', 'bv_v')}
    del _L0_attn_all

    def _L0_xattn_setup():
        import jax, jax.numpy as jnp
        import numpy as np
        DIM = 256
        HEADS = 8
        DIM_HEAD = 64
        HIDDEN = HEADS * DIM_HEAD
        SCALE = DIM_HEAD ** (-0.5)
        key = jax.random.key(seed)
        ks = jax.random.split(key, 9)
        b, n = (8, 2048)
        std = 1.0 / np.sqrt(DIM)
        return {'q': jax.random.normal(ks[0], (b, DIM, n), jnp.float32), 'k': jax.random.normal(ks[1], (b, DIM, n), jnp.float32), 'v': jax.random.normal(ks[2], (b, DIM, n), jnp.float32), 'Wq': jax.random.normal(ks[3], (HIDDEN, DIM), jnp.float32) * std, 'Wk': jax.random.normal(ks[4], (HIDDEN, DIM), jnp.float32) * std, 'Wv': jax.random.normal(ks[5], (HIDDEN, DIM), jnp.float32) * std, 'Wo': jax.random.normal(ks[6], (DIM, HIDDEN), jnp.float32) * (1.0 / np.sqrt(HIDDEN)), 'bo': jax.random.normal(ks[7], (DIM,), jnp.float32) * 0.01, 'g': jnp.ones((1, DIM, 1), jnp.float32)}
    _L0_xattn_all = _L0_xattn_setup()
    _L0_xattn_in = {k: v for k, v in _L0_xattn_all.items() if k in ('Wq', 'Wk', 'Wv', 'Wo', 'bo', 'g')}
    del _L0_xattn_all

    def _L0_ffn_setup():
        import jax, jax.numpy as jnp
        import numpy as np
        LORA_SCALE = 16.0 / jnp.sqrt(16.0)
        TOP_K = 2
        key = jax.random.key(seed)
        k1, k2, k3, k4 = jax.random.split(key, 4)
        B_, S, D, O, E, R = (4, 1024, 2048, 2048, 4, 16)
        x = jax.random.normal(k1, (B_, S, D), dtype=jnp.float32)
        router_w = jax.random.normal(k2, (E, D), dtype=jnp.float32) * 0.02
        A = jax.random.normal(k3, (E, R, D), dtype=jnp.float32) * 0.02
        B = jax.random.normal(k4, (O,), dtype=jnp.float32)
        B = jax.random.normal(k4, (E, O, R), dtype=jnp.float32) * 0.02
        return {'x': x, 'router_w': router_w, 'A': A, 'B': B}
    _L0_ffn_all = _L0_ffn_setup()
    _L0_ffn_in = {k: v for k, v in _L0_ffn_all.items() if k in ('router_w', 'A', 'B')}
    del _L0_ffn_all
    return {'x': x, 'ctx_4096': ctx_4096, 'L0_attn_bv_q': _L0_attn_in['bv_q'], 'L0_attn_bv_k': _L0_attn_in['bv_k'], 'L0_attn_bv_v': _L0_attn_in['bv_v'], 'L0_xattn_Wq': _L0_xattn_in['Wq'], 'L0_xattn_Wk': _L0_xattn_in['Wk'], 'L0_xattn_Wv': _L0_xattn_in['Wv'], 'L0_xattn_Wo': _L0_xattn_in['Wo'], 'L0_xattn_bo': _L0_xattn_in['bo'], 'L0_xattn_g': _L0_xattn_in['g'], 'L0_ffn_router_w': _L0_ffn_in['router_w'], 'L0_ffn_A': _L0_ffn_in['A'], 'L0_ffn_B': _L0_ffn_in['B']}

def reference(x, ctx_4096, L0_attn_bv_q, L0_attn_bv_k, L0_attn_bv_v, L0_xattn_Wq, L0_xattn_Wk, L0_xattn_Wv, L0_xattn_Wo, L0_xattn_bo, L0_xattn_g, L0_ffn_router_w, L0_ffn_A, L0_ffn_B):
    import jax
    import jax.numpy as jnp

    def _L0_attn_ref(x, bv_q, bv_k, bv_v):
        import jax, jax.numpy as jnp
        import numpy as np
        HDC_DIM = 2048
        N_HEADS = 4
        HEAD_DIM = HDC_DIM // N_HEADS

        def _ste_sign(w):
            alpha = jnp.mean(jnp.abs(w), axis=-1, keepdims=True)
            hard = alpha * jnp.sign(w)
            hard = jnp.where(hard == 0, alpha, hard)
            return jax.lax.stop_gradient(hard - w) + w
        B, T, D = x.shape
        H, HD = (N_HEADS, HEAD_DIM)
        scale = HD ** (-0.5)
        q_bind = _ste_sign(bv_q)
        k_bind = _ste_sign(bv_k)
        v_bind = _ste_sign(bv_v)
        xh = x.reshape(B, T, H, HD)
        Q = xh * q_bind
        K = xh * k_bind
        V = xh * v_bind
        scores = jnp.einsum('bthd,bshd->bhts', Q, K) * scale
        causal = jnp.tril(jnp.ones((T, T), dtype=bool))
        attn = jnp.where(causal, jax.nn.sigmoid(scores * 4.0), 0.0)
        out = jnp.einsum('bhts,bshd->bthd', attn, V)
        return out.reshape(B, T, D)

    def _L0_xattn_ref(q, k, v, Wq, Wk, Wv, Wo, bo, g):
        import jax, jax.numpy as jnp
        import numpy as np
        DIM = 256
        HEADS = 8
        DIM_HEAD = 64
        HIDDEN = HEADS * DIM_HEAD
        SCALE = DIM_HEAD ** (-0.5)
        b = q.shape[0]
        qh = jnp.einsum('bcn,oc->bon', q, Wq).reshape(b, HEADS, DIM_HEAD, -1)
        kh = jnp.einsum('bcn,oc->bon', k, Wk).reshape(b, HEADS, DIM_HEAD, -1)
        vh = jnp.einsum('bcn,oc->bon', v, Wv).reshape(b, HEADS, DIM_HEAD, -1)
        qh = jax.nn.softmax(qh, axis=-2) * SCALE
        kh = jax.nn.softmax(kh, axis=-1)
        context = jnp.einsum('bhdn,bhen->bhde', kh, vh)
        out = jnp.einsum('bhde,bhdn->bhen', context, qh)
        out = out.reshape(b, HIDDEN, -1)
        out = jnp.einsum('bcn,oc->bon', out, Wo) + bo[None, :, None]
        norm = jnp.maximum(jnp.sqrt(jnp.sum(out * out, axis=1, keepdims=True)), 1e-12)
        return out / norm * g * np.sqrt(DIM)

    def _L0_ffn_ref(x, router_w, A, B):
        import jax, jax.numpy as jnp
        import numpy as np
        LORA_SCALE = 16.0 / jnp.sqrt(16.0)
        TOP_K = 2
        D = x.shape[-1]
        flat = x.reshape(-1, D)
        logits = flat @ router_w.T
        topk_vals, topk_idx = jax.lax.top_k(logits, TOP_K)
        sparse = jnp.full_like(logits, -jnp.inf)
        rows = jnp.arange(logits.shape[0])[:, None]
        sparse = sparse.at[rows, topk_idx].set(topk_vals)
        gates = jax.nn.softmax(sparse, axis=-1)
        mid = jnp.einsum('tf,erf->ter', flat, A)
        all_deltas = jnp.einsum('ter,eor->teo', mid, B) * LORA_SCALE
        delta = jnp.einsum('te,teo->to', gates, all_deltas)
        return delta.reshape(*x.shape[:-1], -1)
    x = _layernorm(x + _L0_attn_ref(x, L0_attn_bv_q, L0_attn_bv_k, L0_attn_bv_v), axis=-1)
    x = _layernorm(x + _L0_xattn_ref(x, ctx_4096, ctx_4096, L0_xattn_Wq, L0_xattn_Wk, L0_xattn_Wv, L0_xattn_Wo, L0_xattn_bo, L0_xattn_g), axis=-1)
    x = _layernorm(x + _L0_ffn_ref(x, L0_ffn_router_w, L0_ffn_A, L0_ffn_B), axis=-1)
    return x

_drawn_inputs = setup_inputs


def setup_inputs(seed=0):
    import zlib

    import numpy as np

    out = dict(_drawn_inputs(seed))
    spreads = {'L0_xattn_g': (1.0, 0.2)}
    factors = {'L0_attn_bv_q': 64.0, 'L0_attn_bv_k': 64.0}
    for name, (base, spread) in spreads.items():
        noise = np.random.default_rng([zlib.crc32(name.encode()), seed]).standard_normal(out[name].shape)
        drawn = base * np.exp(spread * noise) if base else spread * noise
        out[name] = jnp.asarray(drawn.astype(out[name].dtype))
    for name, factor in factors.items():
        out[name] = (out[name] * factor).astype(out[name].dtype)
    return out
```

```python
from contextlib import ExitStack

import numpy as np

import concourse.bass as bass
from concourse import mybir

F32 = mybir.dt.float32
F32R = mybir.dt.float32r
ACT = mybir.ActivationFunctionType
ALU = mybir.AluOpType
AX = mybir.AxisListType

P = 128
B, T, D = 16, 256, 2048
H, HD = 4, 512
CT_, NT_, DT_ = T // P, D // P, HD // P
HID, LH, LD = 512, 8, 64
OT_ = HID // P
E, R, ER = 4, 16, 64
TOP_K = 2
ARW = ER + E
CH = 4
LN_EPS = 1e-5
LORA_SCALE = 16.0 / 16.0 ** 0.5
HI, LO = 0, 1



def bank_of(stage, n, m=0):
    return {"qk": 4, "x2t": 6 + n % 2, "mid": 5, "k": m, "midt": 4, "av": 6 + m, "et": 6 + m % 2, "g": 5,
            "gated": 4, "mt": 4, "delta": 6 + n % 2, "q": n % 3, "qt": 3 + n % 2, "y": 5, "yt": 6 + n % 2}[stage]


def products(ffn, rest):
    def heads(s, n, k):
        return [(s, n, m) for m in range(k)]

    ffn_a = [("x2t", j, 0) for j in range(8)] + [("mid", 0, 0)] if ffn else []
    midt = [("midt", 0, 0)] if ffn else []
    ffn_b = [("gated", 0, 0)] if ffn else []
    ffn_c = [("delta", k, 0) for k in range(8)] if ffn else []
    if not rest:
        return ffn_a + midt + ffn_b + ffn_c
    out = [("qk", 0, 0)] + ffn_a + heads("k", 0, 4) + midt + heads("av", 0, 2) + [("qk", 1, 0)]
    out += heads("et", 0, 4) + [("g", 0, 0)] + ffn_b + heads("k", 1, 4) + heads("mt", 0, 3) + ffn_c
    out += heads("av", 1, 2) + [("qk", 2, 0)] + heads("et", 1, 4) + [("g", 1, 0)]
    out += heads("av", 2, 2) + [("qk", 3, 0)] + heads("k", 2, 4) + heads("mt", 1, 3) + heads("av", 3, 2)
    out += heads("et", 2, 4) + [("g", 2, 0)] + heads("k", 3, 4) + heads("mt", 2, 3)
    out += heads("et", 3, 4) + [("g", 3, 0)] + heads("mt", 3, 3)
    for s in range(NT_):
        out += [("q", s, 0), ("qt", s, 0), ("y", s, 0)]
    return out + [("yt", p, 0) for p in range(NT_ // 2)]


def uses(order):
    count, at = [0] * 8, {}
    for job in order:
        b = bank_of(*job)
        count[b] += 1
        at[job] = count[b]
    return count, at


FIRST, FIRST_AT = uses(products(False, True))
EACH, EACH_AT = uses(products(True, True))
_, END_AT = uses(products(True, False))


def use_number(i, stage, n=0, m=0):
    job = (stage, n, m)
    b = bank_of(*job)
    if isinstance(i, int) and i == 0:
        return FIRST_AT[job]
    if isinstance(i, int) and i == B:
        return FIRST[b] + (B - 1) * EACH[b] + END_AT[job]
    return i * EACH[b] + (FIRST[b] - EACH[b] + EACH_AT[job])


def use_before(i, stage, n=0, m=0):
    b = bank_of(stage, n, m)
    if isinstance(i, int) and i == 0:
        return None
    return i * EACH[b] + (FIRST[b] - 2 * EACH[b] + EACH_AT[(stage, n, m)])


def build(nc, x, xt, ctx, ctxt, bv_q, bv_k, bv_v, bq_col, bk_col, wqt, wkt, wvt, wot, bo, g, art, bt, out):
    with ExitStack() as stack:
        def sb(name, shape, dt=F32):
            return stack.enter_context(nc.sbuf_tensor(name, shape, dt))

        def sem(name):
            return stack.enter_context(nc.semaphore(name))

        wq = sb("wq", [P, CT_, 2, HID], F32R)
        wk = sb("wk", [P, CT_, 2, HID], F32R)
        wv = sb("wv", [P, CT_, HID])
        wo = sb("wo", [P, OT_, T])
        ar = sb("ar", [P, NT_, 2, ARW], F32R)
        b2 = sb("b2", [P, D], F32R)
        vb = sb("vb", [P, D])
        dcol = sb("dcol", [P, NT_])
        kcol = sb("kcol", [P, NT_])
        bob = sb("bob", [P, T])
        ident = sb("ident", [P, P])
        halfmask = sb("halfmask", [P, 3, P])
        pairmask = sb("pairmask", [P, P])
        before = sb("before", [P, E, E])
        minus_half = sb("minus_half", [P, 2])
        g16 = sb("g16", [P, CT_])
        alpha = sb("alpha", [P, 3, H])
        ste = sb("ste", [P, 4, NT_])

        xa = sb("xa", [P, CT_, D])
        x2 = sb("x2", [P, CT_, D])
        raw = sb("raw", [P, 2, 1024])
        xt_part = sb("xt_part", [P, 2, 2, 2, T], F32R)
        xd_part = sb("xd_part", [P, 2, 2, 2, T], F32R)
        xn_part = sb("xn_part", [P, 2, CT_, HD], F32R)
        prob = sb("prob", [P, 3, P])
        prob_part = sb("prob_part", [P, 2, 3, P], F32R)
        c_part = sb("c_part", [P, 2, CT_, D], F32R)
        ct_part = sb("ct_part", [P, NT_, 2, T], F32R)
        e_buf = sb("e_buf", [P, D])
        t_part = sb("t_part", [P, 2, 2, 512], F32R)
        m_part = sb("m_part", [P, OT_, 2, T], F32R)
        avt = sb("avt", [P, CT_, HD])
        ybuf = sb("ybuf", [P, 4, T])
        gs = sb("gs", [P, T])
        gt = sb("gt", [P, CT_, P])
        cx = sb("cx", [P, P])
        midt = ybuf[:, 0, :]
        md = sb("md", [P, CT_, ARW])
        gated = ybuf[:, 1, :].rearrange("p (t a e) -> p t a e", t=CT_, a=2)
        gated_part = m_part[:, OT_ - 1, :, :].rearrange("p s (t n) -> p s t n", t=CT_)
        kmax4 = sb("kmax4", [P, CH])
        kjunk = sb("kjunk", [P, CH])
        knmax = sb("knmax", [P, 1])
        kden4 = sb("kden4", [P, CH])
        kden = sb("kden", [P, 1])
        krden = sb("krden", [P, 1])
        qmax = sb("qmax", [P, 2, LH])
        qden = sb("qden", [P, 2, LH])
        qrden = sb("qrden", [P, 2, LH])
        yss = sb("yss", [P, 2, 2])
        ln_gate = sb("ln_gate", [P, 1])
        yssm = sb("yssm", [P, 2])
        yr = sb("yr", [P, 2, 2])
        stats = sb("stats", [P, 3, CT_, CH, 6])
        mv = sb("mv", [P, 3, CT_, 2])
        ve = sb("ve", [P, 3, CT_])
        rstd = sb("rstd", [P, 3, CT_])
        nmr = sb("nmr", [P, 3, CT_])
        ggt = sb("ggt", [P, CT_, E, E])
        geq = sb("geq", [P, CT_, E, E])
        grank = sb("grank", [P, CT_, E])
        gmax = sb("gmax", [P, CT_])
        gdif = sb("gdif", [P, CT_, E])
        gexp = sb("gexp", [P, CT_, E])
        gsum = sb("gsum", [P, CT_])

        ps = [stack.enter_context(nc.psum_tensor(f"bank{b}", [P, 512], F32)) for b in range(8)]

        def bank(stage, n=0, m=0):
            return ps[bank_of(stage, n, m)]

        bank_full = [sem(f"bank_full{b}") for b in range(8)]
        bank_free = [sem(f"bank_free{b}") for b in range(8)]

        def full(i, stage, n=0, m=0):
            return bank_full[bank_of(stage, n, m)], use_number(i, stage, n, m)

        def freed(i, stage, n=0, m=0):
            return bank_free[bank_of(stage, n, m)], use_number(i, stage, n, m)

        consts_loaded = sem("consts_loaded")
        ident_made = sem("ident_made")
        pool_made = sem("pool_made")
        setup_abs = sem("setup_abs")
        setup_dve = sem("setup_dve")
        setup_done = sem("setup_done")
        raw_loaded = [sem(f"raw_loaded{k}") for k in range(2)]
        raw_used = sem("raw_used")
        x_loaded = [sem(f"x_loaded{k}") for k in range(CH)]
        stored = sem("stored")
        xt_hi, xt_d, xt_lo = sem("xt_hi"), sem("xt_d"), sem("xt_lo")
        qk_half = sem("qk_half")
        xn_hi, xn_lo = sem("xn_hi"), sem("xn_lo")
        prob_step, prob_ready = sem("prob_step"), sem("prob_ready")
        xt_dhi = sem("xt_dhi")
        c_hi, c_lo = sem("c_hi"), sem("c_lo")
        ct_hi, ct_lo = sem("ct_hi"), sem("ct_lo")
        kmax_step, kmax_ready = sem("kmax_step"), sem("kmax_ready")
        kden_step, krden_ready = sem("kden_step"), sem("krden_ready")
        et_hi, g_chunk = sem("et_hi"), sem("g_chunk")
        m_hi = sem("m_hi")
        res_added = sem("res_added")
        ln_stats = [sem(f"ln_stats{k}") for k in range(3)]
        ln_var = [sem(f"ln_var{k}") for k in range(3)]
        ln_rstd = [sem(f"ln_rstd{k}") for k in range(3)]
        ln_nmr = [sem(f"ln_nmr{k}") for k in range(3)]
        ln_done = [sem(f"ln_done{k}") for k in range(3)]
        x1_hi, x1_lo = sem("x1_hi"), sem("x1_lo")
        q_max, q_exp, q_sum, q_rden, q_norm = sem("q_max"), sem("q_exp"), sem("q_sum"), sem("q_rden"), sem("q_norm")
        qt_hi = sem("qt_hi")
        y_squared, y_guard, y_r, y_scaled = sem("y_squared"), sem("y_guard"), sem("y_r"), sem("y_scaled")
        x2t_hi, mid_used = sem("x2t_hi"), sem("mid_used")
        gate_step, gate_diff, gate_exp, gated_ready = sem("gate_step"), sem("gate_diff"), sem("gate_exp"), sem("gated_ready")
        gated_hi, gate_norm = sem("gated_hi"), sem("gate_norm")
        gate_order = sem("gate_order")
        delta_added = sem("delta_added")

        RAW = [("xt", 0)] + [("c", k) for k in range(4)] + [("xt", 1)] + [("ct", k) for k in range(4)] \
            + [("xt", 2), ("xt", 3)]
        NRAW = len(RAW)

        def raw_slot(kind, k):
            return raw[:, RAW.index((kind, k)) % 2, :]

        def raw_arrived(i, kind, k):
            n = RAW.index((kind, k))
            return raw_loaded[n % 2], i * (16 * NRAW // 2) + 16 * (n // 2 + 1)

        block = stack.enter_context(nc.Block())

        def rounds(engine_type, one):
            one(0, False, True)
            with nc.Fori(1, B, engines=(engine_type,), hint_back_edge=True) as i:
                one(i, True, True)
            one(B, True, False)

        @block.sync
        def _(sp):
            staged = x2[:, 0, :].rearrange("p (a n) -> p a n", a=2)
            for dst, src in ((staged[:, 0, :], wqt), (staged[:, 1, :], wkt), (wv[:], wvt), (wo[:], wot),
                             (xa[:, 0, 0:NT_ * ARW], art), (x2[:, 1, :], bt), (vb[:], bv_v), (e_buf[:], bv_q),
                             (xa[:, 1, :], bv_k), (ste[:, 0, :], bq_col), (ste[:, 1, :], bk_col),
                             (bob[:], bo), (g16[:], g)):
                sp.dma_start(dst, src).then_inc(consts_loaded, 16)

            def load_raw(i, kind, k):
                n = RAW.index((kind, k))
                if not (isinstance(i, int) and i == 0 and n < 2):
                    sp.wait_ge(raw_used, i * NRAW + (n - 1))
                src = {"xt": xt, "c": ctx, "ct": ctxt}[kind]
                sp.dma_start(raw[:, n % 2, :], src[i, k]).then_inc(raw_loaded[n % 2], 16)

            def one(i, ffn, rest):
                if rest:
                    for kind, k in RAW[:6]:
                        load_raw(i, kind, k)
                        if kind == "xt" and k == 0:
                            for h in range(H):
                                if isinstance(i, int):
                                    sp.wait_ge(setup_done, 1)
                                else:
                                    sp.wait_ge(bank_free[bank_of("yt", 2 * h + 1)], use_before(i, "yt", 2 * h + 1))
                                sp.dma_start(xa[:, :, h * HD:(h + 1) * HD], x[i, h]).then_inc(x_loaded[h], 16)
                    for kind, k in RAW[6:11]:
                        load_raw(i, kind, k)
                if ffn:
                    for t in range(CT_):
                        sp.wait_ge(ln_done[2], (i - 1) * CT_ + t + 1)
                        sp.dma_start(out[i - 1, t], x2[:, t, :]).then_inc(stored, 16)
                if rest:
                    load_raw(i, *RAW[11])

            rounds(mybir.EngineType.SP, one)
            sp.wait_ge(stored, 16 * CT_ * B)

        @block.tensor
        def _(pe):
            mm = nc.tensor.matmul

            def free(i, stage, n=0, m=0):
                v = use_number(i, stage, n, m) - 1
                if not (isinstance(v, int) and v <= 0):
                    pe.wait_ge(bank_free[bank_of(stage, n, m)], v)

            def three(dst, stat, mov, first, last):
                mm(dst, stat(HI), mov(HI), start=first, stop=False)
                mm(dst, stat(HI), mov(LO), start=False, stop=False)
                return mm(dst, stat(LO), mov(HI), start=False, stop=last)

            def qk(i, h):
                free(i, "qk", h)
                dst = bank("qk", h)
                for half in range(2):
                    pe.wait_ge(xt_lo, i * 8 + 2 * h + half + 1)
                    pe.wait_ge(xt_d, i * 8 + 2 * h + half + 1)
                    for dt in range(2):
                        for s in range(CT_):
                            def stat(p):
                                return xt_part[:, half, p, dt, s * P:(s + 1) * P]

                            def mov(p):
                                return xd_part[:, half, p, dt, :]
                            o = dst[:, s * T:(s + 1) * T]
                            first = half == 0 and dt == 0 and s == 0
                            mm(o, stat(HI), mov(HI), start=first, stop=False, skip_group_check=True)
                            mm(o, stat(HI), mov(LO), start=False, stop=False, skip_group_check=True)
                            last = mm(o, stat(LO), mov(HI), start=False, stop=half == 1 and dt == 1,
                                      skip_group_check=True)
                    last.then_inc(qk_half if half == 0 else bank_full[bank_of("qk", h)], 1)

            def av(i, h):
                pe.wait_ge(prob_ready, i * H + h + 1)
                pe.wait_ge(xn_lo, i * H + h + 1)
                for t in range(CT_):
                    free(i, "av", h, t)
                    for s in range(t + 1):
                        last = three(bank("av", h, t)[:, :], lambda p: prob_part[:, p, s + t, :],
                                     lambda p: xn_part[:, p, s, :], s == 0, s == t)
                    last.then_inc(bank_full[bank_of("av", h, t)], 1)

            def kproj(i, h, between=()):
                for c in range(CH):
                    if h == 0:
                        pe.wait_ge(c_lo, i * CH + c + 1)
                    free(i, "k", h, c)
                    for k in range(CT_):
                        last = three(bank("k", h, c)[:, :], lambda p: wk[:, k, p, h * P:(h + 1) * P],
                                     lambda p: c_part[:, p, k, c * 512:(c + 1) * 512], k == 0, k == CT_ - 1)
                    last.then_inc(bank_full[bank_of("k", h, c)], 1)
                    for at, what in between:
                        if at == c:
                            what()

            def tg(i, h):
                def products_of(c):
                    if h == 0:
                        pe.wait_ge(ct_lo, i * CH + c + 1)
                    if c == 0:
                        free(i, "g", h)
                    pe.wait_ge(*freed(i, "et", h, c))
                    for n in range(4):
                        last = three(bank("g", h)[:, 0:T], lambda p: t_part[:, c % 2, p, n * P:(n + 1) * P],
                                     lambda p: ct_part[:, 4 * c + n, p, :], c == 0 and n == 0, c == 3 and n == 3)
                    last.then_inc(g_chunk if c < 3 else bank_full[bank_of("g", h)], 1)

                for c in range(CH):
                    pe.wait_ge(*freed(i, "k", h, c))
                    free(i, "et", h, c)
                    for n in range(4):
                        last = nc.tensor.transpose(bank("et", h, c)[:, n * P:(n + 1) * P],
                                                   e_buf[:, (4 * c + n) * P:(4 * c + n + 1) * P], ident[:])
                    last.then_inc(bank_full[bank_of("et", h, c)], 1)
                    if c > 0:
                        products_of(c - 1)
                products_of(3)

            def mt(i, h, s):
                free(i, "mt", h, s)
                dst = bank("mt", h, s)
                if s == 0:
                    pe.wait_ge(*freed(i, "g", h))
                    for k in range(CT_):
                        last = nc.tensor.transpose(dst[:, k * P:(k + 1) * P], gs[:, k * P:(k + 1) * P], ident[:])
                elif s == 1:
                    for k in range(CT_):
                        last = mm(dst[:, 0:P], wv[:, k, h * P:(h + 1) * P], gt[:, k, :], start=k == 0,
                                  stop=k == CT_ - 1)
                else:
                    last = mm(dst[:, 0:T], cx[:], wo[:, h, :], start=True, stop=True)
                last.then_inc(bank_full[bank_of("mt", h, s)], 1)

            def x2_down(i):
                def mid_of(j):
                    pe.wait_ge(*freed(i, "x2t", j))
                    if j == 0:
                        free(i, "mid")
                    for dt in range(2):
                        last = three(bank("mid")[0:ARW, 0:T], lambda p: ar[:, 2 * j + dt, p, :],
                                     lambda p: t_part[:, j % 2, p, dt * T:(dt + 1) * T],
                                     j == 0 and dt == 0, j == 7 and dt == 1)
                    last.then_inc(mid_used if j < 7 else bank_full[bank_of("mid", 0)], 1)

                for j in range(8):
                    pe.wait_ge(ln_done[1], (i - 1) * 8 + 2 * (j // 2) + 2)
                    free(i, "x2t", j)
                    for dt in range(2):
                        for t in range(CT_):
                            o = (dt * CT_ + t) * P
                            last = nc.tensor.transpose(bank("x2t", j)[:, o:o + P],
                                                       x2[:, t, (2 * j + dt) * P:(2 * j + dt + 1) * P], ident[:])
                    last.then_inc(bank_full[bank_of("x2t", j)], 1)
                    if j > 0:
                        mid_of(j - 1)
                mid_of(7)

            def mid_transpose(i):
                pe.wait_ge(*freed(i, "mid"))
                free(i, "midt")
                for t in range(CT_):
                    last = nc.tensor.transpose(bank("midt")[:, t * P:t * P + ARW], midt[0:ARW, t * P:(t + 1) * P],
                                               ident[0:ARW, 0:ARW])
                last.then_inc(bank_full[bank_of("midt", 0)], 1)

            def gated_transpose(i):
                pe.wait_ge(gated_ready, i * 4)
                free(i, "gated")
                for t in range(CT_):
                    last = nc.tensor.transpose(bank("gated")[:, t * P:(t + 1) * P],
                                               gated[:, t, :, :].rearrange("p a e -> p (a e)"), ident[:])
                last.then_inc(bank_full[bank_of("gated", 0)], 1)

            def delta(i):
                pe.wait_ge(*freed(i, "gated"))
                for k in range(8):
                    t, c = divmod(k, CH)
                    free(i, "delta", k)
                    for p in (HI, LO):
                        last = mm(bank("delta", k)[:, :], gated_part[:, p, t, :], b2[:, c * 512:(c + 1) * 512],
                                  start=p == HI, stop=p == LO)
                    last.then_inc(bank_full[bank_of("delta", k)], 1)

            def linear(i):
                for s in range(NT_ + 7):
                    if s < NT_:
                        if s % 4 == 0:
                            pe.wait_ge(x1_lo, i * CH + s // 4 + 1)
                        free(i, "q", s)
                        for k in range(CT_):
                            last = three(bank("q", s)[:, :], lambda p: c_part[:, p, k, s * P:(s + 1) * P],
                                         lambda p: wq[:, k, p, :], k == 0, k == CT_ - 1)
                        last.then_inc(bank_full[bank_of("q", s)], 1)
                    if s < 3:
                        mt(i, 3, s)
                    n = s - 2
                    if 0 <= n < NT_:
                        pe.wait_ge(q_norm, i * NT_ + n + 1)
                        free(i, "qt", n)
                        for j in range(OT_):
                            last = nc.tensor.transpose(bank("qt", n)[:, j * P:(j + 1) * P],
                                                       e_buf[:, (n % 3) * 512 + j * P:(n % 3) * 512 + (j + 1) * P],
                                                       ident[:])
                        last.then_inc(bank_full[bank_of("qt", n)], 1)
                    n = s - 3
                    if 0 <= n < NT_:
                        pe.wait_ge(*freed(i, "qt", n))
                        if n == 0:
                            pe.wait_ge(*freed(i, "mt", 3, 2))
                        free(i, "y", n)
                        for j in range(OT_):
                            last = three(bank("y", n)[:, 0:T], lambda p: t_part[:, n % 2, p, j * P:(j + 1) * P],
                                         lambda p: m_part[:, j, p, :], j == 0, j == OT_ - 1)
                        last.then_inc(bank_full[bank_of("y", n)], 1)
                    n = s - 6
                    if n >= 0 and n % 2 == 0 and n < NT_:
                        q = n // 2
                        pe.wait_ge(y_scaled, i * NT_ + n + 2)
                        free(i, "yt", q)
                        for k in range(CT_):
                            for a in range(2):
                                o = k * T + a * P
                                last = nc.tensor.transpose(bank("yt", q)[:, o:o + P],
                                                           ybuf[:, (n + a) % 4, k * P:(k + 1) * P], ident[:])
                        last.then_inc(bank_full[bank_of("yt", q)], 1)

            def one(i, ffn, rest):
                if rest:
                    qk(i, 0)
                if ffn:
                    x2_down(i)
                if rest:
                    kproj(i, 0, [(1, lambda: mid_transpose(i))] if ffn else [])
                    av(i, 0)
                    qk(i, 1)
                    tg(i, 0)
                else:
                    mid_transpose(i)
                if ffn:
                    gated_transpose(i)
                if rest:
                    kproj(i, 1, [(s, lambda s=s: mt(i, 0, s)) for s in range(3)])
                if ffn:
                    delta(i)
                if rest:
                    av(i, 1)
                    qk(i, 2)
                    tg(i, 1)
                    av(i, 2)
                    qk(i, 3)
                    kproj(i, 2, [(s, lambda s=s: mt(i, 1, s)) for s in range(3)])
                    av(i, 3)
                    tg(i, 2)
                    kproj(i, 3, [(s, lambda s=s: mt(i, 2, s)) for s in range(3)])
                    tg(i, 3)
                    linear(i)

            pe.wait_ge(setup_done, 1)
            pe.wait_ge(ident_made, 2)
            rounds(mybir.EngineType.PE, one)

        @block.scalar
        def _(act):
            activation = nc.scalar.activation

            act.wait_ge(consts_loaded, 16 * 13)
            for v, src in enumerate((e_buf[:, :], xa[:, 1, :], vb[:])):
                for h in range(H):
                    activation(avt[:, 0, :], src[:, h * HD:(h + 1) * HD], ACT.Abs,
                               accum_out=alpha[:, v, h:h + 1]).then_inc(setup_abs, 1)
                    act.wait_ge(setup_abs, v * H + h + 1)

            def xt_split_hi(i, h):
                act.wait_ge(*raw_arrived(i, "xt", h))
                for half in range(2):
                    if not (isinstance(i, int) and i == 0 and h == 0):
                        if half == 0:
                            act.wait_ge(qk_half, i * H + h)
                        elif h > 0:
                            act.wait_ge(*full(i, "qk", h - 1))
                        else:
                            act.wait_ge(bank_full[4], use_before(i, "qk", 3))
                    activation(xt_part[:, half, HI, :, :].rearrange("p a t -> p (a t)"),
                               raw_slot("xt", h)[:, half * 512:(half + 1) * 512], ACT.Copy).then_inc(xt_hi, 1)

            def tanh(i, h):
                act.wait_ge(*full(i, "qk", h))
                if not (isinstance(i, int) and i == 0 and h == 0):
                    act.wait_ge(prob_ready, i * H + h)
                src = bank("qk", h)
                activation(prob[:, 0:2, :].rearrange("p a t -> p (a t)"), src[:, 0:T], ACT.Tanh,
                           scale=2.0 * HD ** -0.5)
                activation(prob[:, 2, :], src[:, T + P:2 * T], ACT.Tanh,
                           scale=2.0 * HD ** -0.5).then_inc(bank_free[bank_of("qk", h)], 1)

            def c_split_hi(i, c):
                act.wait_ge(*raw_arrived(i, "c", c))
                if not isinstance(i, int):
                    act.wait_ge(bank_full[bank_of("q", 4 * c + 3)], use_before(i, "q", 4 * c + 3))
                activation(c_part[:, HI, :, c * 512:(c + 1) * 512],
                           raw_slot("c", c).rearrange("p (k n) -> p k n", k=CT_), ACT.Copy).then_inc(c_hi, 1)

            def x2t_hi_parts(i, j):
                act.wait_ge(*full(i, "x2t", j))
                if j >= 2:
                    act.wait_ge(mid_used, (i - 1) * 7 + j - 1)
                activation(t_part[:, j % 2, HI, :], bank("x2t", j)[:, :], ACT.Copy).then_inc(x2t_hi, 1)

            def exp_keys(i, h):
                act.wait_ge(kmax_ready, i * H + h + 1)
                if h > 0 or not isinstance(i, int):
                    if h > 0:
                        act.wait_ge(*full(i, "et", h - 1, 3))
                    act.wait_ge(krden_ready, i * H + h)
                for c in range(CH):
                    activation(e_buf[:, c * 512:(c + 1) * 512], bank("k", h, c)[:, :], ACT.Exp, bias=knmax[:],
                               accum_out=kden4[:, c:c + 1]).then_inc(bank_free[c], 1)

            def et_hi_parts(i, h, c):
                act.wait_ge(*full(i, "et", h, c))
                if c >= 2:
                    act.wait_ge(g_chunk, i * 12 + h * 3 + c - 1)
                elif h > 0:
                    act.wait_ge(g_chunk, i * 12 + h * 3)
                    if c == 1:
                        act.wait_ge(*full(i, "g", h - 1))
                activation(t_part[:, c % 2, HI, :], bank("et", h, c)[:, :], ACT.Copy).then_inc(et_hi, 1)

            def g_scale(i, h):
                act.wait_ge(*full(i, "g", h))
                act.wait_ge(krden_ready, i * H + h + 1)
                if h > 0:
                    act.wait_ge(*full(i, "mt", h - 1, 0))
                activation(gs[:], bank("g", h)[:, 0:T], ACT.Copy, scale=krden[:]).then_inc(bank_free[5], 1)

            def gt_copy(i, h):
                act.wait_ge(*full(i, "mt", h, 0))
                activation(gt[:].rearrange("p k d -> p (k d)"), bank("mt", h, 0)[:, 0:T],
                           ACT.Copy).then_inc(bank_free[4], 1)

            def m_hi_part(i, h):
                act.wait_ge(*full(i, "mt", h, 2))
                activation(m_part[:, h, HI, :], bank("mt", h, 2)[:, 0:T], ACT.Copy).then_inc(m_hi, 1)

            def mid_copies(i):
                act.wait_ge(*full(i, "mid"))
                activation(midt[0:ARW, :], bank("mid")[0:ARW, 0:T], ACT.Copy).then_inc(bank_free[5], 1)

            def md_copy(i):
                act.wait_ge(*full(i, "midt"))
                activation(md[:], bank("midt")[:, 0:T].rearrange("p (t n) -> p t n", t=CT_)[:, :, 0:ARW],
                           ACT.Copy).then_inc(bank_free[4], 1)

            def gates_exp(i):
                act.wait_ge(gate_diff, i)
                activation(gexp[:], gdif[:], ACT.Exp).then_inc(gate_exp, 1)

            def gated_hi_part(i):
                act.wait_ge(*full(i, "gated"))
                activation(gated_part[:, HI, :, :].rearrange("p t n -> p (t n)"), bank("gated")[:, 0:T],
                           ACT.Copy).then_inc(gated_hi, 1)

            def x1_split_hi(i, c):
                act.wait_ge(ln_done[0], i * 8 + 2 * c + 2)
                act.wait_ge(*full(i, "k", 3, c))
                activation(c_part[:, HI, :, c * 512:(c + 1) * 512], xa[:, :, c * 512:(c + 1) * 512],
                           ACT.Copy).then_inc(x1_hi, 1)

            def linear(i):
                for s in range(NT_ + 4):
                    if s < NT_:
                        act.wait_ge(*freed(i, "q", s))
                        v = e_buf[:, (s % 3) * 512:(s % 3 + 1) * 512]
                        activation(v, v, ACT.Exp).then_inc(q_exp, 1)
                    if s < 3:
                        if s == 0:
                            gt_copy(i, 3)
                        if s == 2:
                            m_hi_part(i, 3)
                    n = s - 2
                    if 0 <= n < NT_:
                        act.wait_ge(*full(i, "qt", n))
                        if n >= 2:
                            act.wait_ge(*full(i, "y", n - 2))
                        activation(t_part[:, n % 2, HI, :], bank("qt", n)[:, :], ACT.Copy).then_inc(qt_hi, 1)
                    n = s - 3
                    if 0 <= n < NT_:
                        act.wait_ge(*freed(i, "y", n))
                        if n >= 2:
                            act.wait_ge(y_squared, i * NT_ + n)
                        activation(avt[:, 1, 0:T], ybuf[:, n % 4, :], ACT.Square,
                                   accum_out=yss[:, n // 2 % 2, n % 2:n % 2 + 1]).then_inc(y_squared, 1)

            def one(i, ffn, rest):
                if rest:
                    xt_split_hi(i, 0)
                    tanh(i, 0)
                    c_split_hi(i, 0)
                for j in range(8):
                    if ffn:
                        x2t_hi_parts(i, j)
                    if rest and j in (1, 3, 5):
                        c_split_hi(i, (j + 1) // 2)
                if ffn:
                    mid_copies(i)
                if rest:
                    xt_split_hi(i, 1)
                if ffn:
                    md_copy(i)
                if rest:
                    exp_keys(i, 0)
                if ffn:
                    gates_exp(i)
                if rest:
                    tanh(i, 1)
                    for c in range(CH):
                        et_hi_parts(i, 0, c)
                    g_scale(i, 0)
                if ffn:
                    gated_hi_part(i)
                if rest:
                    xt_split_hi(i, 2)
                    gt_copy(i, 0)
                    m_hi_part(i, 0)
                    exp_keys(i, 1)
                    tanh(i, 2)
                    for c in range(CH):
                        et_hi_parts(i, 1, c)
                    g_scale(i, 1)
                    xt_split_hi(i, 3)
                    tanh(i, 3)
                    gt_copy(i, 1)
                    m_hi_part(i, 1)
                    exp_keys(i, 2)
                    for c in range(CH):
                        et_hi_parts(i, 2, c)
                    g_scale(i, 2)
                    gt_copy(i, 2)
                    m_hi_part(i, 2)
                    x1_split_hi(i, 0)
                    exp_keys(i, 3)
                    for c in range(CH):
                        et_hi_parts(i, 3, c)
                        if c < 3:
                            x1_split_hi(i, c + 1)
                    g_scale(i, 3)
                    linear(i)

            rounds(mybir.EngineType.Activation, one)

        @block.gpsimd
        def _(pool):
            tt = nc.gpsimd.tensor_tensor
            made = [0]

            def link(ins):
                made[0] += 1
                ins.then_inc(pool_made, 1)
                pool.wait_ge(pool_made, made[0])

            link(nc.gpsimd.memset(ident[:], 0.0))
            nc.gpsimd.affine_select(out=ident[:], in_=ident[:], compare_op=ALU.not_equal, fill=1.0, base=0,
                                    pattern=[[-1, P]], channel_multiplier=1).then_inc(ident_made, 1)
            link(nc.gpsimd.memset(halfmask[:], 0.5))
            for b in (0, 2):
                link(nc.gpsimd.affine_select(out=halfmask[:, b, :], in_=halfmask[:, b, :], compare_op=ALU.is_ge,
                                             fill=0.0, base=0, pattern=[[1, P]], channel_multiplier=-1))
            link(nc.gpsimd.memset(pairmask[:], 1.0))
            link(nc.gpsimd.affine_select(out=pairmask[:, 0:LD], in_=pairmask[:, 0:LD], compare_op=ALU.is_ge,
                                         fill=0.0, base=LD - 1, pattern=[[0, LD]], channel_multiplier=-1))
            link(nc.gpsimd.affine_select(out=pairmask[:, LD:P], in_=pairmask[:, LD:P], compare_op=ALU.is_ge,
                                         fill=0.0, base=-LD, pattern=[[0, LD]], channel_multiplier=1))
            link(nc.gpsimd.memset(before[:], 1.0))
            link(nc.gpsimd.affine_select(out=before[:], in_=before[:], compare_op=ALU.is_gt, fill=0.0, base=0,
                                         pattern=[[1, E], [-1, E]], channel_multiplier=0))
            nc.gpsimd.memset(minus_half[:], -0.5).then_inc(ident_made, 1)
            pool.wait_ge(ident_made, 2)

            def xt_split_lo(i, h):
                for half in range(2):
                    pool.wait_ge(xt_hi, i * 8 + 2 * h + half + 1)
                    if half == 1:
                        pool.wait_ge(xt_d, i * 8 + 2 * h + 2)
                    tt(xt_part[:, half, LO, :, :].rearrange("p a t -> p (a t)"),
                       raw_slot("xt", h)[:, half * 512:(half + 1) * 512],
                       xt_part[:, half, HI, :, :].rearrange("p a t -> p (a t)").bitcast(F32),
                       ALU.subtract).then_inc(xt_lo, 1)
                pool.wait_ge(xt_lo, i * 8 + 2 * h + 2)
                pool.sem_inc(raw_used, 1)

            def c_split_lo(i, c):
                pool.wait_ge(c_hi, i * CH + c + 1)
                tt(c_part[:, LO, :, c * 512:(c + 1) * 512], raw_slot("c", c).rearrange("p (k n) -> p k n", k=CT_),
                   c_part[:, HI, :, c * 512:(c + 1) * 512].bitcast(F32), ALU.subtract).then_inc(c_lo, 1)
                pool.wait_ge(c_lo, i * CH + c + 1)
                pool.sem_inc(raw_used, 1)

            def ct_split_lo(i, c):
                pool.wait_ge(ct_hi, i * CH + c + 1)
                tt(ct_part[:, 4 * c:4 * c + 4, LO, :], raw_slot("ct", c).rearrange("p (k n) -> p k n", k=4),
                   ct_part[:, 4 * c:4 * c + 4, HI, :].bitcast(F32), ALU.subtract).then_inc(ct_lo, 1)
                pool.wait_ge(ct_lo, i * CH + c + 1)
                pool.sem_inc(raw_used, 1)

            def xn_split_lo(i, h):
                pool.wait_ge(xn_hi, i * H + h + 1)
                tt(xn_part[:, LO, :, :], xa[:, :, h * HD:(h + 1) * HD], xn_part[:, HI, :, :].bitcast(F32),
                   ALU.subtract).then_inc(xn_lo, 1)

            def x1_split_lo(i, c):
                pool.wait_ge(x1_hi, i * CH + c + 1)
                tt(c_part[:, LO, :, c * 512:(c + 1) * 512], xa[:, :, c * 512:(c + 1) * 512],
                   c_part[:, HI, :, c * 512:(c + 1) * 512].bitcast(F32), ALU.subtract).then_inc(x1_lo, 1)

            def root(r, which):
                pool.wait_ge(ln_var[which], r + 1)
                tt(rstd[:, which, :], ve[:, which, :], minus_half[:], ALU.pow).then_inc(ln_rstd[which], 1)

            def linear(i):
                for s in range(1, NT_ + 4):
                    n = s - 1
                    if n < NT_:
                        pool.wait_ge(q_rden, i * NT_ + n + 1)
                        v = e_buf[:, (n % 3) * 512:(n % 3 + 1) * 512].rearrange("p (h d) -> p h d", h=LH)
                        tt(v, v, qrden[:, n % 2, :].unsqueeze(2).to_broadcast([P, LH, LD]),
                           ALU.mult).then_inc(q_norm, 1)
                    n = s - 4
                    if n >= 0 and n % 2 == 0 and n < NT_:
                        q = n // 2
                        pool.wait_ge(y_guard, i * 8 + q + 1)
                        tt(yr[:, q % 2, :], yssm[:], minus_half[:], ALU.pow).then_inc(y_r, 1)

            def one(i, ffn, rest):
                if rest:
                    xt_split_lo(i, 0)
                    c_split_lo(i, 0)
                    xn_split_lo(i, 0)
                    for c in range(1, CH):
                        c_split_lo(i, c)
                    xt_split_lo(i, 1)
                    for c in range(CH):
                        ct_split_lo(i, c)
                    xn_split_lo(i, 1)
                    xt_split_lo(i, 2)
                if ffn:
                    root(i - 1, 2)
                if rest:
                    xn_split_lo(i, 2)
                    xt_split_lo(i, 3)
                    xn_split_lo(i, 3)
                    root(i, 0)
                    for c in range(CH):
                        x1_split_lo(i, c)
                    linear(i)
                    root(i, 1)

            rounds(mybir.EngineType.Pool, one)

        @block.vector
        def _(dve):
            v = nc.vector
            done = [0]

            def link(ins):
                done[0] += 1
                ins.then_inc(setup_dve, 1)
                dve.wait_ge(setup_dve, done[0])

            dve.wait_ge(consts_loaded, 16 * 13)
            staged = x2[:, 0, :].rearrange("p (a n) -> p a n", a=2)
            for dst, src, k in ((wq, staged[:, 0, :], CT_), (wk, staged[:, 1, :], CT_),
                                (ar, xa[:, 0, 0:NT_ * ARW], NT_)):
                s3 = src.rearrange("p (k n) -> p k n", k=k)
                link(v.tensor_copy(dst[:, :, HI, :], s3))
                link(v.tensor_tensor(dst[:, :, LO, :], s3, dst[:, :, HI, :].bitcast(F32), ALU.subtract))
            link(v.tensor_copy(b2[:], x2[:, 1, :]))
            link(v.tensor_tensor(b2[ER:P, :], x2[ER:P, 1, :], b2[ER:P, :].bitcast(F32), ALU.subtract))
            link(v.tensor_scalar(g16[:], g16[:], float(T) ** 0.5, None, ALU.mult))
            dve.wait_ge(setup_abs, 12)
            link(v.tensor_scalar(alpha[:], alpha[:], 1.0 / HD, None, ALU.mult))

            def ste_sign(dst, w, tmp, a):
                link(v.tensor_scalar(tmp, w, 0.0, None, ALU.is_ge))
                link(v.tensor_scalar(tmp, tmp, 2.0, -1.0, ALU.mult, ALU.add))
                link(v.scalar_tensor_tensor(tmp, tmp, a, w, ALU.mult, ALU.subtract))
                link(v.tensor_tensor(dst, tmp, w, ALU.add))

            for h in range(H):
                c4 = slice(h * DT_, (h + 1) * DT_)
                ste_sign(ste[:, 0, c4], ste[:, 0, c4], ste[:, 2, c4], alpha[:, 0, h:h + 1])
                ste_sign(ste[:, 1, c4], ste[:, 1, c4], ste[:, 3, c4], alpha[:, 1, h:h + 1])
                c5 = slice(h * HD, (h + 1) * HD)
                ste_sign(vb[:, c5], vb[:, c5], avt[:, 1, :], alpha[:, 2, h:h + 1])
            v.tensor_tensor(dcol[:], ste[:, 0, :], ste[:, 1, :], ALU.mult).then_inc(setup_dve, 1)
            dve.wait_ge(setup_dve, done[0] + 1)
            dve.sem_inc(setup_done, 1)

            def xt_split_d(i, h):
                dve.wait_ge(*raw_arrived(i, "xt", h))
                for half in range(2):
                    if not (isinstance(i, int) and i == 0 and h == 0):
                        if half == 0:
                            dve.wait_ge(qk_half, i * H + h)
                        elif h > 0:
                            dve.wait_ge(*full(i, "qk", h - 1))
                        else:
                            dve.wait_ge(bank_full[4], use_before(i, "qk", 3))
                    for dt in range(2):
                        src = raw_slot("xt", h)[:, half * 512 + dt * T:half * 512 + (dt + 1) * T]
                        col = h * DT_ + half * 2 + dt
                        v.tensor_scalar(xd_part[:, half, HI, dt, :], src, dcol[:, col:col + 1], None,
                                        ALU.mult).then_inc(xt_dhi, 1)
                    for dt in range(2):
                        src = raw_slot("xt", h)[:, half * 512 + dt * T:half * 512 + (dt + 1) * T]
                        col = h * DT_ + half * 2 + dt
                        dve.wait_ge(xt_dhi, i * 16 + (2 * h + half) * 2 + dt + 1)
                        last = v.scalar_tensor_tensor(xd_part[:, half, LO, dt, :], src, dcol[:, col:col + 1],
                                                      xd_part[:, half, HI, dt, :].bitcast(F32), ALU.mult,
                                                      ALU.subtract)
                    last.then_inc(xt_d, 1)

            def xn_split_hi(i, h):
                dve.wait_ge(x_loaded[h], i * 16 + 16)
                if h > 0:
                    dve.wait_ge(*full(i, "av", h - 1, 1))
                v.tensor_copy(xn_part[:, HI, :, :], xa[:, :, h * HD:(h + 1) * HD]).then_inc(xn_hi, 1)

            def ct_split_hi(i, c):
                dve.wait_ge(*raw_arrived(i, "ct", c))
                v.tensor_copy(ct_part[:, 4 * c:4 * c + 4, HI, :],
                              raw_slot("ct", c).rearrange("p (k n) -> p k n", k=4)).then_inc(ct_hi, 1)

            def probs(i, h):
                dve.wait_ge(*freed(i, "qk", h))
                v.scalar_tensor_tensor(prob[:], prob[:], 1.0, halfmask[:], ALU.add,
                                       ALU.mult).then_inc(prob_step, 1)
                dve.wait_ge(prob_step, i * 2 * H + 2 * h + 1)
                if h > 0:
                    dve.wait_ge(*full(i, "av", h - 1, 1))
                v.tensor_copy(prob_part[:, HI, :, :], prob[:]).then_inc(prob_step, 1)
                dve.wait_ge(prob_step, i * 2 * H + 2 * h + 2)
                v.tensor_tensor(prob_part[:, LO, :, :], prob[:], prob_part[:, HI, :, :].bitcast(F32),
                                ALU.subtract).then_inc(prob_ready, 1)

            def x2t_lo_parts(i, j):
                dve.wait_ge(x2t_hi, (i - 1) * 8 + j + 1)
                v.tensor_tensor(t_part[:, j % 2, LO, :], bank("x2t", j)[:, :],
                                t_part[:, j % 2, HI, :].bitcast(F32),
                                ALU.subtract).then_inc(bank_free[bank_of("x2t", j)], 1)

            def key_max(i, h):
                for c in range(CH):
                    dve.wait_ge(*full(i, "k", h, c))
                    v.tensor_reduce(kmax4[:, c:c + 1], bank("k", h, c)[:, :], AX.X, ALU.max).then_inc(kmax_step, 1)
                dve.wait_ge(kmax_step, i * 16 + h * 4 + 4)
                v.tensor_scalar(kjunk[:], kmax4[:], -1.0, None, ALU.mult, ALU.min,
                                accum_out=knmax[:]).then_inc(kmax_ready, 1)

            def key_sum(i, h):
                dve.wait_ge(*freed(i, "k", h, 3))
                if h > 0:
                    dve.wait_ge(*freed(i, "g", h - 1))
                v.tensor_reduce(kden[:], kden4[:], AX.X, ALU.add).then_inc(kden_step, 1)
                dve.wait_ge(kden_step, i * 8 + h * 2 + 1)
                v.reciprocal(krden[:], kden[:]).then_inc(kden_step, 1)
                dve.wait_ge(kden_step, i * 8 + h * 2 + 2)
                v.tensor_scalar(krden[:], krden[:], LD ** -0.5, None, ALU.mult).then_inc(krden_ready, 1)

            def et_lo_parts(i, h, c):
                dve.wait_ge(et_hi, i * 16 + h * 4 + c + 1)
                v.tensor_tensor(t_part[:, c % 2, LO, :], bank("et", h, c)[:, :],
                                t_part[:, c % 2, HI, :].bitcast(F32),
                                ALU.subtract).then_inc(bank_free[bank_of("et", h, c)], 1)

            def cx_mask(i, h):
                dve.wait_ge(*full(i, "mt", h, 1))
                v.tensor_tensor(cx[:], bank("mt", h, 1)[:, 0:P], pairmask[:], ALU.mult).then_inc(bank_free[4], 1)

            def m_lo_part(i, h):
                dve.wait_ge(m_hi, i * OT_ + h + 1)
                v.tensor_tensor(m_part[:, h, LO, :], bank("mt", h, 2)[:, 0:T], m_part[:, h, HI, :].bitcast(F32),
                                ALU.subtract).then_inc(bank_free[4], 1)

            def residual(i, h):
                cols = slice(h * HD, (h + 1) * HD)
                for t in range(CT_):
                    dve.wait_ge(*full(i, "av", h, t))
                    v.tensor_tensor(avt[:, t, :], bank("av", h, t)[:, :], vb[:, cols],
                                    ALU.mult).then_inc(bank_free[bank_of("av", h, t)], 1)
                for t in range(CT_):
                    dve.wait_ge(*freed(i, "av", h, t))
                    v.tensor_tensor(xa[:, t, cols], xa[:, t, cols], avt[:, t, :], ALU.add).then_inc(res_added, 1)
                for t in range(CT_):
                    dve.wait_ge(res_added, i * 8 + 2 * h + t + 1)
                    v.bn_stats(stats[:, 0, t, h, :], xa[:, t, cols]).then_inc(ln_stats[0], 1)

            def ln_prepare(r, w):
                dve.wait_ge(ln_stats[w], r * 10 + 8)
                v.memset(ln_gate[:], 0.0)
                for t in range(CT_):
                    v.bn_aggr(mv[:, w, t, :], stats[:, w, t, :, :].rearrange("p c s -> p (c s)")).then_inc(
                        ln_stats[w], 1)
                dve.wait_ge(ln_stats[w], r * 10 + 10)
                v.tensor_scalar(ve[:, w, :], mv[:, w, :, 1], LN_EPS, None, ALU.add).then_inc(ln_var[w], 1)

            def ln_finish(r, w):
                dve.wait_ge(ln_rstd[w], r + 1)
                v.scalar_tensor_tensor(nmr[:, w, :], mv[:, w, :, 0], -1.0, rstd[:, w, :], ALU.mult,
                                       ALU.mult).then_inc(ln_nmr[w], 1)
                dve.wait_ge(ln_nmr[w], r + 1)

            def ln_apply(buf, w, t, cols):
                v.tensor_scalar(buf[:, t, cols], buf[:, t, cols], rstd[:, w, t:t + 1], nmr[:, w, t:t + 1],
                                ALU.mult, ALU.add).then_inc(ln_done[w], 1)

            def gates(i):
                r = i - 1
                n = [0]

                def step(ins):
                    n[0] += 1
                    ins.then_inc(gate_step, 1)
                    dve.wait_ge(gate_step, r * 8 + n[0])

                dve.wait_ge(*freed(i, "midt"))
                logits = md[:, :, ER:ARW]
                step(v.tensor_reduce(gmax[:], logits, AX.X, ALU.max))
                v.tensor_tensor(gdif[:], logits, gmax[:].unsqueeze(2).to_broadcast([P, CT_, E]),
                                ALU.subtract).then_inc(gate_diff, 1)
                other = logits.unsqueeze(2).to_broadcast([P, CT_, E, E])
                own = logits.unsqueeze(3).to_broadcast([P, CT_, E, E])
                step(v.tensor_tensor(geq[:], other, own, ALU.is_equal))
                for t in range(CT_):
                    v.tensor_tensor(geq[:, t, :, :], geq[:, t, :, :], before[:], ALU.mult).then_inc(gate_order, 1)
                dve.wait_ge(gate_order, r * 2 + 2)
                step(v.tensor_tensor(ggt[:], other, own, ALU.is_gt))
                step(v.tensor_tensor(ggt[:], ggt[:], geq[:], ALU.add))
                step(v.tensor_reduce(grank[:], ggt[:], AX.X, ALU.add))
                dve.wait_ge(gate_exp, i)
                step(v.scalar_tensor_tensor(gexp[:], grank[:], TOP_K - 0.5, gexp[:], ALU.is_lt, ALU.mult))
                step(v.tensor_reduce(gsum[:], gexp[:], AX.X, ALU.add))
                step(v.reciprocal(gsum[:], gsum[:]))
                assert n[0] == 8

            def gate_mid(i):
                r = i - 1
                v.tensor_tensor(gdif[:], gexp[:], gsum[:].unsqueeze(2).to_broadcast([P, CT_, E]),
                                ALU.mult).then_inc(gate_norm, 1)
                dve.wait_ge(gate_norm, r + 1)
                for t in range(CT_):
                    for a in range(2):
                        v.scalar_tensor_tensor(gated[:, t, a, :].rearrange("p (e r) -> p e r", e=E),
                                               md[:, t, 0:ER].rearrange("p (e r) -> p e r", e=E), LORA_SCALE,
                                               gdif[:, t, :].unsqueeze(2).to_broadcast([P, E, R]),
                                               ALU.mult, ALU.mult).then_inc(gated_ready, 1)

            def gated_lo_part(i):
                dve.wait_ge(gated_hi, i)
                v.tensor_tensor(gated_part[:, LO, :, :].rearrange("p t n -> p (t n)"), bank("gated")[:, 0:T],
                                gated_part[:, HI, :, :].rearrange("p t n -> p (t n)").bitcast(F32),
                                ALU.subtract).then_inc(bank_free[4], 1)

            def ffn_out(i):
                r = i - 1
                for k in range(8):
                    t, c = divmod(k, CH)
                    cols = slice(c * 512, (c + 1) * 512)
                    dve.wait_ge(*full(i, "delta", k))
                    v.tensor_tensor(x2[:, t, cols], x2[:, t, cols], bank("delta", k)[:, :],
                                    ALU.add).then_inc(bank_free[bank_of("delta", k)], 1)
                    dve.wait_ge(*freed(i, "delta", k))
                    v.bn_stats(stats[:, 2, t, c, :], x2[:, t, cols]).then_inc(ln_stats[2], 1)
                ln_prepare(r, 2)

            def ffn_norm(i):
                ln_finish(i - 1, 2)
                for t in range(CT_):
                    ln_apply(x2, 2, t, slice(0, D))

            def linear(i):
                for s in range(NT_ + 7):
                    if s < NT_:
                        dve.wait_ge(*full(i, "q", s))
                        src = bank("q", s)[:, :].rearrange("p (h d) -> p h d", h=LH)
                        v.tensor_reduce(qmax[:, s % 2, :], src, AX.X, ALU.max).then_inc(q_max, 1)
                        dve.wait_ge(q_max, i * NT_ + s + 1)
                        if s >= 3:
                            dve.wait_ge(*full(i, "qt", s - 3))
                        v.tensor_tensor(e_buf[:, (s % 3) * 512:(s % 3 + 1) * 512].rearrange("p (h d) -> p h d", h=LH),
                                        src, qmax[:, s % 2, :].unsqueeze(2).to_broadcast([P, LH, LD]),
                                        ALU.subtract).then_inc(bank_free[bank_of("q", s)], 1)
                    if s == 1:
                        cx_mask(i, 3)
                    if s == 2:
                        m_lo_part(i, 3)
                    n = s - 1
                    if 0 <= n < NT_:
                        dve.wait_ge(q_exp, i * NT_ + n + 1)
                        v.tensor_reduce(qden[:, n % 2, :],
                                        e_buf[:, (n % 3) * 512:(n % 3 + 1) * 512].rearrange("p (h d) -> p h d", h=LH),
                                        AX.X, ALU.add).then_inc(q_sum, 1)
                        dve.wait_ge(q_sum, i * NT_ + n + 1)
                        if n >= 2:
                            dve.wait_ge(q_norm, i * NT_ + n - 1)
                        v.reciprocal(qrden[:, n % 2, :], qden[:, n % 2, :]).then_inc(q_rden, 1)
                    n = s - 2
                    if 0 <= n < NT_:
                        dve.wait_ge(qt_hi, i * NT_ + n + 1)
                        v.tensor_tensor(t_part[:, n % 2, LO, :], bank("qt", n)[:, :],
                                        t_part[:, n % 2, HI, :].bitcast(F32),
                                        ALU.subtract).then_inc(bank_free[bank_of("qt", n)], 1)
                    n = s - 3
                    if 0 <= n < NT_:
                        dve.wait_ge(*full(i, "y", n))
                        if n >= 4:
                            dve.wait_ge(*full(i, "yt", (n - 4) // 2))
                        v.tensor_tensor(ybuf[:, n % 4, :], bank("y", n)[:, 0:T], bob[:],
                                        ALU.add).then_inc(bank_free[5], 1)
                    n = s - 4
                    if n >= 0 and n % 2 == 0 and n < NT_:
                        q = n // 2
                        dve.wait_ge(y_squared, i * NT_ + n + 2)
                        if q > 0:
                            dve.wait_ge(y_r, i * 8 + q)
                        v.tensor_scalar(yssm[:], yss[:, q % 2, :], 1e-24, None, ALU.max).then_inc(y_guard, 1)
                    n = s - 5
                    if n >= 0 and n % 2 == 0 and n < NT_:
                        q = n // 2
                        dve.wait_ge(y_r, i * 8 + q + 1)
                        for a in range(2):
                            yb = ybuf[:, (n + a) % 4, :]
                            v.tensor_scalar(yb, yb, yr[:, q % 2, a:a + 1], None, ALU.mult).then_inc(y_scaled, 1)
                    n = s - 6
                    if n >= 0 and n % 2 == 0 and n < NT_:
                        q = n // 2
                        cols = slice(q * T, (q + 1) * T)
                        dve.wait_ge(*full(i, "yt", q))
                        if q == 0 and not isinstance(i, int):
                            dve.wait_ge(stored, i * 16 * CT_)
                        v.scalar_tensor_tensor(x2[:, 0, cols], bank("yt", q)[:, 0:T], g16[:, 0:1], xa[:, 0, cols],
                                               ALU.mult, ALU.add)
                        v.scalar_tensor_tensor(x2[:, 1, cols], bank("yt", q)[:, T:2 * T], g16[:, 1:2],
                                               xa[:, 1, cols], ALU.mult,
                                               ALU.add).then_inc(bank_free[bank_of("yt", q)], 1)
                        if q % 2 == 1:
                            c = q // 2
                            dve.wait_ge(*freed(i, "yt", q))
                            for t in range(CT_):
                                v.bn_stats(stats[:, 1, t, c, :], x2[:, t, c * 512:(c + 1) * 512]).then_inc(
                                    ln_stats[1], 1)
                ln_prepare(i, 1)
                ln_finish(i, 1)
                for c in range(CH):
                    for t in range(CT_):
                        ln_apply(x2, 1, t, slice(c * 512, (c + 1) * 512))

            def one(i, ffn, rest):
                if rest:
                    xt_split_d(i, 0)
                    xn_split_hi(i, 0)
                    probs(i, 0)
                if ffn:
                    for j in range(8):
                        x2t_lo_parts(i, j)
                if rest:
                    xt_split_d(i, 1)
                    key_max(i, 0)
                if ffn:
                    gates(i)
                    gate_mid(i)
                if rest:
                    key_sum(i, 0)
                    for c in range(CH):
                        ct_split_hi(i, c)
                    residual(i, 0)
                    xn_split_hi(i, 1)
                    probs(i, 1)
                    for c in range(CH):
                        et_lo_parts(i, 0, c)
                    xt_split_d(i, 2)
                if ffn:
                    gated_lo_part(i)
                if rest:
                    cx_mask(i, 0)
                    m_lo_part(i, 0)
                    key_max(i, 1)
                if ffn:
                    ffn_out(i)
                if rest:
                    key_sum(i, 1)
                    residual(i, 1)
                    xn_split_hi(i, 2)
                    probs(i, 2)
                if ffn:
                    ffn_norm(i)
                if rest:
                    for c in range(CH):
                        et_lo_parts(i, 1, c)
                    xt_split_d(i, 3)
                    residual(i, 2)
                    xn_split_hi(i, 3)
                    probs(i, 3)
                    cx_mask(i, 1)
                    m_lo_part(i, 1)
                    key_max(i, 2)
                    residual(i, 3)
                    ln_prepare(i, 0)
                    key_sum(i, 2)
                    for c in range(CH):
                        et_lo_parts(i, 2, c)
                    ln_finish(i, 0)
                    for c in range(CH):
                        for t in range(CT_):
                            ln_apply(xa, 0, t, slice(c * 512, (c + 1) * 512))
                        if c == 0:
                            cx_mask(i, 2)
                        if c == 1:
                            m_lo_part(i, 2)
                    key_max(i, 3)
                    key_sum(i, 3)
                    for c in range(CH):
                        et_lo_parts(i, 3, c)
                    linear(i)

            dve.wait_ge(ident_made, 2)
            rounds(mybir.EngineType.DVE, one)


def kernel(x, ctx_4096, L0_attn_bv_q, L0_attn_bv_k, L0_attn_bv_v, L0_xattn_Wq, L0_xattn_Wk, L0_xattn_Wv,
           L0_xattn_Wo, L0_xattn_bo, L0_xattn_g, L0_ffn_router_w, L0_ffn_A, L0_ffn_B):
    import concourse.bacc as bacc
    from concourse.bass_utils import run_bass_kernel_spmd

    def rows(v):
        return np.broadcast_to(np.asarray(v).reshape(1, -1), (P, np.asarray(v).size))

    def tiles(w, n):
        return np.asarray(w).reshape(n, P, -1).transpose(1, 0, 2).reshape(P, -1)

    def chunks(a):
        return np.asarray(a).reshape(B, CT_, P, CH, 512).transpose(0, 3, 2, 1, 4).reshape(B, CH, P, CT_ * 512)

    def turned(a):
        return np.asarray(a).transpose(0, 2, 1).reshape(B, CH, 4, P, T).transpose(0, 1, 3, 2, 4).reshape(
            B, CH, P, 4 * T)

    a_rows = np.concatenate([np.asarray(L0_ffn_A).reshape(ER, D), np.asarray(L0_ffn_router_w)], 0)
    b_rows = np.asarray(L0_ffn_B).transpose(0, 2, 1).reshape(ER, D)
    arrays = {
        "x": chunks(x), "xt": turned(x), "ctx": chunks(ctx_4096), "ctxt": turned(ctx_4096),
        "bv_q": rows(L0_attn_bv_q), "bv_k": rows(L0_attn_bv_k), "bv_v": rows(L0_attn_bv_v),
        "bq_col": np.asarray(L0_attn_bv_q).reshape(NT_, P).T, "bk_col": np.asarray(L0_attn_bv_k).reshape(NT_, P).T,
        "wqt": tiles(np.asarray(L0_xattn_Wq).T, CT_), "wkt": tiles(np.asarray(L0_xattn_Wk).T, CT_),
        "wvt": tiles(np.asarray(L0_xattn_Wv).T, CT_), "wot": tiles(np.asarray(L0_xattn_Wo).T, OT_),
        "bo": rows(L0_xattn_bo), "g": np.asarray(L0_xattn_g).reshape(CT_, P).T,
        "art": tiles(a_rows.T, NT_), "bt": np.concatenate([b_rows, b_rows], 0),
    }
    arrays = {f"in_{k}": np.ascontiguousarray(a) for k, a in arrays.items()}
    nc = bacc.Bacc("TRN2", target_bir_lowering=False, num_devices=1, dynamic_dma_scratch_size=1024)
    args = [nc.dram_tensor(k, a.shape, mybir.dt.from_np(a.dtype), kind="ExternalInput").ap()
            for k, a in arrays.items()]
    args.append(nc.dram_tensor("out", (B, CT_, P, D), F32, kind="ExternalOutput").ap())
    build(nc, *args)
    done = run_bass_kernel_spmd(nc, [arrays], core_ids=[0])
    return done.results[0]["out"].reshape(B, T, D)
```

```python
from contextlib import ExitStack

import numpy as np

import concourse.bass as bass
from concourse import mybir

F32 = mybir.dt.float32
F32R = mybir.dt.float32r
ACT = mybir.ActivationFunctionType
ALU = mybir.AluOpType
AX = mybir.AxisListType

P = 128
B, T, D = 16, 256, 2048
H, HD = 4, 512
CT_, NT_, DT_ = T // P, D // P, HD // P
HID, LH, LD = 512, 8, 64
OT_ = HID // P
E, R, ER = 4, 16, 64
TOP_K = 2
AH = 4
ARW = ER + E
CH = 4
LN_EPS = 1e-5
LORA_SCALE = 16.0 / 16.0 ** 0.5
HI, LO = 0, 1



def bank_of(stage, n, m=0):
    return {"qk": 4, "x2t": 6 + n % 2, "mid": 5, "k": m, "midt": 4, "av": 6 + m, "et": 6 + m % 2, "g": 5,
            "gated": 4, "mt": 4, "delta": 6 + n % 2, "q": n % 3, "qt": 3 + n % 2, "y": 5, "yt": 6 + n % 2}[stage]


def products(ffn, rest):
    def heads(s, n, k):
        return [(s, n, m) for m in range(k)]

    ffn_a = [("x2t", j, 0) for j in range(8)] + [("mid", 0, 0)] if ffn else []
    midt = [("midt", 0, 0)] if ffn else []
    ffn_b = [("gated", 0, 0)] if ffn else []
    ffn_c = [("delta", k, 0) for k in range(8)] if ffn else []
    if not rest:
        return ffn_a + midt + ffn_b + ffn_c
    deltas = [ffn_c[:CH], ffn_c[CH:]]
    out = [("qk", 0, 0)] + heads("k", 0, 4) + ffn_a + heads("av", 0, 2) + [("qk", 1, 0)] + midt
    out += heads("et", 0, 4) + [("g", 0, 0)] + ffn_b + heads("k", 1, 4) + heads("mt", 0, 3) + deltas[0]
    out += heads("av", 1, 2) + [("qk", 2, 0)] + heads("et", 1, 4) + [("g", 1, 0)]
    out += heads("av", 2, 2) + [("qk", 3, 0)] + heads("k", 2, 4) + heads("mt", 1, 3) + deltas[1]
    out += heads("av", 3, 2) + heads("k", 3, 4) + heads("et", 2, 4) + [("g", 2, 0)]
    out += heads("et", 3, 4) + [("g", 3, 0)] + heads("mt", 2, 3) + heads("mt", 3, 3)
    for s in range(NT_):
        out += [("q", s, 0), ("qt", s, 0), ("y", s, 0)]
    return out + [("yt", p, 0) for p in range(NT_ // 2)]


def uses(order):
    count, at = [0] * 8, {}
    for job in order:
        b = bank_of(*job)
        count[b] += 1
        at[job] = count[b]
    return count, at


FIRST, FIRST_AT = uses(products(False, True))
EACH, EACH_AT = uses(products(True, True))
_, END_AT = uses(products(True, False))


def use_number(i, stage, n=0, m=0):
    job = (stage, n, m)
    b = bank_of(*job)
    if isinstance(i, int) and i == 0:
        return FIRST_AT[job]
    if isinstance(i, int) and i == B:
        return FIRST[b] + (B - 1) * EACH[b] + END_AT[job]
    return i * EACH[b] + (FIRST[b] - EACH[b] + EACH_AT[job])


def use_before(i, stage, n=0, m=0):
    b = bank_of(stage, n, m)
    if isinstance(i, int) and i == 0:
        return None
    return i * EACH[b] + (FIRST[b] - 2 * EACH[b] + EACH_AT[(stage, n, m)])


def build(nc, x, xt, ctx, ctxt, bv_q, bv_k, bv_v, bq_col, bk_col, wqt, wkt, wvt, wot, bo, g, art, bt, out):
    with ExitStack() as stack:
        def sb(name, shape, dt=F32):
            return stack.enter_context(nc.sbuf_tensor(name, shape, dt))

        def sem(name):
            return stack.enter_context(nc.semaphore(name))

        wq = sb("wq", [P, CT_, 2, HID], F32R)
        wk = sb("wk", [P, CT_, 2, HID], F32R)
        wv = sb("wv", [P, CT_, HID])
        wo = sb("wo", [P, OT_, T])
        ar = sb("ar", [P, NT_, 2, ARW], F32R)
        b2 = sb("b2", [P, D], F32R)
        vb = sb("vb", [P, D])
        dcol = sb("dcol", [P, NT_])
        kcol = sb("kcol", [P, NT_])
        bo8 = sb("bo8", [P, T])
        ident = sb("ident", [P, P])
        halfmask = sb("halfmask", [P, 3, P])
        pairmask = sb("pairmask", [P, P])
        before = sb("before", [P, E, E])
        minus_half = sb("minus_half", [P, 2])
        g16 = sb("g16", [P, CT_])
        alpha = sb("alpha", [P, 3, H])
        ste = sb("ste", [P, 4, NT_])

        xa = sb("xa", [P, CT_, D])
        x2 = sb("x2", [P, CT_, D])
        raw = sb("raw", [P, 2, 1024])
        xt_part = sb("xt_part", [P, 2, 2, 2, T], F32R)
        xd_part = sb("xd_part", [P, 2, 2, 2, T], F32R)
        xn_part = sb("xn_part", [P, 2, CT_, HD], F32R)
        prob = sb("prob", [P, 3, P])
        prob_part = sb("prob_part", [P, 2, 3, P], F32R)
        c_part = sb("c_part", [P, 2, CT_, D], F32R)
        ct_part = sb("ct_part", [P, NT_, 2, T], F32R)
        e_buf = sb("e_buf", [P, D])
        t_part = sb("t_part", [P, 2, 2, 512], F32R)
        m_part = sb("m_part", [P, OT_, 2, T], F32R)
        xv = sb("xv", [P, CT_, HD])
        ybuf = sb("ybuf", [P, 4, T])
        gs = sb("gs", [P, T])
        gt = sb("gt", [P, CT_, P])
        cx = sb("cx", [P, P])
        midt = ybuf[:, 0, :]
        md = sb("md", [P, CT_, ARW])
        msum = ybuf[:, 3, :]
        gated = ybuf[:, 1, :].rearrange("p (t a e) -> p t a e", t=CT_, a=2)
        gated_part = m_part[:, OT_ - 1, :, :].rearrange("p s (t n) -> p s t n", t=CT_)
        kmax4 = sb("kmax4", [P, CH])
        knmax = sb("knmax", [P, 1])
        kden4 = sb("kden4", [P, CH])
        kden = sb("kden", [P, 1])
        krden = sb("krden", [P, 1])
        qmin = sb("qmin", [P, 2, LH])
        qden = sb("qden", [P, 2, LH])
        qrden = sb("qrden", [P, 2, LH])
        yss = sb("yss", [P, 2, 2])
        ln_gate = sb("ln_gate", [P, 1])
        yssm = sb("yssm", [P, 2])
        yr = sb("yr", [P, 2, 2])
        stats = sb("stats", [P, 3, CT_, CH, 6])
        mv = sb("mv", [P, 3, CT_, 2])
        ve = sb("ve", [P, 3, CT_])
        rstd = sb("rstd", [P, 3, CT_])
        nmr = sb("nmr", [P, 3, CT_])
        ggt = sb("ggt", [P, CT_, E, E])
        geq = sb("geq", [P, CT_, E, E])
        grank = sb("grank", [P, CT_, E])
        gmax = sb("gmax", [P, CT_])
        gdif = sb("gdif", [P, CT_, E])
        gexp = sb("gexp", [P, CT_, E])
        gsum = sb("gsum", [P, CT_])

        ps = [stack.enter_context(nc.psum_tensor(f"bank{b}", [P, 512], F32)) for b in range(8)]

        def bank(stage, n=0, m=0):
            return ps[bank_of(stage, n, m)]

        bank_full = [sem(f"bank_full{b}") for b in range(8)]
        bank_free = [sem(f"bank_free{b}") for b in range(8)]

        def full(i, stage, n=0, m=0):
            return bank_full[bank_of(stage, n, m)], use_number(i, stage, n, m)

        def freed(i, stage, n=0, m=0):
            return bank_free[bank_of(stage, n, m)], use_number(i, stage, n, m)

        consts_loaded = sem("consts_loaded")
        ident_made = sem("ident_made")
        pool_made = sem("pool_made")
        setup_abs = sem("setup_abs")
        setup_dve = sem("setup_dve")
        setup_done = sem("setup_done")
        raw_loaded = [sem(f"raw_loaded{k}") for k in range(2)]
        raw_used = sem("raw_used")
        x_loaded = [sem(f"x_loaded{k}") for k in range(CH)]
        stored = sem("stored")
        xt_hi, xt_d, xt_lo = sem("xt_hi"), sem("xt_d"), sem("xt_lo")
        qk_half = sem("qk_half")
        xn_hi, xn_lo = sem("xn_hi"), sem("xn_lo")
        prob_step, prob_ready = sem("prob_step"), sem("prob_ready")
        xt_dhi = sem("xt_dhi")
        c_hi, c_lo = sem("c_hi"), sem("c_lo")
        ct_hi, ct_lo = sem("ct_hi"), sem("ct_lo")
        kmax_step, kmax_ready = sem("kmax_step"), sem("kmax_ready")
        kden_step, krden_ready = sem("kden_step"), sem("krden_ready")
        et_hi, g_chunk = sem("et_hi"), sem("g_chunk")
        m_hi, m_lo = sem("m_hi"), sem("m_lo")
        res_added = sem("res_added")
        ln_stats = [sem(f"ln_stats{k}") for k in range(3)]
        ln_var = [sem(f"ln_var{k}") for k in range(3)]
        ln_rstd = [sem(f"ln_rstd{k}") for k in range(3)]
        ln_nmr = [sem(f"ln_nmr{k}") for k in range(3)]
        ln_done = [sem(f"ln_done{k}") for k in range(3)]
        x1_hi, x1_lo, xv_made = sem("x1_hi"), sem("x1_lo"), sem("xv_made")
        q_min, q_sub, q_exp, q_sum, q_rden, q_norm = sem("q_min"), sem("q_sub"), sem("q_exp"), sem("q_sum"), sem("q_rden"), sem("q_norm")
        qt_hi = sem("qt_hi")
        y_copied, y_guard, y_r, y_scaled = sem("y_copied"), sem("y_guard"), sem("y_r"), sem("y_scaled")
        x2t_hi, mid_used = sem("x2t_hi"), sem("mid_used")
        gate_step, gate_diff, gate_exp, gated_ready = sem("gate_step"), sem("gate_diff"), sem("gate_exp"), sem("gated_ready")
        gated_hi, gate_norm = sem("gated_hi"), sem("gate_norm")
        gate_order = sem("gate_order")
        delta_added = sem("delta_added")

        RAW = [("ct", 0), ("xt", 0), ("ct", 1), ("c", 0), ("ct", 2), ("c", 1), ("ct", 3), ("c", 2), ("c", 3),
               ("xt", 1), ("xt", 2), ("xt", 3)]
        NRAW = len(RAW)

        def raw_slot(kind, k):
            return raw[:, RAW.index((kind, k)) % 2, :]

        def raw_arrived(i, kind, k):
            n = RAW.index((kind, k))
            return raw_loaded[n % 2], i * (16 * NRAW // 2) + 16 * (n // 2 + 1)

        block = stack.enter_context(nc.Block())

        def rounds(engine_type, first, heads, linear, rest):
            first()
            heads(0, False)
            with nc.Fori(1, B, engines=(engine_type,), hint_back_edge=True) as i:
                linear(i - 1, i)
                heads(i, True)
            linear(B - 1, None)
            rest(B)

        @block.sync
        def _(sp):
            staged = x2[:, 0, :].rearrange("p (a n) -> p a n", a=2)
            for dst, src in ((staged[:, 0, :], wqt), (staged[:, 1, :], wkt), (wv[:], wvt), (wo[:], wot),
                             (xa[:, 0, 0:NT_ * ARW], art), (x2[:, 1, :], bt), (vb[:], bv_v), (e_buf[:], bv_q),
                             (xa[:, 1, :], bv_k), (ste[:, 0, :], bq_col), (ste[:, 1, :], bk_col),
                             (bo8[:], bo), (g16[:], g)):
                sp.dma_start(dst, src).then_inc(consts_loaded, 16)

            def load_raw(i, kind, k):
                n = RAW.index((kind, k))
                if not (isinstance(i, int) and i == 0 and n < 2):
                    sp.wait_ge(raw_used, i * NRAW + (n - 1))
                src = {"xt": xt, "c": ctx, "ct": ctxt}[kind]
                sp.dma_start(raw[:, n % 2, :], src[i, k]).then_inc(raw_loaded[n % 2], 16)

            def load_x(i, h):
                if isinstance(i, int):
                    sp.wait_ge(setup_done, 1)
                else:
                    sp.wait_ge(bank_free[bank_of("yt", 2 * h + 1)], use_before(i, "yt", 2 * h + 1))
                sp.dma_start(xa[:, :, h * HD:(h + 1) * HD], x[i, h]).then_inc(x_loaded[h], 16)

            def ahead(i):
                for n in range(7):
                    load_raw(i, *RAW[n])
                load_x(i, 0)
                load_raw(i, *RAW[7])
                load_x(i, 1)
                load_raw(i, *RAW[8])
                load_x(i, 2)
                load_raw(i, *RAW[9])
                load_x(i, 3)

            def store(i):
                for t in range(CT_):
                    sp.wait_ge(ln_done[2], (i - 1) * CT_ + t + 1)
                    sp.dma_start(out[i - 1, t], x2[:, t, :]).then_inc(stored, 16)

            def heads(i, ffn):
                load_raw(i, *RAW[10])
                load_raw(i, *RAW[11])
                if ffn:
                    store(i)

            rounds(mybir.EngineType.SP, lambda: ahead(0), heads,
                   lambda i, nxt: ahead(nxt) if nxt is not None else None, store)
            sp.wait_ge(stored, 16 * CT_ * B)

        @block.tensor
        def _(pe):
            mm = nc.tensor.matmul

            def free(i, stage, n=0, m=0):
                v = use_number(i, stage, n, m) - 1
                if not (isinstance(v, int) and v <= 0):
                    pe.wait_ge(bank_free[bank_of(stage, n, m)], v)

            def three(dst, stat, mov, first, last):
                mm(dst, stat(HI), mov(HI), start=first, stop=False)
                mm(dst, stat(HI), mov(LO), start=False, stop=False)
                return mm(dst, stat(LO), mov(HI), start=False, stop=last)

            def qk(i, h):
                free(i, "qk", h)
                dst = bank("qk", h)
                for half in range(2):
                    pe.wait_ge(xt_lo, i * 8 + 2 * h + half + 1)
                    pe.wait_ge(xt_d, i * 8 + 2 * h + half + 1)
                    for dt in range(2):
                        for s in range(CT_):
                            def stat(p):
                                return xt_part[:, half, p, dt, s * P:(s + 1) * P]

                            def mov(p):
                                return xd_part[:, half, p, dt, :]
                            o = dst[:, s * T:(s + 1) * T]
                            first = half == 0 and dt == 0 and s == 0
                            mm(o, stat(HI), mov(HI), start=first, stop=False, skip_group_check=True)
                            mm(o, stat(HI), mov(LO), start=False, stop=False, skip_group_check=True)
                            last = mm(o, stat(LO), mov(HI), start=False, stop=half == 1 and dt == 1,
                                      skip_group_check=True)
                    last.then_inc(qk_half if half == 0 else bank_full[bank_of("qk", h)], 1)

            def av(i, h):
                pe.wait_ge(prob_ready, i * H + h + 1)
                pe.wait_ge(xn_lo, i * H + h + 1)
                for t in range(CT_):
                    free(i, "av", h, t)
                    for s in range(t + 1):
                        last = three(bank("av", h, t)[:, :], lambda p: prob_part[:, p, s + t, :],
                                     lambda p: xn_part[:, p, s, :], s == 0, s == t)
                    last.then_inc(bank_full[bank_of("av", h, t)], 1)

            def kproj(i, h, between=()):
                for c in range(CH):
                    if h == 0:
                        pe.wait_ge(c_lo, i * CH + c + 1)
                    free(i, "k", h, c)
                    for k in range(CT_):
                        last = three(bank("k", h, c)[:, :], lambda p: wk[:, k, p, h * P:(h + 1) * P],
                                     lambda p: c_part[:, p, k, c * 512:(c + 1) * 512], k == 0, k == CT_ - 1)
                    last.then_inc(bank_full[bank_of("k", h, c)], 1)
                    for at, what in between:
                        if at == c:
                            what()

            def tg(i, h, between=()):
                def products_of(c):
                    if h == 0:
                        pe.wait_ge(ct_lo, i * CH + c + 1)
                    if c == 0:
                        free(i, "g", h)
                    pe.wait_ge(*freed(i, "et", h, c))
                    for n in range(4):
                        last = three(bank("g", h)[:, 0:T], lambda p: t_part[:, c % 2, p, n * P:(n + 1) * P],
                                     lambda p: ct_part[:, 4 * c + n, p, :], c == 0 and n == 0, c == 3 and n == 3)
                    last.then_inc(g_chunk if c < 3 else bank_full[bank_of("g", h)], 1)

                for c in range(CH):
                    pe.wait_ge(*freed(i, "k", h, c))
                    free(i, "et", h, c)
                    for n in range(4):
                        last = nc.tensor.transpose(bank("et", h, c)[:, n * P:(n + 1) * P],
                                                   e_buf[:, (4 * c + n) * P:(4 * c + n + 1) * P], ident[:])
                    last.then_inc(bank_full[bank_of("et", h, c)], 1)
                    if c > 0:
                        products_of(c - 1)
                        for at, what in between:
                            if at == c - 1:
                                what()
                products_of(3)

            def mt(i, h, s):
                free(i, "mt", h, s)
                dst = bank("mt", h, s)
                if s == 0:
                    pe.wait_ge(*freed(i, "g", h))
                    for k in range(CT_):
                        last = nc.tensor.transpose(dst[:, k * P:(k + 1) * P], gs[:, k * P:(k + 1) * P], ident[:])
                elif s == 1:
                    for k in range(CT_):
                        last = mm(dst[:, 0:P], wv[:, k, h * P:(h + 1) * P], gt[:, k, :], start=k == 0,
                                  stop=k == CT_ - 1)
                else:
                    last = mm(dst[:, 0:T], cx[:], wo[:, h, :], start=True, stop=True)
                last.then_inc(bank_full[bank_of("mt", h, s)], 1)

            def x2_down(i):
                def mid_of(j):
                    pe.wait_ge(*freed(i, "x2t", j))
                    if j == 0:
                        free(i, "mid")
                    for dt in range(2):
                        last = three(bank("mid")[0:ARW, 0:T], lambda p: ar[:, 2 * j + dt, p, :],
                                     lambda p: t_part[:, j % 2, p, dt * T:(dt + 1) * T],
                                     j == 0 and dt == 0, j == 7 and dt == 1)
                    last.then_inc(mid_used if j < 7 else bank_full[bank_of("mid", 0)], 1)

                for j in range(8):
                    pe.wait_ge(ln_done[1], (i - 1) * 8 + 2 * (j // 2) + 2)
                    free(i, "x2t", j)
                    for dt in range(2):
                        for t in range(CT_):
                            o = (dt * CT_ + t) * P
                            last = nc.tensor.transpose(bank("x2t", j)[:, o:o + P],
                                                       x2[:, t, (2 * j + dt) * P:(2 * j + dt + 1) * P], ident[:])
                    last.then_inc(bank_full[bank_of("x2t", j)], 1)
                    if j > 0:
                        mid_of(j - 1)
                mid_of(7)

            def mid_transpose(i):
                pe.wait_ge(*freed(i, "mid"))
                free(i, "midt")
                for t in range(CT_):
                    last = nc.tensor.transpose(bank("midt")[:, t * P:t * P + ARW], midt[0:ARW, t * P:(t + 1) * P],
                                               ident[0:ARW, 0:ARW])
                last.then_inc(bank_full[bank_of("midt", 0)], 1)

            def gated_transpose(i):
                pe.wait_ge(gated_ready, i * 4)
                free(i, "gated")
                for t in range(CT_):
                    last = nc.tensor.transpose(bank("gated")[:, t * P:(t + 1) * P],
                                               gated[:, t, :, :].rearrange("p a e -> p (a e)"), ident[:])
                last.then_inc(bank_full[bank_of("gated", 0)], 1)

            def delta(i, ks):
                for k in ks:
                    if k == 0:
                        pe.wait_ge(*freed(i, "gated"))
                    t, c = divmod(k, CH)
                    free(i, "delta", k)
                    for p in (HI, LO):
                        last = mm(bank("delta", k)[:, :], gated_part[:, p, t, :], b2[:, c * 512:(c + 1) * 512],
                                  start=p == HI, stop=p == LO)
                    last.then_inc(bank_full[bank_of("delta", k)], 1)

            def linear(i):
                for s in range(NT_ + 6):
                    if s < NT_:
                        if s % 4 == 0:
                            pe.wait_ge(x1_lo, i * CH + s // 4 + 1)
                        free(i, "q", s)
                        for k in range(CT_):
                            last = three(bank("q", s)[:, :], lambda p: c_part[:, p, k, s * P:(s + 1) * P],
                                         lambda p: wq[:, k, p, :], k == 0, k == CT_ - 1)
                        last.then_inc(bank_full[bank_of("q", s)], 1)
                    if s < 3:
                        mt(i, 3, s)
                    n = s - 3
                    if 0 <= n < NT_:
                        pe.wait_ge(q_norm, i * NT_ + n + 1)
                        free(i, "qt", n)
                        for j in range(OT_):
                            last = nc.tensor.transpose(bank("qt", n)[:, j * P:(j + 1) * P],
                                                       e_buf[:, (n % 4) * 512 + j * P:(n % 4) * 512 + (j + 1) * P],
                                                       ident[:])
                        last.then_inc(bank_full[bank_of("qt", n)], 1)
                    n = s - 4
                    if 0 <= n < NT_:
                        pe.wait_ge(*freed(i, "qt", n))
                        if n == 0:
                            pe.wait_ge(m_lo, (i + 1) * OT_)
                        free(i, "y", n)
                        for j in range(OT_):
                            last = three(bank("y", n)[:, 0:T], lambda p: t_part[:, n % 2, p, j * P:(j + 1) * P],
                                         lambda p: m_part[:, j, p, :], j == 0, j == OT_ - 1)
                        last.then_inc(bank_full[bank_of("y", n)], 1)
                    n = s - 7
                    if n >= 0 and n % 2 == 0 and n < NT_:
                        q = n // 2
                        pe.wait_ge(y_scaled, i * NT_ + n + 2)
                        free(i, "yt", q)
                        for k in range(CT_):
                            for a in range(2):
                                o = k * T + a * P
                                last = nc.tensor.transpose(bank("yt", q)[:, o:o + P],
                                                           ybuf[:, (n + a) % 4, k * P:(k + 1) * P], ident[:])
                        last.then_inc(bank_full[bank_of("yt", q)], 1)

            def heads(i, ffn):
                def with_delta(h, ks):
                    return ([(s, lambda s=s: mt(i, h, s)) for s in range(3)]
                            + ([(c, lambda k=k: delta(i, [k])) for c, k in enumerate(ks)] if ffn else []))

                qk(i, 0)
                kproj(i, 0)
                if ffn:
                    x2_down(i)
                av(i, 0)
                qk(i, 1)
                if ffn:
                    mid_transpose(i)
                tg(i, 0)
                if ffn:
                    gated_transpose(i)
                kproj(i, 1, with_delta(0, range(0, 4)))
                av(i, 1)
                qk(i, 2)
                tg(i, 1)
                av(i, 2)
                qk(i, 3)
                kproj(i, 2, with_delta(1, range(4, 8)))
                av(i, 3)
                kproj(i, 3)
                tg(i, 2)
                tg(i, 3, [(s, lambda s=s: mt(i, 2, s)) for s in range(3)])

            def rest(i):
                x2_down(i)
                mid_transpose(i)
                gated_transpose(i)
                delta(i, range(8))

            def first():
                pe.wait_ge(setup_done, 1)
                pe.wait_ge(ident_made, 2)

            rounds(mybir.EngineType.PE, first, heads, lambda i, nxt: linear(i), rest)

        @block.scalar
        def _(act):
            activation = nc.scalar.activation

            act.wait_ge(consts_loaded, 16 * 13)
            for v, src in enumerate((e_buf[:, :], xa[:, 1, :], vb[:])):
                for h in range(H):
                    activation(xv[:, 0, :], src[:, h * HD:(h + 1) * HD], ACT.Abs,
                               accum_out=alpha[:, v, h:h + 1]).then_inc(setup_abs, 1)
                    act.wait_ge(setup_abs, v * H + h + 1)

            def xt_split_hi(i, h):
                act.wait_ge(*raw_arrived(i, "xt", h))
                for half in range(2):
                    if not (isinstance(i, int) and i == 0 and h == 0):
                        if half == 0:
                            act.wait_ge(qk_half, i * H + h)
                        elif h > 0:
                            act.wait_ge(*full(i, "qk", h - 1))
                        else:
                            act.wait_ge(bank_full[4], use_before(i, "qk", 3))
                    activation(xt_part[:, half, HI, :, :].rearrange("p a t -> p (a t)"),
                               raw_slot("xt", h)[:, half * 512:(half + 1) * 512], ACT.Copy).then_inc(xt_hi, 1)

            def tanh(i, h):
                act.wait_ge(*full(i, "qk", h))
                if not (isinstance(i, int) and i == 0 and h == 0):
                    act.wait_ge(prob_ready, i * H + h)
                src = bank("qk", h)
                activation(prob[:, 0:2, :].rearrange("p a t -> p (a t)"), src[:, 0:T], ACT.Tanh,
                           scale=2.0 * HD ** -0.5)
                activation(prob[:, 2, :], src[:, T + P:2 * T], ACT.Tanh,
                           scale=2.0 * HD ** -0.5).then_inc(bank_free[bank_of("qk", h)], 1)

            def c_split_hi(i, c):
                act.wait_ge(*raw_arrived(i, "c", c))
                if not isinstance(i, int):
                    act.wait_ge(bank_full[bank_of("q", 4 * c + 3)], use_before(i, "q", 4 * c + 3))
                activation(c_part[:, HI, :, c * 512:(c + 1) * 512],
                           raw_slot("c", c).rearrange("p (k n) -> p k n", k=CT_), ACT.Copy).then_inc(c_hi, 1)

            def x2t_hi_parts(i, j):
                act.wait_ge(*full(i, "x2t", j))
                if j >= 2:
                    act.wait_ge(mid_used, (i - 1) * 7 + j - 1)
                activation(t_part[:, j % 2, HI, :], bank("x2t", j)[:, :], ACT.Copy).then_inc(x2t_hi, 1)

            def exp_keys(i, h, chunks=range(CH)):
                for c in chunks:
                    if c == 0:
                        act.wait_ge(kmax_ready, i * H + h + 1)
                        if h > 0:
                            act.wait_ge(krden_ready, i * H + h)
                    if h > 0:
                        act.wait_ge(*full(i, "et", h - 1, c))
                    activation(e_buf[:, c * 512:(c + 1) * 512], bank("k", h, c)[:, :], ACT.Exp, bias=knmax[:],
                               scale=-1.0, accum_out=kden4[:, c:c + 1]).then_inc(bank_free[c], 1)

            def et_hi_parts(i, h, c):
                act.wait_ge(*full(i, "et", h, c))
                if c >= 2:
                    act.wait_ge(g_chunk, i * 12 + h * 3 + c - 1)
                elif h > 0:
                    act.wait_ge(g_chunk, i * 12 + h * 3)
                    if c == 1:
                        act.wait_ge(*full(i, "g", h - 1))
                activation(t_part[:, c % 2, HI, :], bank("et", h, c)[:, :], ACT.Copy).then_inc(et_hi, 1)

            def g_scale(i, h):
                act.wait_ge(*full(i, "g", h))
                act.wait_ge(krden_ready, i * H + h + 1)
                if h > 0:
                    act.wait_ge(*full(i, "mt", h - 1, 0))
                activation(gs[:], bank("g", h)[:, 0:T], ACT.Copy, scale=krden[:]).then_inc(bank_free[5], 1)

            def gt_copy(i, h):
                act.wait_ge(*full(i, "mt", h, 0))
                activation(gt[:].rearrange("p k d -> p (k d)"), bank("mt", h, 0)[:, 0:T],
                           ACT.Copy).then_inc(bank_free[4], 1)

            def m_hi_part(i, h):
                act.wait_ge(*freed(i, "mt", h, 2))
                activation(m_part[:, h, HI, :], msum, ACT.Copy).then_inc(m_hi, 1)

            def xv_split_hi(i, h):
                act.wait_ge(xv_made, i * H + h + 1)
                if h > 0:
                    act.wait_ge(*full(i, "av", h - 1, 1))
                activation(xn_part[:, HI, :, :], xv[:], ACT.Copy).then_inc(xn_hi, 1)

            def mid_copies(i):
                act.wait_ge(*full(i, "mid"))
                activation(midt[0:ARW, :], bank("mid")[0:ARW, 0:T], ACT.Copy).then_inc(bank_free[5], 1)

            def md_copy(i):
                act.wait_ge(*full(i, "midt"))
                activation(md[:], bank("midt")[:, 0:T].rearrange("p (t n) -> p t n", t=CT_)[:, :, 0:ARW],
                           ACT.Copy).then_inc(bank_free[4], 1)

            def gates_exp(i):
                act.wait_ge(gate_diff, i)
                activation(gexp[:], gdif[:], ACT.Exp).then_inc(gate_exp, 1)

            def gated_hi_part(i):
                act.wait_ge(*full(i, "gated"))
                activation(gated_part[:, HI, :, :].rearrange("p t n -> p (t n)"), bank("gated")[:, 0:T],
                           ACT.Copy).then_inc(gated_hi, 1)

            def x1_split_hi(i, c):
                act.wait_ge(ln_done[0], i * 8 + 2 * c + 2)
                act.wait_ge(*full(i, "k", 3, c))
                activation(c_part[:, HI, :, c * 512:(c + 1) * 512], xa[:, :, c * 512:(c + 1) * 512],
                           ACT.Copy).then_inc(x1_hi, 1)

            def linear(i, nxt):
                ahead = {4: lambda: xt_split_hi(nxt, 0), 6: lambda: c_split_hi(nxt, 0),
                         9: lambda: c_split_hi(nxt, 1), 13: lambda: c_split_hi(nxt, 2),
                         15: lambda: xv_split_hi(nxt, 0), 18: lambda: c_split_hi(nxt, 3)}
                for s in range(NT_ + 4):
                    n = s - 3
                    if 0 <= n < NT_:
                        act.wait_ge(*full(i, "qt", n))
                        if n >= 2:
                            act.wait_ge(*full(i, "y", n - 2))
                        activation(t_part[:, n % 2, HI, :], bank("qt", n)[:, :], ACT.Copy).then_inc(qt_hi, 1)
                    if s < NT_:
                        act.wait_ge(q_sub, i * NT_ + s + 1)
                        if s >= 4:
                            act.wait_ge(*full(i, "qt", s - 4))
                        o = (s % 4) * 512
                        for h in range(AH):
                            one = activation(e_buf[:, o + h * LD:o + (h + 1) * LD],
                                             bank("q", s)[:, h * LD:(h + 1) * LD], ACT.Exp,
                                             bias=qmin[:, s % 2, h:h + 1], scale=-1.0,
                                             accum_out=qden[:, s % 2, h:h + 1])
                        one.then_inc(bank_free[bank_of("q", s)], 1)
                        rest = e_buf[:, o + AH * LD:o + 512]
                        activation(rest, rest, ACT.Exp, scale=-1.0).then_inc(q_exp, 1)
                    if s == 0:
                        m_hi_part(i, 2)
                        gt_copy(i, 3)
                    if s == 2:
                        m_hi_part(i, 3)
                    n = s - 4
                    if 0 <= n < NT_:
                        act.wait_ge(*full(i, "y", n))
                        if n >= 4:
                            act.wait_ge(*full(i, "yt", (n - 4) // 2))
                        src = bank("y", n)[:, 0:T]
                        activation(ybuf[:, n % 4, :], src, ACT.Copy).then_inc(y_copied, 1)
                        activation(src, src, ACT.Square,
                                   accum_out=yss[:, n // 2 % 2, n % 2:n % 2 + 1]).then_inc(bank_free[5], 1)
                    if nxt is not None and s in ahead:
                        ahead[s]()

            def heads(i, ffn):
                tanh(i, 0)
                for c in range(CH):
                    if ffn:
                        x2t_hi_parts(i, 2 * c)
                        x2t_hi_parts(i, 2 * c + 1)
                    exp_keys(i, 0, [c])
                xt_split_hi(i, 1)
                if ffn:
                    mid_copies(i)
                tanh(i, 1)
                if ffn:
                    md_copy(i)
                xv_split_hi(i, 1)
                et_hi_parts(i, 0, 0)
                if ffn:
                    gates_exp(i)
                for c in range(1, CH):
                    et_hi_parts(i, 0, c)
                g_scale(i, 0)
                if ffn:
                    gated_hi_part(i)
                xt_split_hi(i, 2)
                gt_copy(i, 0)
                m_hi_part(i, 0)
                exp_keys(i, 1)
                tanh(i, 2)
                xv_split_hi(i, 2)
                for c in range(CH):
                    et_hi_parts(i, 1, c)
                g_scale(i, 1)
                xt_split_hi(i, 3)
                tanh(i, 3)
                xv_split_hi(i, 3)
                gt_copy(i, 1)
                m_hi_part(i, 1)
                exp_keys(i, 2)
                for c in range(CH):
                    et_hi_parts(i, 2, c)
                g_scale(i, 2)
                exp_keys(i, 3)
                x1_split_hi(i, 0)
                et_hi_parts(i, 3, 0)
                gt_copy(i, 2)
                x1_split_hi(i, 1)
                et_hi_parts(i, 3, 1)
                x1_split_hi(i, 2)
                et_hi_parts(i, 3, 2)
                x1_split_hi(i, 3)
                et_hi_parts(i, 3, 3)
                g_scale(i, 3)

            def first():
                xt_split_hi(0, 0)
                for c in range(CH):
                    c_split_hi(0, c)
                xv_split_hi(0, 0)

            def rest(i):
                for j in range(8):
                    x2t_hi_parts(i, j)
                mid_copies(i)
                md_copy(i)
                gates_exp(i)
                gated_hi_part(i)

            rounds(mybir.EngineType.Activation, first, heads, linear, rest)

        @block.gpsimd
        def _(pool):
            tt = nc.gpsimd.tensor_tensor
            made = [0]

            def link(ins):
                made[0] += 1
                ins.then_inc(pool_made, 1)
                pool.wait_ge(pool_made, made[0])

            link(nc.gpsimd.memset(ident[:], 0.0))
            nc.gpsimd.affine_select(out=ident[:], in_=ident[:], compare_op=ALU.not_equal, fill=1.0, base=0,
                                    pattern=[[-1, P]], channel_multiplier=1).then_inc(ident_made, 1)
            link(nc.gpsimd.memset(halfmask[:], 0.5))
            for b in (0, 2):
                link(nc.gpsimd.affine_select(out=halfmask[:, b, :], in_=halfmask[:, b, :], compare_op=ALU.is_ge,
                                             fill=0.0, base=0, pattern=[[1, P]], channel_multiplier=-1))
            link(nc.gpsimd.memset(pairmask[:], 1.0))
            link(nc.gpsimd.affine_select(out=pairmask[:, 0:LD], in_=pairmask[:, 0:LD], compare_op=ALU.is_ge,
                                         fill=0.0, base=LD - 1, pattern=[[0, LD]], channel_multiplier=-1))
            link(nc.gpsimd.affine_select(out=pairmask[:, LD:P], in_=pairmask[:, LD:P], compare_op=ALU.is_ge,
                                         fill=0.0, base=-LD, pattern=[[0, LD]], channel_multiplier=1))
            link(nc.gpsimd.memset(before[:], 1.0))
            link(nc.gpsimd.affine_select(out=before[:], in_=before[:], compare_op=ALU.is_gt, fill=0.0, base=0,
                                         pattern=[[1, E], [-1, E]], channel_multiplier=0))
            nc.gpsimd.memset(minus_half[:], -0.5).then_inc(ident_made, 1)
            pool.wait_ge(ident_made, 2)

            def xt_split_lo(i, h):
                for half in range(2):
                    pool.wait_ge(xt_hi, i * 8 + 2 * h + half + 1)
                    if half == 1:
                        pool.wait_ge(xt_d, i * 8 + 2 * h + 2)
                    tt(xt_part[:, half, LO, :, :].rearrange("p a t -> p (a t)"),
                       raw_slot("xt", h)[:, half * 512:(half + 1) * 512],
                       xt_part[:, half, HI, :, :].rearrange("p a t -> p (a t)").bitcast(F32),
                       ALU.subtract).then_inc(xt_lo, 1)
                pool.wait_ge(xt_lo, i * 8 + 2 * h + 2)
                pool.sem_inc(raw_used, 1)

            def c_split_lo(i, c):
                pool.wait_ge(c_hi, i * CH + c + 1)
                tt(c_part[:, LO, :, c * 512:(c + 1) * 512], raw_slot("c", c).rearrange("p (k n) -> p k n", k=CT_),
                   c_part[:, HI, :, c * 512:(c + 1) * 512].bitcast(F32), ALU.subtract).then_inc(c_lo, 1)
                pool.wait_ge(c_lo, i * CH + c + 1)
                pool.sem_inc(raw_used, 1)

            def ct_split_lo(i, c):
                pool.wait_ge(ct_hi, i * CH + c + 1)
                tt(ct_part[:, 4 * c:4 * c + 4, LO, :], raw_slot("ct", c).rearrange("p (k n) -> p k n", k=4),
                   ct_part[:, 4 * c:4 * c + 4, HI, :].bitcast(F32), ALU.subtract).then_inc(ct_lo, 1)
                pool.wait_ge(ct_lo, i * CH + c + 1)
                pool.sem_inc(raw_used, 1)

            def xv_make(i, h):
                pool.wait_ge(x_loaded[h], i * 16 + 16)
                if not (isinstance(i, int) and i == 0 and h == 0):
                    pool.wait_ge(xn_lo, i * H + h)
                cols = slice(h * HD, (h + 1) * HD)
                tt(xv[:], xa[:, :, cols], vb[:, cols].unsqueeze(1).to_broadcast([P, CT_, HD]),
                   ALU.mult).then_inc(xv_made, 1)

            def xv_split_lo(i, h):
                pool.wait_ge(xn_hi, i * H + h + 1)
                tt(xn_part[:, LO, :, :], xv[:], xn_part[:, HI, :, :].bitcast(F32),
                   ALU.subtract).then_inc(xn_lo, 1)

            def x1_split_lo(i, c):
                pool.wait_ge(x1_hi, i * CH + c + 1)
                tt(c_part[:, LO, :, c * 512:(c + 1) * 512], xa[:, :, c * 512:(c + 1) * 512],
                   c_part[:, HI, :, c * 512:(c + 1) * 512].bitcast(F32), ALU.subtract).then_inc(x1_lo, 1)

            def root(r, which):
                pool.wait_ge(ln_var[which], r + 1)
                tt(rstd[:, which, :], ve[:, which, :], minus_half[:], ALU.pow).then_inc(ln_rstd[which], 1)

            def linear(i, nxt):
                ahead = {1: lambda: ct_split_lo(nxt, 0), 4: lambda: xt_split_lo(nxt, 0),
                         5: lambda: ct_split_lo(nxt, 1), 6: lambda: c_split_lo(nxt, 0),
                         8: lambda: ct_split_lo(nxt, 2), 9: lambda: c_split_lo(nxt, 1),
                         11: lambda: ct_split_lo(nxt, 3), 13: lambda: c_split_lo(nxt, 2),
                         14: lambda: xv_make(nxt, 0), 15: lambda: xv_split_lo(nxt, 0),
                         18: lambda: c_split_lo(nxt, 3)}
                for s in range(1, NT_ + 5):
                    n = s - 6
                    if n >= 0 and n % 2 == 0 and n < NT_:
                        q = n // 2
                        pool.wait_ge(y_guard, i * 8 + q + 1)
                        tt(yr[:, q % 2, :], yssm[:], minus_half[:], ALU.pow).then_inc(y_r, 1)
                    n = s - 1
                    if n < NT_:
                        pool.wait_ge(q_rden, i * NT_ + n + 1)
                        v = e_buf[:, (n % 4) * 512:(n % 4 + 1) * 512].rearrange("p (h d) -> p h d", h=LH)
                        tt(v, v, qrden[:, n % 2, :].unsqueeze(2).to_broadcast([P, LH, LD]),
                           ALU.mult).then_inc(q_norm, 1)
                    if nxt is not None and s in ahead:
                        ahead[s]()
                root(i, 1)

            def heads(i, ffn):
                for h in range(1, H):
                    xt_split_lo(i, h)
                    xv_make(i, h)
                    xv_split_lo(i, h)
                if ffn:
                    root(i - 1, 2)
                root(i, 0)
                for c in range(CH):
                    x1_split_lo(i, c)

            def first():
                ct_split_lo(0, 0)
                xt_split_lo(0, 0)
                ct_split_lo(0, 1)
                c_split_lo(0, 0)
                ct_split_lo(0, 2)
                c_split_lo(0, 1)
                ct_split_lo(0, 3)
                c_split_lo(0, 2)
                c_split_lo(0, 3)
                xv_make(0, 0)
                xv_split_lo(0, 0)

            rounds(mybir.EngineType.Pool, first, heads, linear, lambda i: root(i - 1, 2))

        @block.vector
        def _(dve):
            v = nc.vector
            done = [0]

            def link(ins):
                done[0] += 1
                ins.then_inc(setup_dve, 1)
                dve.wait_ge(setup_dve, done[0])

            dve.wait_ge(consts_loaded, 16 * 13)
            staged = x2[:, 0, :].rearrange("p (a n) -> p a n", a=2)
            for dst, src, k in ((wq, staged[:, 0, :], CT_), (wk, staged[:, 1, :], CT_),
                                (ar, xa[:, 0, 0:NT_ * ARW], NT_)):
                s3 = src.rearrange("p (k n) -> p k n", k=k)
                if dst is not ar:
                    link(v.tensor_scalar(s3, s3, -1.0, None, ALU.mult))
                link(v.tensor_copy(dst[:, :, HI, :], s3))
                link(v.tensor_tensor(dst[:, :, LO, :], s3, dst[:, :, HI, :].bitcast(F32), ALU.subtract))
            link(v.tensor_copy(b2[:], x2[:, 1, :]))
            link(v.tensor_tensor(b2[ER:P, :], x2[ER:P, 1, :], b2[ER:P, :].bitcast(F32), ALU.subtract))
            link(v.tensor_scalar(bo8[:], bo8[:], 1.0 / LH, None, ALU.mult))
            link(v.tensor_scalar(g16[:], g16[:], float(T) ** 0.5, None, ALU.mult))
            dve.wait_ge(setup_abs, 12)
            link(v.tensor_scalar(alpha[:], alpha[:], 1.0 / HD, None, ALU.mult))

            def ste_sign(dst, w, tmp, a):
                link(v.tensor_scalar(tmp, w, 0.0, None, ALU.is_ge))
                link(v.tensor_scalar(tmp, tmp, 2.0, -1.0, ALU.mult, ALU.add))
                link(v.scalar_tensor_tensor(tmp, tmp, a, w, ALU.mult, ALU.subtract))
                link(v.tensor_tensor(dst, tmp, w, ALU.add))

            for h in range(H):
                c4 = slice(h * DT_, (h + 1) * DT_)
                ste_sign(ste[:, 0, c4], ste[:, 0, c4], ste[:, 2, c4], alpha[:, 0, h:h + 1])
                ste_sign(ste[:, 1, c4], ste[:, 1, c4], ste[:, 3, c4], alpha[:, 1, h:h + 1])
                c5 = slice(h * HD, (h + 1) * HD)
                ste_sign(vb[:, c5], vb[:, c5], xv[:, 1, :], alpha[:, 2, h:h + 1])
            v.tensor_tensor(dcol[:], ste[:, 0, :], ste[:, 1, :], ALU.mult).then_inc(setup_dve, 1)
            dve.wait_ge(setup_dve, done[0] + 1)
            dve.sem_inc(setup_done, 1)

            def xt_split_d(i, h):
                dve.wait_ge(*raw_arrived(i, "xt", h))
                for half in range(2):
                    if not (isinstance(i, int) and i == 0 and h == 0):
                        if half == 0:
                            dve.wait_ge(qk_half, i * H + h)
                        elif h > 0:
                            dve.wait_ge(*full(i, "qk", h - 1))
                        else:
                            dve.wait_ge(bank_full[4], use_before(i, "qk", 3))
                    for dt in range(2):
                        src = raw_slot("xt", h)[:, half * 512 + dt * T:half * 512 + (dt + 1) * T]
                        col = h * DT_ + half * 2 + dt
                        v.tensor_scalar(xd_part[:, half, HI, dt, :], src, dcol[:, col:col + 1], None,
                                        ALU.mult).then_inc(xt_dhi, 1)
                    for dt in range(2):
                        src = raw_slot("xt", h)[:, half * 512 + dt * T:half * 512 + (dt + 1) * T]
                        col = h * DT_ + half * 2 + dt
                        dve.wait_ge(xt_dhi, i * 16 + (2 * h + half) * 2 + dt + 1)
                        last = v.scalar_tensor_tensor(xd_part[:, half, LO, dt, :], src, dcol[:, col:col + 1],
                                                      xd_part[:, half, HI, dt, :].bitcast(F32), ALU.mult,
                                                      ALU.subtract)
                    last.then_inc(xt_d, 1)

            def ct_split_hi(i, c):
                dve.wait_ge(*raw_arrived(i, "ct", c))
                v.tensor_copy(ct_part[:, 4 * c:4 * c + 4, HI, :],
                              raw_slot("ct", c).rearrange("p (k n) -> p k n", k=4)).then_inc(ct_hi, 1)

            def probs(i, h):
                dve.wait_ge(*freed(i, "qk", h))
                v.scalar_tensor_tensor(prob[:], prob[:], 1.0, halfmask[:], ALU.add,
                                       ALU.mult).then_inc(prob_step, 1)
                dve.wait_ge(prob_step, i * 2 * H + 2 * h + 1)
                if h > 0:
                    dve.wait_ge(*full(i, "av", h - 1, 1))
                v.tensor_copy(prob_part[:, HI, :, :], prob[:]).then_inc(prob_step, 1)
                dve.wait_ge(prob_step, i * 2 * H + 2 * h + 2)
                v.tensor_tensor(prob_part[:, LO, :, :], prob[:], prob_part[:, HI, :, :].bitcast(F32),
                                ALU.subtract).then_inc(prob_ready, 1)

            def x2t_lo_parts(i, j):
                dve.wait_ge(x2t_hi, (i - 1) * 8 + j + 1)
                v.tensor_tensor(t_part[:, j % 2, LO, :], bank("x2t", j)[:, :],
                                t_part[:, j % 2, HI, :].bitcast(F32),
                                ALU.subtract).then_inc(bank_free[bank_of("x2t", j)], 1)

            def key_min(i, h, c):
                dve.wait_ge(*full(i, "k", h, c))
                v.tensor_reduce(kmax4[:, c:c + 1], bank("k", h, c)[:, :], AX.X, ALU.min).then_inc(kmax_step, 1)
                if c == CH - 1:
                    dve.wait_ge(kmax_step, i * 16 + h * 4 + 4)
                    v.tensor_reduce(knmax[:], kmax4[:], AX.X, ALU.min).then_inc(kmax_ready, 1)

            def key_sum(i, h):
                dve.wait_ge(*freed(i, "k", h, 3))
                if h > 0:
                    dve.wait_ge(*freed(i, "g", h - 1))
                v.tensor_reduce(kden[:], kden4[:], AX.X, ALU.add).then_inc(kden_step, 1)
                dve.wait_ge(kden_step, i * 8 + h * 2 + 1)
                v.reciprocal(krden[:], kden[:]).then_inc(kden_step, 1)
                dve.wait_ge(kden_step, i * 8 + h * 2 + 2)
                v.tensor_scalar(krden[:], krden[:], LD ** -0.5, None, ALU.mult).then_inc(krden_ready, 1)

            def et_lo_parts(i, h, c):
                dve.wait_ge(et_hi, i * 16 + h * 4 + c + 1)
                v.tensor_tensor(t_part[:, c % 2, LO, :], bank("et", h, c)[:, :],
                                t_part[:, c % 2, HI, :].bitcast(F32),
                                ALU.subtract).then_inc(bank_free[bank_of("et", h, c)], 1)

            def cx_mask(i, h):
                dve.wait_ge(*full(i, "mt", h, 1))
                v.tensor_tensor(cx[:], bank("mt", h, 1)[:, 0:P], pairmask[:], ALU.mult).then_inc(bank_free[4], 1)

            def m_add(i, h):
                dve.wait_ge(*full(i, "mt", h, 2))
                v.tensor_tensor(msum, bank("mt", h, 2)[:, 0:T], bo8[:], ALU.add).then_inc(bank_free[4], 1)

            def m_lo_part(i, h):
                dve.wait_ge(m_hi, i * OT_ + h + 1)
                v.tensor_tensor(m_part[:, h, LO, :], msum, m_part[:, h, HI, :].bitcast(F32),
                                ALU.subtract).then_inc(m_lo, 1)

            def residual(i, h):
                cols = slice(h * HD, (h + 1) * HD)
                for t in range(CT_):
                    dve.wait_ge(*full(i, "av", h, t))
                    v.tensor_tensor(xa[:, t, cols], xa[:, t, cols], bank("av", h, t)[:, :],
                                    ALU.add).then_inc(bank_free[bank_of("av", h, t)], 1)
                for t in range(CT_):
                    dve.wait_ge(*freed(i, "av", h, t))
                    v.bn_stats(stats[:, 0, t, h, :], xa[:, t, cols]).then_inc(ln_stats[0], 1)

            def ln_prepare(r, w):
                dve.wait_ge(ln_stats[w], r * 10 + 8)
                v.memset(ln_gate[:], 0.0)
                for t in range(CT_):
                    v.bn_aggr(mv[:, w, t, :], stats[:, w, t, :, :].rearrange("p c s -> p (c s)")).then_inc(
                        ln_stats[w], 1)
                dve.wait_ge(ln_stats[w], r * 10 + 10)
                v.tensor_scalar(ve[:, w, :], mv[:, w, :, 1], LN_EPS, None, ALU.add).then_inc(ln_var[w], 1)

            def ln_finish(r, w):
                dve.wait_ge(ln_rstd[w], r + 1)
                v.scalar_tensor_tensor(nmr[:, w, :], mv[:, w, :, 0], -1.0, rstd[:, w, :], ALU.mult,
                                       ALU.mult).then_inc(ln_nmr[w], 1)
                dve.wait_ge(ln_nmr[w], r + 1)

            def ln_apply(buf, w, t, cols):
                v.tensor_scalar(buf[:, t, cols], buf[:, t, cols], rstd[:, w, t:t + 1], nmr[:, w, t:t + 1],
                                ALU.mult, ALU.add).then_inc(ln_done[w], 1)

            def gates(i):
                r = i - 1
                n = [0]

                def step(ins):
                    n[0] += 1
                    ins.then_inc(gate_step, 1)
                    dve.wait_ge(gate_step, r * 8 + n[0])

                dve.wait_ge(*freed(i, "midt"))
                logits = md[:, :, ER:ARW]
                step(v.tensor_reduce(gmax[:], logits, AX.X, ALU.max))
                v.tensor_tensor(gdif[:], logits, gmax[:].unsqueeze(2).to_broadcast([P, CT_, E]),
                                ALU.subtract).then_inc(gate_diff, 1)
                other = logits.unsqueeze(2).to_broadcast([P, CT_, E, E])
                own = logits.unsqueeze(3).to_broadcast([P, CT_, E, E])
                step(v.tensor_tensor(geq[:], other, own, ALU.is_equal))
                for t in range(CT_):
                    v.tensor_tensor(geq[:, t, :, :], geq[:, t, :, :], before[:], ALU.mult).then_inc(gate_order, 1)
                dve.wait_ge(gate_order, r * 2 + 2)
                step(v.tensor_tensor(ggt[:], other, own, ALU.is_gt))
                step(v.tensor_tensor(ggt[:], ggt[:], geq[:], ALU.add))
                step(v.tensor_reduce(grank[:], ggt[:], AX.X, ALU.add))
                dve.wait_ge(gate_exp, i)
                step(v.scalar_tensor_tensor(gexp[:], grank[:], TOP_K - 0.5, gexp[:], ALU.is_lt, ALU.mult))
                step(v.tensor_reduce(gsum[:], gexp[:], AX.X, ALU.add))
                step(v.reciprocal(gsum[:], gsum[:]))
                assert n[0] == 8

            def gate_mid(i):
                r = i - 1
                v.tensor_tensor(gdif[:], gexp[:], gsum[:].unsqueeze(2).to_broadcast([P, CT_, E]),
                                ALU.mult).then_inc(gate_norm, 1)
                dve.wait_ge(gate_norm, r + 1)
                for t in range(CT_):
                    for a in range(2):
                        v.scalar_tensor_tensor(gated[:, t, a, :].rearrange("p (e r) -> p e r", e=E),
                                               md[:, t, 0:ER].rearrange("p (e r) -> p e r", e=E), LORA_SCALE,
                                               gdif[:, t, :].unsqueeze(2).to_broadcast([P, E, R]),
                                               ALU.mult, ALU.mult).then_inc(gated_ready, 1)

            def gated_lo_part(i):
                dve.wait_ge(gated_hi, i)
                v.tensor_tensor(gated_part[:, LO, :, :].rearrange("p t n -> p (t n)"), bank("gated")[:, 0:T],
                                gated_part[:, HI, :, :].rearrange("p t n -> p (t n)").bitcast(F32),
                                ALU.subtract).then_inc(bank_free[4], 1)

            def ffn_out(i, k):
                r = i - 1
                t, c = divmod(k, CH)
                cols = slice(c * 512, (c + 1) * 512)
                dve.wait_ge(*full(i, "delta", k))
                v.tensor_tensor(x2[:, t, cols], x2[:, t, cols], bank("delta", k)[:, :],
                                ALU.add).then_inc(bank_free[bank_of("delta", k)], 1)
                dve.wait_ge(*freed(i, "delta", k))
                v.bn_stats(stats[:, 2, t, c, :], x2[:, t, cols]).then_inc(ln_stats[2], 1)
                if k == 7:
                    ln_prepare(r, 2)

            def ffn_norm(i):
                ln_finish(i - 1, 2)
                for t in range(CT_):
                    ln_apply(x2, 2, t, slice(0, D))

            def x2_norm(i, c):
                for t in range(CT_):
                    ln_apply(x2, 1, t, slice(c * 512, (c + 1) * 512))

            def linear(i, nxt):
                ahead = {1: lambda: ct_split_hi(nxt, 0), 4: lambda: xt_split_d(nxt, 0),
                         5: lambda: ct_split_hi(nxt, 1), 8: lambda: ct_split_hi(nxt, 2),
                         11: lambda: ct_split_hi(nxt, 3)}
                for s in range(NT_ + 7):
                    n = s - 6
                    if n >= 0 and n % 2 == 0 and n < NT_:
                        q = n // 2
                        dve.wait_ge(*freed(i, "y", n + 1))
                        if q > 0:
                            dve.wait_ge(y_r, i * 8 + q)
                        v.tensor_scalar(yssm[:], yss[:, q % 2, :], 1e-24, None, ALU.max).then_inc(y_guard, 1)
                    n = s - 7
                    if n >= 0 and n % 2 == 0 and n < NT_:
                        q = n // 2
                        dve.wait_ge(y_r, i * 8 + q + 1)
                        dve.wait_ge(y_copied, i * NT_ + n + 2)
                        for a in range(2):
                            yb = ybuf[:, (n + a) % 4, :]
                            v.tensor_scalar(yb, yb, yr[:, q % 2, a:a + 1], None, ALU.mult).then_inc(y_scaled, 1)
                    n = s - 8
                    if n >= 0 and n % 2 == 0 and n < NT_:
                        q = n // 2
                        cols = slice(q * T, (q + 1) * T)
                        dve.wait_ge(*full(i, "yt", q))
                        v.scalar_tensor_tensor(x2[:, 0, cols], bank("yt", q)[:, 0:T], g16[:, 0:1], xa[:, 0, cols],
                                               ALU.mult, ALU.add)
                        v.scalar_tensor_tensor(x2[:, 1, cols], bank("yt", q)[:, T:2 * T], g16[:, 1:2],
                                               xa[:, 1, cols], ALU.mult,
                                               ALU.add).then_inc(bank_free[bank_of("yt", q)], 1)
                        if q % 2 == 1:
                            c = q // 2
                            dve.wait_ge(*freed(i, "yt", q))
                            for t in range(CT_):
                                v.bn_stats(stats[:, 1, t, c, :], x2[:, t, c * 512:(c + 1) * 512]).then_inc(
                                    ln_stats[1], 1)
                    if s < NT_:
                        dve.wait_ge(*full(i, "q", s))
                        src = bank("q", s)[:, :].rearrange("p (h d) -> p h d", h=LH)
                        v.tensor_reduce(qmin[:, s % 2, :], src, AX.X, ALU.min).then_inc(q_min, 1)
                        dve.wait_ge(q_min, i * NT_ + s + 1)
                        if s >= 4:
                            dve.wait_ge(*full(i, "qt", s - 4))
                        v.tensor_tensor(e_buf[:, (s % 4) * 512 + AH * LD:(s % 4 + 1) * 512].rearrange(
                                            "p (h d) -> p h d", h=LH - AH), src[:, AH:LH, :],
                                        qmin[:, s % 2, AH:LH].unsqueeze(2).to_broadcast([P, LH - AH, LD]),
                                        ALU.subtract).then_inc(q_sub, 1)
                    if s == 0:
                        m_add(i, 2)
                    if s == 1:
                        m_lo_part(i, 2)
                        cx_mask(i, 3)
                    if s == 2:
                        m_add(i, 3)
                        m_lo_part(i, 3)
                    n = s - 3
                    if 0 <= n < NT_:
                        dve.wait_ge(qt_hi, i * NT_ + n + 1)
                        v.tensor_tensor(t_part[:, n % 2, LO, :], bank("qt", n)[:, :],
                                        t_part[:, n % 2, HI, :].bitcast(F32),
                                        ALU.subtract).then_inc(bank_free[bank_of("qt", n)], 1)
                    n = s - 1
                    if 0 <= n < NT_:
                        dve.wait_ge(q_exp, i * NT_ + n + 1)
                        v.tensor_reduce(qden[:, n % 2, AH:LH],
                                        e_buf[:, (n % 4) * 512 + AH * LD:(n % 4 + 1) * 512].rearrange(
                                            "p (h d) -> p h d", h=LH - AH), AX.X, ALU.add).then_inc(q_sum, 1)
                        dve.wait_ge(q_sum, i * NT_ + n + 1)
                        if n >= 2:
                            dve.wait_ge(q_norm, i * NT_ + n - 1)
                        v.reciprocal(qrden[:, n % 2, :], qden[:, n % 2, :]).then_inc(q_rden, 1)
                    if nxt is not None and s in ahead:
                        ahead[s]()
                ln_prepare(i, 1)

            def heads(i, ffn):
                probs(i, 0)
                if ffn:
                    ln_finish(i - 1, 1)
                    x2_norm(i, 0)
                for c in range(CH):
                    key_min(i, 0, c)
                if ffn:
                    for c in range(CH):
                        if c > 0:
                            x2_norm(i, c)
                        x2t_lo_parts(i, 2 * c)
                        x2t_lo_parts(i, 2 * c + 1)
                xt_split_d(i, 1)
                key_sum(i, 0)
                residual(i, 0)
                probs(i, 1)
                et_lo_parts(i, 0, 0)
                if ffn:
                    gates(i)
                    gate_mid(i)
                for c in range(1, CH):
                    et_lo_parts(i, 0, c)
                xt_split_d(i, 2)
                if ffn:
                    gated_lo_part(i)
                for c in range(CH):
                    key_min(i, 1, c)
                    if c == 1:
                        cx_mask(i, 0)
                    if c == 2:
                        m_add(i, 0)
                        m_lo_part(i, 0)
                    if ffn:
                        ffn_out(i, c)
                key_sum(i, 1)
                residual(i, 1)
                probs(i, 2)
                for c in range(CH):
                    et_lo_parts(i, 1, c)
                xt_split_d(i, 3)
                residual(i, 2)
                probs(i, 3)
                for c in range(CH):
                    key_min(i, 2, c)
                    if c == 1:
                        cx_mask(i, 1)
                    if c == 2:
                        m_add(i, 1)
                        m_lo_part(i, 1)
                    if ffn:
                        ffn_out(i, 4 + c)
                residual(i, 3)
                ln_prepare(i, 0)
                key_sum(i, 2)
                if ffn:
                    ffn_norm(i)
                ln_finish(i, 0)
                for c in range(CH):
                    key_min(i, 3, c)
                et_lo_parts(i, 2, 0)
                for c in range(CH):
                    for t in range(CT_):
                        ln_apply(xa, 0, t, slice(c * 512, (c + 1) * 512))
                    if c < 3:
                        et_lo_parts(i, 2, c + 1)
                key_sum(i, 3)
                for c in range(CH):
                    et_lo_parts(i, 3, c)
                    if c == 2:
                        cx_mask(i, 2)
                if ffn:
                    dve.wait_ge(stored, i * 16 * CT_)

            def first():
                for c in range(CH):
                    ct_split_hi(0, c)
                    if c == 0:
                        xt_split_d(0, 0)

            def rest(i):
                ln_finish(i - 1, 1)
                for c in range(CH):
                    x2_norm(i, c)
                for j in range(8):
                    x2t_lo_parts(i, j)
                gates(i)
                gate_mid(i)
                gated_lo_part(i)
                for k in range(8):
                    ffn_out(i, k)
                ffn_norm(i)

            dve.wait_ge(ident_made, 2)
            rounds(mybir.EngineType.DVE, first, heads, linear, rest)


def kernel(x, ctx_4096, L0_attn_bv_q, L0_attn_bv_k, L0_attn_bv_v, L0_xattn_Wq, L0_xattn_Wk, L0_xattn_Wv,
           L0_xattn_Wo, L0_xattn_bo, L0_xattn_g, L0_ffn_router_w, L0_ffn_A, L0_ffn_B):
    import concourse.bacc as bacc
    from concourse.bass_utils import run_bass_kernel_spmd

    def rows(v):
        return np.broadcast_to(np.asarray(v).reshape(1, -1), (P, np.asarray(v).size))

    def tiles(w, n):
        return np.asarray(w).reshape(n, P, -1).transpose(1, 0, 2).reshape(P, -1)

    def chunks(a):
        return np.asarray(a).reshape(B, CT_, P, CH, 512).transpose(0, 3, 2, 1, 4).reshape(B, CH, P, CT_ * 512)

    def turned(a):
        return np.asarray(a).transpose(0, 2, 1).reshape(B, CH, 4, P, T).transpose(0, 1, 3, 2, 4).reshape(
            B, CH, P, 4 * T)

    a_rows = np.concatenate([np.asarray(L0_ffn_A).reshape(ER, D), np.asarray(L0_ffn_router_w)], 0)
    b_rows = np.asarray(L0_ffn_B).transpose(0, 2, 1).reshape(ER, D)
    arrays = {
        "x": chunks(x), "xt": turned(x), "ctx": chunks(ctx_4096), "ctxt": turned(ctx_4096),
        "bv_q": rows(L0_attn_bv_q), "bv_k": rows(L0_attn_bv_k), "bv_v": rows(L0_attn_bv_v),
        "bq_col": np.asarray(L0_attn_bv_q).reshape(NT_, P).T, "bk_col": np.asarray(L0_attn_bv_k).reshape(NT_, P).T,
        "wqt": tiles(np.asarray(L0_xattn_Wq).T, CT_), "wkt": tiles(np.asarray(L0_xattn_Wk).T, CT_),
        "wvt": tiles(np.asarray(L0_xattn_Wv).T, CT_), "wot": tiles(np.asarray(L0_xattn_Wo).T, OT_),
        "bo": rows(L0_xattn_bo), "g": np.asarray(L0_xattn_g).reshape(CT_, P).T,
        "art": tiles(a_rows.T, NT_), "bt": np.concatenate([b_rows, b_rows], 0),
    }
    arrays = {f"in_{k}": np.ascontiguousarray(a) for k, a in arrays.items()}
    nc = bacc.Bacc("TRN2", target_bir_lowering=False, num_devices=1, dynamic_dma_scratch_size=1024)
    args = [nc.dram_tensor(k, a.shape, mybir.dt.from_np(a.dtype), kind="ExternalInput").ap()
            for k, a in arrays.items()]
    args.append(nc.dram_tensor("out", (B, CT_, P, D), F32, kind="ExternalOutput").ap())
    build(nc, *args)
    done = run_bass_kernel_spmd(nc, [arrays], core_ids=[0])
    return done.results[0]["out"].reshape(B, T, D)
```

```python
from contextlib import ExitStack

import numpy as np

import concourse.bass as bass
from concourse import mybir

F32 = mybir.dt.float32
F32R = mybir.dt.float32r
ACT = mybir.ActivationFunctionType
ALU = mybir.AluOpType
AX = mybir.AxisListType

P = 128
B, T, D = 16, 256, 2048
H, HD = 4, 512
CT_, NT_, DT_ = T // P, D // P, HD // P
HID, LH, LD = 512, 8, 64
OT_ = HID // P
E, R, ER = 4, 16, 64
TOP_K = 2
KEY_ORDER = [range(4)] * 3 + [(0, 2, 3, 1)]
AH = 4
ARW = ER + E
CH = 4
LN_EPS = 1e-5
LORA_SCALE = 16.0 / 16.0 ** 0.5
HI, LO = 0, 1



def bank_of(stage, n, m=0):
    return {"qk": 4, "av": 6 + m, "k": m, "g": 5, "mt": 4 if n < 3 else 7,
            "et": m % 2 if n < 2 else (5, 1, 6, 7)[m] if n == 2 else 6 + m % 2,
            "q": n % 3, "qt": 3 + n % 2, "y": 5 + 2 * (n % 2), "yt": 6,
            "x2t": (6, 7, 4)[n % 3], "mid": 5, "midt": 3, "gated": 2, "delta": (6, 7, 5, 4)[n % 4]}[stage]


def products(ffn, rest):
    def heads(s, n, k):
        return [(s, n, m) for m in range(k)]

    ffn_a = [("x2t", j, 0) for j in range(8)] + [("mid", 0, 0)] if ffn else []
    midt = [("midt", 0, 0)] if ffn else []
    ffn_b = [("gated", 0, 0)] if ffn else []
    ffn_c = [("delta", k, 0) for k in range(8)] if ffn else []
    if not rest:
        return ffn_a + midt + ffn_b + ffn_c
    deltas = [ffn_c[:CH], ffn_c[CH:]]

    def turned(s, *cs):
        return [("et", s, c) for c in cs]

    out = [("qk", 0, 0)] + heads("k", 0, 4) + heads("av", 0, 2) + ffn_a + turned(0, 0, 1) + [("qk", 1, 0)]
    out += midt + [("g", 0, 0)] + turned(0, 2, 3) + ffn_b + heads("k", 1, 4) + heads("mt", 0, 3) + deltas[0]
    out += heads("av", 1, 2) + turned(1, 0, 1) + [("qk", 2, 0), ("g", 1, 0)] + turned(1, 2, 3)
    out += heads("av", 2, 2) + [("qk", 3, 0)] + heads("k", 2, 4) + heads("mt", 1, 3) + deltas[1]
    out += heads("av", 3, 2) + turned(2, 0, 1) + heads("k", 3, 4) + [("g", 2, 0)] + turned(2, 2, 3)
    out += turned(3, 0, 1) + [("g", 3, 0)] + heads("mt", 2, 3) + turned(3, 2, 3) + heads("mt", 3, 3)
    for s in range(NT_):
        out += [("q", s, 0), ("qt", s, 0)]
    return out + [(s, p, 0) for p in range(NT_ // 2) for s in ("y", "yt")]


def uses(order):
    count, at = [0] * 8, {}
    for job in order:
        b = bank_of(*job)
        count[b] += 1
        at[job] = count[b]
    return count, at


FIRST, FIRST_AT = uses(products(False, True))
EACH, EACH_AT = uses(products(True, True))
_, END_AT = uses(products(True, False))


def use_number(i, stage, n=0, m=0):
    job = (stage, n, m)
    b = bank_of(*job)
    if isinstance(i, int) and i == 0:
        return FIRST_AT[job]
    if isinstance(i, int) and i == B:
        return FIRST[b] + (B - 1) * EACH[b] + END_AT[job]
    return i * EACH[b] + (FIRST[b] - EACH[b] + EACH_AT[job])


def use_before(i, stage, n=0, m=0):
    b = bank_of(stage, n, m)
    if isinstance(i, int) and i == 0:
        return None
    return i * EACH[b] + (FIRST[b] - 2 * EACH[b] + EACH_AT[(stage, n, m)])


def build(nc, x, xt, ctx, ctxt, bv_v, b_cols, wqt, wkt, wvt, wot, bo, g, art, bt, out):
    with ExitStack() as stack:
        def sb(name, shape, dt=F32):
            return stack.enter_context(nc.sbuf_tensor(name, shape, dt))

        def sem(name):
            return stack.enter_context(nc.semaphore(name))

        wq = sb("wq", [P, CT_, 2, HID], F32R)
        wk = sb("wk", [P, CT_, 2, HID], F32R)
        wv = sb("wv", [P, CT_, HID])
        wo = sb("wo", [P, OT_, T])
        ar = sb("ar", [P, NT_, 2, ARW], F32R)
        b2 = sb("b2", [P, D], F32R)
        vb = sb("vb", [P, D])
        dcol = sb("dcol", [P, NT_])
        bo8 = sb("bo8", [P, T])
        ident = sb("ident", [P, P])
        halfmask = sb("halfmask", [P, 3, P])
        pairmask = sb("pairmask", [P, P])
        before = sb("before", [P, E, E])
        minus_half = sb("minus_half", [P, 2])
        g16 = sb("g16", [P, CT_])
        alpha = sb("alpha", [P, 3, H])
        cols = sb("cols", [P, 3, NT_])
        cols_tmp = sb("cols_tmp", [P, 3, NT_])

        xa = sb("xa", [P, CT_, D])
        x2 = sb("x2", [P, CT_, D])
        raw = sb("raw", [P, 2, 1024])
        xt_part = sb("xt_part", [P, 2, 2, 2, T], F32R)
        xd_part = sb("xd_part", [P, 2, 2, 2, T], F32R)
        xn_part = sb("xn_part", [P, 2, CT_, HD], F32R)
        prob = sb("prob", [P, 3, P])
        prob_part = sb("prob_part", [P, 2, 3, P], F32R)
        c_part = sb("c_part", [P, 2, CT_, D], F32R)
        ct_part = sb("ct_part", [P, NT_, 2, T], F32R)
        e_buf = sb("e_buf", [P, D])
        t_part = sb("t_part", [P, 2, 2, 512], F32R)
        m_part = sb("m_part", [P, OT_, 2, T], F32R)
        xv = sb("xv", [P, CT_, HD])
        ybuf = sb("ybuf", [P, 4, T])
        gs = sb("gs", [P, T])
        gt = sb("gt", [P, CT_, P])
        cx = sb("cx", [P, P])
        midt = ybuf[:, 0, :]
        md = sb("md", [P, CT_, ARW])
        msum = ybuf[:, 3, :]
        gated = ybuf[:, 1, :].rearrange("p (t a e) -> p t a e", t=CT_, a=2)
        gated_part = m_part[:, OT_ - 1, :, :].rearrange("p s (t n) -> p s t n", t=CT_)
        kmax4 = sb("kmax4", [P, CH])
        knmax = sb("knmax", [P, 1])
        kden4 = sb("kden4", [P, CH])
        kden = sb("kden", [P, 1])
        krden = sb("krden", [P, 1])
        qmin = sb("qmin", [P, 2, LH])
        qden = sb("qden", [P, 2, LH])
        qrden = sb("qrden", [P, 2, LH])
        yss = sb("yss", [P, 2, 2])
        ln_gate = sb("ln_gate", [P, 1])
        yssm = sb("yssm", [P, 2])
        yr = sb("yr", [P, 2, 2])
        stats = sb("stats", [P, 3, CT_, CH, 6])
        mv = sb("mv", [P, 3, CT_, 2])
        ve = sb("ve", [P, 3, CT_])
        rstd = sb("rstd", [P, 3, CT_])
        nmr = sb("nmr", [P, 3, CT_])
        ggt = sb("ggt", [P, CT_, E, E])
        geq = sb("geq", [P, CT_, E, E])
        grank = sb("grank", [P, CT_, E])
        gmax = sb("gmax", [P, CT_])
        gdif = sb("gdif", [P, CT_, E])
        gexp = sb("gexp", [P, CT_, E])
        gsum = sb("gsum", [P, CT_])

        ps = [stack.enter_context(nc.psum_tensor(f"bank{b}", [P, 512], F32)) for b in range(8)]

        def bank(stage, n=0, m=0):
            return ps[bank_of(stage, n, m)]

        bank_full = [sem(f"bank_full{b}") for b in range(8)]
        bank_free = [sem(f"bank_free{b}") for b in range(8)]

        def full(i, stage, n=0, m=0):
            return bank_full[bank_of(stage, n, m)], use_number(i, stage, n, m)

        def freed(i, stage, n=0, m=0):
            return bank_free[bank_of(stage, n, m)], use_number(i, stage, n, m)

        cols_loaded = sem("cols_loaded")
        wk_loaded, vb_loaded, late_loaded = sem("wk_loaded"), sem("vb_loaded"), sem("late_loaded")
        ident_made = sem("ident_made")
        pool_made = sem("pool_made")
        abs_made, abs_summed = sem("abs_made"), sem("abs_summed")
        setup_dve = sem("setup_dve")
        wk_ready, vb_ready, weights_ready = sem("wk_ready"), sem("vb_ready"), sem("weights_ready")
        raw_loaded = [sem(f"raw_loaded{k}") for k in range(2)]
        raw_used = sem("raw_used")
        x_loaded = [sem(f"x_loaded{k}") for k in range(CH)]
        stored = sem("stored")
        xt_hi, xt_d, xt_lo = sem("xt_hi"), sem("xt_d"), sem("xt_lo")
        qk_half = sem("qk_half")
        xn_hi, xn_lo = sem("xn_hi"), sem("xn_lo")
        prob_step, prob_ready = sem("prob_step"), sem("prob_ready")
        xt_dhi = sem("xt_dhi")
        c_hi, c_lo = sem("c_hi"), sem("c_lo")
        ct_hi, ct_lo = sem("ct_hi"), sem("ct_lo")
        kmax_step, kmax_ready = sem("kmax_step"), sem("kmax_ready")
        kden_step, krden_ready = sem("kden_step"), sem("krden_ready")
        et_hi, g_chunk = sem("et_hi"), sem("g_chunk")
        m_hi, m_lo = sem("m_hi"), sem("m_lo")
        ln_stats = [sem(f"ln_stats{k}") for k in range(3)]
        ln_var = [sem(f"ln_var{k}") for k in range(3)]
        ln_rstd = [sem(f"ln_rstd{k}") for k in range(3)]
        ln_nmr = [sem(f"ln_nmr{k}") for k in range(3)]
        ln_done = [sem(f"ln_done{k}") for k in range(3)]
        x1_hi, x1_lo, xv_made = sem("x1_hi"), sem("x1_lo"), sem("xv_made")
        q_min, q_sub, q_exp = sem("q_min"), sem("q_sub"), sem("q_exp")
        q_sum, q_rden, q_norm = sem("q_sum"), sem("q_rden"), sem("q_norm")
        qt_hi = sem("qt_hi")
        y_made, y_square, y_guard, y_r = sem("y_made"), sem("y_square"), sem("y_guard"), sem("y_r")
        x2t_hi, mid_used = sem("x2t_hi"), sem("mid_used")
        gate_step, gate_diff, gate_exp = sem("gate_step"), sem("gate_diff"), sem("gate_exp")
        gated_ready = sem("gated_ready")
        gated_hi, gate_norm = sem("gated_hi"), sem("gate_norm")
        gate_order = sem("gate_order")
        x2_normed, x3_begun = sem("x2_normed"), sem("x3_begun")

        RAW = [("xt", 0), ("c", 0), ("c", 1), ("c", 2), ("c", 3), ("xt", 1),
               ("ct", 0), ("ct", 1), ("ct", 2), ("ct", 3), ("xt", 2), ("xt", 3)]
        NRAW = len(RAW)

        def raw_slot(kind, k):
            return raw[:, RAW.index((kind, k)) % 2, :]

        def raw_arrived(i, kind, k):
            n = RAW.index((kind, k))
            return raw_loaded[n % 2], i * (16 * NRAW // 2) + 16 * (n // 2 + 1)

        w_staged = ybuf[:].rearrange("p a t -> p (a t)")
        ar_staged = x2[:, 0, 0:NT_ * ARW]

        block = stack.enter_context(nc.Block())

        def rounds(engine_type, first, heads, linear, rest):
            first()
            heads(0, False)
            with nc.Fori(1, B, engines=(engine_type,), hint_back_edge=True) as i:
                linear(i - 1, i)
                heads(i, True)
            linear(B - 1, None)
            rest(B)

        @block.sync
        def _(sp):
            sp.dma_start(cols[:].rearrange("p v n -> p (v n)"), b_cols).then_inc(cols_loaded, 16)

            def consts():
                sp.dma_start(w_staged, wkt).then_inc(wk_loaded, 16)
                sp.dma_start(vb[:], bv_v).then_inc(vb_loaded, 16)

            def late_consts():
                sp.wait_ge(wk_ready, 1)
                for dst, src in ((w_staged, wqt), (wv[:], wvt), (wo[:], wot), (ar_staged, art), (x2[:, 1, :], bt),
                                 (bo8[:], bo), (g16[:], g)):
                    sp.dma_start(dst, src).then_inc(late_loaded, 16)

            def load_raw(i, kind, k):
                n = RAW.index((kind, k))
                if not (isinstance(i, int) and i == 0 and n < 2):
                    sp.wait_ge(raw_used, i * NRAW + (n - 1))
                src = {"xt": xt, "c": ctx, "ct": ctxt}[kind]
                sp.dma_start(raw[:, n % 2, :], src[i, k]).then_inc(raw_loaded[n % 2], 16)

            def load_x(i, h):
                if not isinstance(i, int):
                    sp.wait_ge(bank_free[bank_of("yt", 2 * h + 1)], use_before(i, "yt", 2 * h + 1))
                sp.dma_start(xa[:, :, h * HD:(h + 1) * HD], x[i, h]).then_inc(x_loaded[h], 16)

            def ahead(i):
                load_raw(i, *RAW[0])
                load_raw(i, *RAW[1])
                if isinstance(i, int):
                    consts()
                load_raw(i, *RAW[2])
                load_x(i, 0)
                load_raw(i, *RAW[3])
                load_raw(i, *RAW[4])
                load_x(i, 1)
                load_raw(i, *RAW[5])
                load_x(i, 2)
                load_raw(i, *RAW[6])
                load_x(i, 3)

            def store(i):
                for t in range(CT_):
                    sp.wait_ge(ln_done[2], (i - 1) * CT_ + t + 1)
                    sp.dma_start(out[i - 1, t], x2[:, t, :]).then_inc(stored, 16)

            def heads(i, ffn):
                for n in range(7, NRAW):
                    load_raw(i, *RAW[n])
                if ffn:
                    store(i)
                else:
                    late_consts()

            rounds(mybir.EngineType.SP, lambda: ahead(0), heads,
                   lambda i, nxt: ahead(nxt) if nxt is not None else None, store)
            sp.wait_ge(stored, 16 * CT_ * B)

        @block.tensor
        def _(pe):
            mm = nc.tensor.matmul

            def free(i, stage, n=0, m=0):
                v = use_number(i, stage, n, m) - 1
                if not (isinstance(v, int) and v <= 0):
                    pe.wait_ge(bank_free[bank_of(stage, n, m)], v)

            def three(dst, stat, mov, first, last):
                mm(dst, stat(HI), mov(HI), start=first, stop=False)
                mm(dst, stat(HI), mov(LO), start=False, stop=False)
                return mm(dst, stat(LO), mov(HI), start=False, stop=last)

            def qk(i, h):
                free(i, "qk", h)
                dst = bank("qk", h)
                for half in range(2):
                    pe.wait_ge(xt_lo, i * 8 + 2 * h + half + 1)
                    pe.wait_ge(xt_d, i * 8 + 2 * h + half + 1)
                    for dt in range(2):
                        for s in range(CT_):
                            def stat(p):
                                return xt_part[:, half, p, dt, s * P:(s + 1) * P]

                            def mov(p):
                                return xd_part[:, half, p, dt, :]
                            o = dst[:, s * T:(s + 1) * T]
                            first = half == 0 and dt == 0 and s == 0
                            mm(o, stat(HI), mov(HI), start=first, stop=False, skip_group_check=True)
                            mm(o, stat(HI), mov(LO), start=False, stop=False, skip_group_check=True)
                            last = mm(o, stat(LO), mov(HI), start=False, stop=half == 1 and dt == 1,
                                      skip_group_check=True)
                    last.then_inc(qk_half if half == 0 else bank_full[bank_of("qk", h)], 1)

            def av(i, h):
                pe.wait_ge(prob_ready, i * H + h + 1)
                pe.wait_ge(xn_lo, (i * H + h) * 2 + 2)
                for t in range(CT_):
                    free(i, "av", h, t)
                    for s in range(t + 1):
                        last = three(bank("av", h, t)[:, :], lambda p: prob_part[:, p, s + t, :],
                                     lambda p: xn_part[:, p, s, :], s == 0, s == t)
                    last.then_inc(bank_full[bank_of("av", h, t)], 1)

            def kproj(i, h, between=()):
                for c in KEY_ORDER[h]:
                    if h == 0:
                        pe.wait_ge(c_lo, i * 2 * CH + 2 * c + 2)
                    free(i, "k", h, c)
                    for k in range(CT_):
                        last = three(bank("k", h, c)[:, :], lambda p: wk[:, k, p, h * P:(h + 1) * P],
                                     lambda p: c_part[:, p, k, c * 512:(c + 1) * 512], k == 0, k == CT_ - 1)
                    last.then_inc(bank_full[bank_of("k", h, c)], 1)
                    for at, what in between:
                        if at == c:
                            what()

            def keys_turned(i, h, c):
                pe.wait_ge(*freed(i, "k", h, c))
                free(i, "et", h, c)
                for n in range(4):
                    last = nc.tensor.transpose(bank("et", h, c)[:, n * P:(n + 1) * P],
                                               e_buf[:, (4 * c + n) * P:(4 * c + n + 1) * P], ident[:])
                last.then_inc(bank_full[bank_of("et", h, c)], 1)

            def context(i, h, c, turn=None):
                if h == 0:
                    pe.wait_ge(ct_lo, i * CH + c + 1)
                if c == 0:
                    free(i, "g", h)
                pe.wait_ge(*freed(i, "et", h, c))
                if turn is not None:
                    keys_turned(i, *turn)
                for n in range(4):
                    last = three(bank("g", h)[:, 0:T], lambda p: t_part[:, c % 2, p, n * P:(n + 1) * P],
                                 lambda p: ct_part[:, 4 * c + n, p, :], c == 0 and n == 0, c == 3 and n == 3)
                last.then_inc(g_chunk if c < 3 else bank_full[bank_of("g", h)], 1)

            def contexts(i, h):
                context(i, h, 0, (h, 2))
                context(i, h, 1, (h, 3))
                context(i, h, 2)
                context(i, h, 3)

            def mt(i, h, s):
                free(i, "mt", h, s)
                dst = bank("mt", h, s)
                if s == 0:
                    pe.wait_ge(*freed(i, "g", h))
                    for k in range(CT_):
                        last = nc.tensor.transpose(dst[:, k * P:(k + 1) * P], gs[:, k * P:(k + 1) * P], ident[:])
                elif s == 1:
                    for k in range(CT_):
                        last = mm(dst[:, 0:P], wv[:, k, h * P:(h + 1) * P], gt[:, k, :], start=k == 0,
                                  stop=k == CT_ - 1)
                else:
                    last = mm(dst[:, 0:T], cx[:], wo[:, h, :], start=True, stop=True)
                last.then_inc(bank_full[bank_of("mt", h, s)], 1)

            def x2_turned(i, j):
                pe.wait_ge(ln_done[1], (i - 1) * CH + j // 2 + 1)
                pe.wait_ge(x2_normed, (i - 1) * CH + j // 2 + 1)
                free(i, "x2t", j)
                for dt in range(2):
                    for t in range(CT_):
                        o = (dt * CT_ + t) * P
                        last = nc.tensor.transpose(bank("x2t", j)[:, o:o + P],
                                                   x2[:, t, (2 * j + dt) * P:(2 * j + dt + 1) * P], ident[:])
                last.then_inc(bank_full[bank_of("x2t", j)], 1)

            def x2_down(i):
                for j in range(8):
                    if j < 6:
                        x2_turned(i, j + 2)
                    pe.wait_ge(*freed(i, "x2t", j))
                    if j == 0:
                        free(i, "mid")
                    for dt in range(2):
                        last = three(bank("mid")[0:ARW, 0:T], lambda p: ar[:, 2 * j + dt, p, :],
                                     lambda p: t_part[:, j % 2, p, dt * T:(dt + 1) * T],
                                     j == 0 and dt == 0, j == 7 and dt == 1)
                    last.then_inc(mid_used if j < 7 else bank_full[bank_of("mid", 0)], 1)

            def mid_transpose(i):
                pe.wait_ge(*freed(i, "mid"))
                free(i, "midt")
                for t in range(CT_):
                    last = nc.tensor.transpose(bank("midt")[:, t * P:t * P + ARW], midt[0:ARW, t * P:(t + 1) * P],
                                               ident[0:ARW, 0:ARW])
                last.then_inc(bank_full[bank_of("midt", 0)], 1)

            def gated_transpose(i):
                pe.wait_ge(gated_ready, i * 4)
                free(i, "gated")
                for t in range(CT_):
                    last = nc.tensor.transpose(bank("gated")[:, t * P:(t + 1) * P],
                                               gated[:, t, :, :].rearrange("p a e -> p (a e)"), ident[:])
                last.then_inc(bank_full[bank_of("gated", 0)], 1)

            def delta(i, ks):
                for k in ks:
                    if k == 0:
                        pe.wait_ge(*freed(i, "gated"))
                    t, c = divmod(k, CH)
                    free(i, "delta", k)
                    for p in (HI, LO):
                        last = mm(bank("delta", k)[:, :], gated_part[:, p, t, :], b2[:, c * 512:(c + 1) * 512],
                                  start=p == HI, stop=p == LO)
                    last.then_inc(bank_full[bank_of("delta", k)], 1)

            def q_product(i, s):
                if s % 4 == 0:
                    pe.wait_ge(x1_lo, i * CH + s // 4 + 1)
                free(i, "q", s)
                for k in range(CT_):
                    last = three(bank("q", s)[:, :], lambda p: c_part[:, p, k, s * P:(s + 1) * P],
                                 lambda p: wq[:, k, p, :], k == 0, k == CT_ - 1)
                last.then_inc(bank_full[bank_of("q", s)], 1)

            def linear(i, nxt):
                for s in range(3, NT_ + 7):
                    if s == 3:
                        mt(i, 3, 0)
                    if s < NT_:
                        q_product(i, s)
                    if s == 3:
                        mt(i, 3, 1)
                    n = s - 3
                    if 0 <= n < NT_:
                        pe.wait_ge(q_norm, i * NT_ + n + 1)
                        free(i, "qt", n)
                        for j in range(OT_):
                            last = nc.tensor.transpose(bank("qt", n)[:, j * P:(j + 1) * P],
                                                       e_buf[:, (n % 4) * 512 + j * P:(n % 4) * 512 + (j + 1) * P],
                                                       ident[:])
                        last.then_inc(bank_full[bank_of("qt", n)], 1)
                    if s == 3:
                        mt(i, 3, 2)
                    n = s - 4
                    if 0 <= n < NT_:
                        pe.wait_ge(*freed(i, "qt", n))
                        if n == 0:
                            pe.wait_ge(m_lo, i * OT_ + OT_ - 1)
                        pair, a = divmod(n, 2)
                        if a == 0:
                            free(i, "y", pair)
                        for j in range(OT_):
                            if n == 0 and j == OT_ - 1:
                                pe.wait_ge(m_lo, (i + 1) * OT_)
                            last = three(bank("y", pair)[:, a * T:(a + 1) * T],
                                         lambda p: t_part[:, n % 2, p, j * P:(j + 1) * P],
                                         lambda p: m_part[:, j, p, :], j == 0, j == OT_ - 1)
                        last.then_inc(y_made if a == 0 else bank_full[bank_of("y", pair)], 1)
                    q, a = divmod(s - 8, 2)
                    if a == 0 and 0 <= q < NT_ // 2:
                        if q == NT_ // 2 - 1 and nxt is not None:
                            qk(nxt, 0)
                        pe.wait_ge(*freed(i, "y", q))
                        free(i, "yt", q)
                        for k in range(CT_):
                            for a in range(2):
                                o = k * T + a * P
                                last = nc.tensor.transpose(bank("yt", q)[:, o:o + P],
                                                           ybuf[:, (2 * q + a) % 4, k * P:(k + 1) * P], ident[:])
                        last.then_inc(bank_full[bank_of("yt", q)], 1)

            def heads(i, ffn):
                def with_delta(h, ks):
                    return ([(s, lambda s=s: mt(i, h, s)) for s in range(3)]
                            + ([(c, lambda k=k: delta(i, [k])) for c, k in zip((1, 2, 3, 3), ks)] if ffn else []))

                def turned_first(h):
                    keys_turned(i, h, 0)
                    keys_turned(i, h, 1)

                if not ffn:
                    pe.wait_ge(wk_ready, 1)
                kproj(i, 0)
                av(i, 0)
                if ffn:
                    x2_turned(i, 0)
                    x2_turned(i, 1)
                    x2_down(i)
                turned_first(0)
                if ffn:
                    mid_transpose(i)
                qk(i, 1)
                contexts(i, 0)
                if ffn:
                    gated_transpose(i)
                if not ffn:
                    pe.wait_ge(late_loaded, 16 * 7)
                kproj(i, 1, with_delta(0, range(0, 4)))
                av(i, 1)
                turned_first(1)
                qk(i, 2)
                contexts(i, 1)
                av(i, 2)
                qk(i, 3)
                kproj(i, 2, with_delta(1, range(4, 8)))
                av(i, 3)
                turned_first(2)
                kproj(i, 3)
                context(i, 2, 0, (2, 2))
                context(i, 2, 1, (2, 3))
                context(i, 2, 2)
                keys_turned(i, 3, 0)
                context(i, 2, 3)
                keys_turned(i, 3, 1)
                context(i, 3, 0, (3, 2))
                mt(i, 2, 0)
                if not ffn:
                    pe.wait_ge(weights_ready, 1)
                q_product(i, 0)
                context(i, 3, 1, (3, 3))
                mt(i, 2, 1)
                context(i, 3, 2)
                q_product(i, 1)
                mt(i, 2, 2)
                context(i, 3, 3)
                q_product(i, 2)

            def rest(i):
                x2_turned(i, 0)
                x2_turned(i, 1)
                x2_down(i)
                mid_transpose(i)
                gated_transpose(i)
                delta(i, range(8))

            def first():
                pe.wait_ge(ident_made, 2)
                pe.wait_ge(abs_made, 1)
                mm(ps[7][:, 0:3 * NT_], gs[:, 0:P], cols_tmp[:].rearrange("p v n -> p (v n)"), start=True,
                   stop=True).then_inc(abs_summed, 1)
                qk(0, 0)

            rounds(mybir.EngineType.PE, first, heads, linear, rest)

        @block.scalar
        def _(act):
            activation = nc.scalar.activation

            act.wait_ge(cols_loaded, 16)
            activation(cols_tmp[:], cols[:], ACT.Abs).then_inc(abs_made, 1)

            def xt_split_hi(i, h):
                act.wait_ge(*raw_arrived(i, "xt", h))
                for half in range(2):
                    if not (isinstance(i, int) and i == 0 and h == 0):
                        if half == 0:
                            act.wait_ge(qk_half, i * H + h)
                        elif h > 0:
                            act.wait_ge(*full(i, "qk", h - 1))
                        else:
                            act.wait_ge(bank_full[bank_of("qk", 3)], use_before(i, "qk", 3))
                    activation(xt_part[:, half, HI, :, :].rearrange("p a t -> p (a t)"),
                               raw_slot("xt", h)[:, half * 512:(half + 1) * 512], ACT.Copy).then_inc(xt_hi, 1)

            def tanh(i, h):
                act.wait_ge(*full(i, "qk", h))
                if not (isinstance(i, int) and i == 0 and h == 0):
                    act.wait_ge(prob_ready, i * H + h)
                src = bank("qk", h)
                activation(prob[:, 0:2, :].rearrange("p a t -> p (a t)"), src[:, 0:T], ACT.Tanh,
                           scale=2.0 * HD ** -0.5)
                activation(prob[:, 2, :], src[:, T + P:2 * T], ACT.Tanh,
                           scale=2.0 * HD ** -0.5).then_inc(bank_free[bank_of("qk", h)], 1)

            def c_split_hi(i, c):
                act.wait_ge(*raw_arrived(i, "c", c))
                if not isinstance(i, int):
                    act.wait_ge(bank_full[bank_of("q", 4 * c + 3)], use_before(i, "q", 4 * c + 3))
                activation(c_part[:, HI, :, c * 512:(c + 1) * 512],
                           raw_slot("c", c).rearrange("p (k n) -> p k n", k=CT_), ACT.Copy).then_inc(c_hi, 1)

            def ct_split_hi(i, c):
                act.wait_ge(*raw_arrived(i, "ct", c))
                activation(ct_part[:, 4 * c:4 * c + 4, HI, :], raw_slot("ct", c).rearrange("p (k n) -> p k n", k=4),
                           ACT.Copy).then_inc(ct_hi, 1)

            def x2t_hi_parts(i, j):
                act.wait_ge(*full(i, "x2t", j))
                if j >= 2:
                    act.wait_ge(mid_used, (i - 1) * 7 + j - 1)
                activation(t_part[:, j % 2, HI, :], bank("x2t", j)[:, :], ACT.Copy).then_inc(x2t_hi, 1)

            def exp_keys(i, h, chunks=range(CH)):
                for c in chunks:
                    if c == 0:
                        act.wait_ge(kmax_ready, i * H + h + 1)
                        if h > 0:
                            act.wait_ge(krden_ready, i * H + h)
                    if h > 0:
                        act.wait_ge(*full(i, "et", h - 1, c))
                    activation(e_buf[:, c * 512:(c + 1) * 512], bank("k", h, c)[:, :], ACT.Exp, bias=knmax[:],
                               scale=-1.0, accum_out=kden4[:, c:c + 1]).then_inc(bank_free[bank_of("k", h, c)], 1)

            def et_hi_parts(i, h, c):
                act.wait_ge(*full(i, "et", h, c))
                if c >= 2:
                    act.wait_ge(g_chunk, i * 12 + h * 3 + c - 1)
                elif h > 0:
                    act.wait_ge(g_chunk, i * 12 + h * 3)
                    if c == 1:
                        act.wait_ge(*full(i, "g", h - 1))
                activation(t_part[:, c % 2, HI, :], bank("et", h, c)[:, :], ACT.Copy).then_inc(et_hi, 1)

            def g_scale(i, h):
                act.wait_ge(*full(i, "g", h))
                act.wait_ge(krden_ready, i * H + h + 1)
                if h > 0:
                    act.wait_ge(*full(i, "mt", h - 1, 0))
                activation(gs[:], bank("g", h)[:, 0:T], ACT.Copy,
                           scale=krden[:]).then_inc(bank_free[bank_of("g", h)], 1)

            def gt_copy(i, h):
                act.wait_ge(*full(i, "mt", h, 0))
                activation(gt[:].rearrange("p k d -> p (k d)"), bank("mt", h, 0)[:, 0:T],
                           ACT.Copy).then_inc(bank_free[bank_of("mt", h)], 1)

            def m_hi_part(i, h):
                act.wait_ge(*freed(i, "mt", h, 2))
                activation(m_part[:, h, HI, :], msum, ACT.Copy).then_inc(m_hi, 1)

            def xv_split_hi(i, h):
                act.wait_ge(xv_made, (i * H + h) * 2 + 2)
                if h > 0:
                    act.wait_ge(*full(i, "av", h - 1, 1))
                activation(xn_part[:, HI, :, :], xv[:], ACT.Copy).then_inc(xn_hi, 1)

            def mid_copies(i):
                act.wait_ge(*full(i, "mid"))
                activation(midt[0:ARW, :], bank("mid")[0:ARW, 0:T],
                           ACT.Copy).then_inc(bank_free[bank_of("mid", 0)], 1)

            def md_copy(i):
                act.wait_ge(*full(i, "midt"))
                activation(md[:], bank("midt")[:, 0:T].rearrange("p (t n) -> p t n", t=CT_)[:, :, 0:ARW],
                           ACT.Copy).then_inc(bank_free[bank_of("midt", 0)], 1)

            def gates_exp(i):
                act.wait_ge(gate_diff, i)
                activation(gexp[:], gdif[:], ACT.Exp).then_inc(gate_exp, 1)

            def gated_hi_part(i):
                act.wait_ge(*full(i, "gated"))
                activation(gated_part[:, HI, :, :].rearrange("p t n -> p (t n)"), bank("gated")[:, 0:T],
                           ACT.Copy).then_inc(gated_hi, 1)

            def x1_split_hi(i, c):
                act.wait_ge(ln_done[0], i * 8 + 2 * c + 2)
                act.wait_ge(*full(i, "k", 3, c))
                activation(c_part[:, HI, :, c * 512:(c + 1) * 512], xa[:, :, c * 512:(c + 1) * 512],
                           ACT.Copy).then_inc(x1_hi, 1)

            def x2_norm(i, c):
                if c == 0:
                    act.wait_ge(ln_nmr[1], i)
                cols = slice(c * 512, (c + 1) * 512)
                activation(x2[:, 1, cols], x2[:, 1, cols], ACT.Identity, bias=nmr[:, 1, 1:2],
                           scale=rstd[:, 1, 1:2]).then_inc(x2_normed, 1)

            def q_exps(i, s):
                act.wait_ge(q_sub, i * NT_ + s + 1)
                if s >= 4:
                    act.wait_ge(*full(i, "qt", s - 4))
                else:
                    act.wait_ge(*full(i, "et", 3, s))
                o = (s % 4) * 512
                for h in range(AH):
                    one = activation(e_buf[:, o + h * LD:o + (h + 1) * LD],
                                     bank("q", s)[:, h * LD:(h + 1) * LD], ACT.Exp,
                                     bias=qmin[:, s % 2, h:h + 1], scale=-1.0,
                                     accum_out=qden[:, s % 2, h:h + 1])
                one.then_inc(bank_free[bank_of("q", s)], 1)
                rest = e_buf[:, o + AH * LD:o + 512]
                activation(rest, rest, ACT.Exp, scale=-1.0).then_inc(q_exp, 1)

            def linear(i, nxt):
                ahead = {4: lambda: xt_split_hi(nxt, 0), 6: lambda: c_split_hi(nxt, 0),
                         9: lambda: c_split_hi(nxt, 1), 13: lambda: c_split_hi(nxt, 2),
                         18: lambda: c_split_hi(nxt, 3), 19: lambda: xv_split_hi(nxt, 0)}
                for s in range(3, NT_ + 5):
                    n = s - 3
                    if 0 <= n < NT_:
                        act.wait_ge(*full(i, "qt", n))
                        if n >= 2 and n % 2 == 0:
                            act.wait_ge(y_made, i * (NT_ // 2) + n // 2)
                        elif n >= 2:
                            act.wait_ge(*full(i, "y", (n - 2) // 2))
                        activation(t_part[:, n % 2, HI, :], bank("qt", n)[:, :], ACT.Copy).then_inc(qt_hi, 1)
                    if s == 3:
                        m_hi_part(i, 3)
                    if s < NT_:
                        q_exps(i, s)
                    if s == 5:
                        x1_split_hi(i, 3)
                    q, a = divmod(s - 6, 2)
                    if a == 0 and 0 <= q < NT_ // 2:
                        act.wait_ge(y_r, i * (NT_ // 2) + q + 1)
                        for a in range(2):
                            last = activation(ybuf[:, (2 * q + a) % 4, :], bank("y", q)[:, a * T:(a + 1) * T],
                                              ACT.Copy, scale=yr[:, q % 2, a:a + 1])
                        last.then_inc(bank_free[bank_of("y", q)], 1)
                    q, a = divmod(s - 5, 2)
                    if a == 0 and 0 <= q < NT_ // 2:
                        act.wait_ge(*full(i, "y", q))
                        if q >= 2:
                            act.wait_ge(*full(i, "yt", q - 2))
                        for a in range(2):
                            activation(ybuf[:, (2 * q + a) % 4, :], bank("y", q)[:, a * T:(a + 1) * T], ACT.Square,
                                       accum_out=yss[:, q % 2, a:a + 1]).then_inc(y_square, 1)
                    if nxt is not None and s in ahead:
                        ahead[s]()
                if nxt is not None:
                    tanh(nxt, 0)
                    xt_split_hi(nxt, 1)

            def heads(i, ffn):
                ct_split_hi(i, 0)
                if ffn:
                    x2_norm(i, 0)
                    x2_norm(i, 1)
                    x2t_hi_parts(i, 0)
                    x2t_hi_parts(i, 1)
                    x2_norm(i, 2)
                    x2_norm(i, 3)
                    x2t_hi_parts(i, 2)
                    x2t_hi_parts(i, 3)
                ct_split_hi(i, 1)
                if ffn:
                    x2t_hi_parts(i, 4)
                    x2t_hi_parts(i, 5)
                    x2t_hi_parts(i, 6)
                exp_keys(i, 0, [0])
                if ffn:
                    x2t_hi_parts(i, 7)
                exp_keys(i, 0, [1, 2, 3])
                if ffn:
                    mid_copies(i)
                et_hi_parts(i, 0, 0)
                et_hi_parts(i, 0, 1)
                ct_split_hi(i, 2)
                if ffn:
                    md_copy(i)
                    gates_exp(i)
                ct_split_hi(i, 3)
                tanh(i, 1)
                et_hi_parts(i, 0, 2)
                et_hi_parts(i, 0, 3)
                xt_split_hi(i, 2)
                xv_split_hi(i, 1)
                g_scale(i, 0)
                if ffn:
                    gated_hi_part(i)
                gt_copy(i, 0)
                m_hi_part(i, 0)
                exp_keys(i, 1, [0, 1, 2])
                et_hi_parts(i, 1, 0)
                exp_keys(i, 1, [3])
                et_hi_parts(i, 1, 1)
                xv_split_hi(i, 2)
                tanh(i, 2)
                et_hi_parts(i, 1, 2)
                et_hi_parts(i, 1, 3)
                xt_split_hi(i, 3)
                g_scale(i, 1)
                tanh(i, 3)
                xv_split_hi(i, 3)
                gt_copy(i, 1)
                m_hi_part(i, 1)
                exp_keys(i, 2, [0, 1, 2])
                et_hi_parts(i, 2, 0)
                et_hi_parts(i, 2, 1)
                exp_keys(i, 2, [3])
                et_hi_parts(i, 2, 2)
                exp_keys(i, 3, [0])
                et_hi_parts(i, 2, 3)
                exp_keys(i, 3, [1, 2, 3])
                et_hi_parts(i, 3, 0)
                x1_split_hi(i, 0)
                g_scale(i, 2)
                et_hi_parts(i, 3, 1)
                et_hi_parts(i, 3, 2)
                gt_copy(i, 2)
                q_exps(i, 0)
                et_hi_parts(i, 3, 3)
                x1_split_hi(i, 1)
                q_exps(i, 1)
                g_scale(i, 3)
                m_hi_part(i, 2)
                gt_copy(i, 3)
                q_exps(i, 2)
                x1_split_hi(i, 2)

            def first():
                xt_split_hi(0, 0)
                for c in range(CH):
                    c_split_hi(0, c)
                xv_split_hi(0, 0)
                tanh(0, 0)
                xt_split_hi(0, 1)

            def rest(i):
                for c in range(CH):
                    x2_norm(i, c)
                for j in range(8):
                    x2t_hi_parts(i, j)
                mid_copies(i)
                md_copy(i)
                gates_exp(i)
                gated_hi_part(i)

            rounds(mybir.EngineType.Activation, first, heads, linear, rest)

        @block.gpsimd
        def _(pool):
            tt = nc.gpsimd.tensor_tensor
            made = [0]

            def link(ins):
                made[0] += 1
                ins.then_inc(pool_made, 1)
                pool.wait_ge(pool_made, made[0])

            link(nc.gpsimd.memset(gs[:], 1.0))
            link(nc.gpsimd.memset(ident[:], 0.0))
            nc.gpsimd.affine_select(out=ident[:], in_=ident[:], compare_op=ALU.not_equal, fill=1.0, base=0,
                                    pattern=[[-1, P]], channel_multiplier=1).then_inc(ident_made, 1)
            link(nc.gpsimd.memset(halfmask[:], 0.5))
            for b in (0, 2):
                link(nc.gpsimd.affine_select(out=halfmask[:, b, :], in_=halfmask[:, b, :], compare_op=ALU.is_ge,
                                             fill=0.0, base=0, pattern=[[1, P]], channel_multiplier=-1))
            link(nc.gpsimd.memset(pairmask[:], 1.0))
            link(nc.gpsimd.affine_select(out=pairmask[:, 0:LD], in_=pairmask[:, 0:LD], compare_op=ALU.is_ge,
                                         fill=0.0, base=LD - 1, pattern=[[0, LD]], channel_multiplier=-1))
            link(nc.gpsimd.affine_select(out=pairmask[:, LD:P], in_=pairmask[:, LD:P], compare_op=ALU.is_ge,
                                         fill=0.0, base=-LD, pattern=[[0, LD]], channel_multiplier=1))
            link(nc.gpsimd.memset(before[:], 1.0))
            link(nc.gpsimd.affine_select(out=before[:], in_=before[:], compare_op=ALU.is_gt, fill=0.0, base=0,
                                         pattern=[[1, E], [-1, E]], channel_multiplier=0))
            nc.gpsimd.memset(minus_half[:], -0.5).then_inc(ident_made, 1)
            pool.wait_ge(ident_made, 2)

            def xt_split_lo(i, h, halves=range(2)):
                for half in halves:
                    pool.wait_ge(xt_hi, i * 8 + 2 * h + half + 1)
                    if half == 1:
                        pool.wait_ge(xt_d, i * 8 + 2 * h + 2)
                    tt(xt_part[:, half, LO, :, :].rearrange("p a t -> p (a t)"),
                       raw_slot("xt", h)[:, half * 512:(half + 1) * 512],
                       xt_part[:, half, HI, :, :].rearrange("p a t -> p (a t)").bitcast(F32),
                       ALU.subtract).then_inc(xt_lo, 1)
                if 1 in halves:
                    pool.wait_ge(xt_lo, i * 8 + 2 * h + 2)
                    pool.sem_inc(raw_used, 1)

            def c_split_lo(i, c, tiles=range(CT_)):
                if 0 in tiles:
                    pool.wait_ge(c_hi, i * CH + c + 1)
                cols = slice(c * 512, (c + 1) * 512)
                for t in tiles:
                    tt(c_part[:, LO, t, cols], raw_slot("c", c)[:, t * 512:(t + 1) * 512],
                       c_part[:, HI, t, cols].bitcast(F32), ALU.subtract).then_inc(c_lo, 1)
                if 1 in tiles:
                    pool.wait_ge(c_lo, i * 2 * CH + 2 * c + 2)
                    pool.sem_inc(raw_used, 1)

            def ct_split_lo(i, c):
                pool.wait_ge(ct_hi, i * CH + c + 1)
                tt(ct_part[:, 4 * c:4 * c + 4, LO, :], raw_slot("ct", c).rearrange("p (k n) -> p k n", k=4),
                   ct_part[:, 4 * c:4 * c + 4, HI, :].bitcast(F32), ALU.subtract).then_inc(ct_lo, 1)
                pool.wait_ge(ct_lo, i * CH + c + 1)
                pool.sem_inc(raw_used, 1)

            def xv_make(i, h, tiles=range(CT_)):
                if 0 in tiles:
                    pool.wait_ge(x_loaded[h], i * 16 + 16)
                    if not (isinstance(i, int) and i == 0 and h == 0):
                        pool.wait_ge(xn_lo, (i * H + h) * 2)
                cols = slice(h * HD, (h + 1) * HD)
                for t in tiles:
                    tt(xv[:, t, :], xa[:, t, cols], vb[:, cols], ALU.mult).then_inc(xv_made, 1)

            def xv_split_lo(i, h, tiles=range(CT_)):
                if 0 in tiles:
                    pool.wait_ge(xn_hi, i * H + h + 1)
                for t in tiles:
                    tt(xn_part[:, LO, t, :], xv[:, t, :], xn_part[:, HI, t, :].bitcast(F32),
                       ALU.subtract).then_inc(xn_lo, 1)

            def x1_split_lo(i, c):
                pool.wait_ge(x1_hi, i * CH + c + 1)
                tt(c_part[:, LO, :, c * 512:(c + 1) * 512], xa[:, :, c * 512:(c + 1) * 512],
                   c_part[:, HI, :, c * 512:(c + 1) * 512].bitcast(F32), ALU.subtract).then_inc(x1_lo, 1)

            def root(r, which):
                pool.wait_ge(ln_var[which], r + 1)
                tt(rstd[:, which, :], ve[:, which, :], minus_half[:], ALU.pow).then_inc(ln_rstd[which], 1)

            def q_normed(i, n):
                pool.wait_ge(q_rden, i * NT_ + n + 1)
                v = e_buf[:, (n % 4) * 512:(n % 4 + 1) * 512].rearrange("p (h d) -> p h d", h=LH)
                tt(v, v, qrden[:, n % 2, :].unsqueeze(2).to_broadcast([P, LH, LD]),
                   ALU.mult).then_inc(q_norm, 1)

            def x3_norm(i, t):
                if t == 0:
                    pool.wait_ge(ln_nmr[2], i)
                    pool.sem_inc(x3_begun, 1)
                nc.gpsimd.tensor_scalar(x2[:, t, :], x2[:, t, :], rstd[:, 2, t:t + 1], nmr[:, 2, t:t + 1],
                                        ALU.mult, ALU.add).then_inc(ln_done[2], 1)

            def linear(i, nxt):
                ahead = {4: lambda: xt_split_lo(nxt, 0, [0]), 5: lambda: xt_split_lo(nxt, 0, [1]),
                         6: lambda: c_split_lo(nxt, 0, [0]), 7: lambda: c_split_lo(nxt, 0, [1]),
                         10: lambda: c_split_lo(nxt, 1, [0]), 11: lambda: c_split_lo(nxt, 1, [1]),
                         13: lambda: c_split_lo(nxt, 2, [0]), 14: lambda: c_split_lo(nxt, 2, [1]),
                         15: lambda: xv_make(nxt, 0, [0]), 16: lambda: xv_make(nxt, 0, [1]),
                         20: lambda: (c_split_lo(nxt, 3), xv_split_lo(nxt, 0))}
                for s in range(3, NT_ + 5):
                    q, a = divmod(s - 6, 2)
                    if a == 0 and 0 <= q < NT_ // 2:
                        pool.wait_ge(y_guard, i * (NT_ // 2) + q + 1)
                        tt(yr[:, q % 2, :], yssm[:], minus_half[:], ALU.pow).then_inc(y_r, 1)
                    if s == 8:
                        x1_split_lo(i, 3)
                    if 2 <= s - 1 < NT_:
                        q_normed(i, s - 1)
                    if nxt is not None and s in ahead:
                        ahead[s]()
                root(i, 1)

            def heads(i, ffn):
                xt_split_lo(i, 1)
                ct_split_lo(i, 0)
                xv_make(i, 1)
                for c in range(1, CH):
                    ct_split_lo(i, c)
                xv_split_lo(i, 1)
                for h in (2, 3):
                    xt_split_lo(i, h)
                    xv_make(i, h)
                    xv_split_lo(i, h)
                if ffn:
                    root(i - 1, 2)
                root(i, 0)
                if ffn:
                    x3_norm(i, 0)
                x1_split_lo(i, 0)
                if ffn:
                    x3_norm(i, 1)
                x1_split_lo(i, 1)
                q_normed(i, 0)
                q_normed(i, 1)
                x1_split_lo(i, 2)

            def first():
                xt_split_lo(0, 0)
                for c in range(CH):
                    c_split_lo(0, c)
                    if c == 2:
                        pool.wait_ge(vb_ready, 1)
                        xv_make(0, 0)
                xv_split_lo(0, 0)

            def rest(i):
                root(i - 1, 2)
                x3_norm(i, 0)
                x3_norm(i, 1)

            rounds(mybir.EngineType.Pool, first, heads, linear, rest)

        @block.vector
        def _(dve):
            v = nc.vector
            done = [0]

            def link(ins):
                done[0] += 1
                ins.then_inc(setup_dve, 1)
                dve.wait_ge(setup_dve, done[0])

            def split(dst, src, k, sign=1.0):
                s3 = src.rearrange("p (k n) -> p k n", k=k)
                if sign != 1.0:
                    link(v.tensor_scalar(s3, s3, sign, None, ALU.mult))
                link(v.tensor_copy(dst[:, :, HI, :], s3))
                link(v.tensor_tensor(dst[:, :, LO, :], s3, dst[:, :, HI, :].bitcast(F32), ALU.subtract))

            def alpha_and_dcol():
                dve.wait_ge(abs_summed, 1)
                link(v.tensor_reduce(alpha[:], ps[7][:, 0:3 * NT_].rearrange("p (v h k) -> p v h k", v=3, h=H),
                                     AX.X, ALU.add))
                link(v.tensor_scalar(alpha[:], alpha[:], 1.0 / HD, None, ALU.mult))
                w, tmp = cols[:, 0:2, :], cols_tmp[:, 0:2, :]
                link(v.tensor_scalar(tmp, w, 0.0, None, ALU.is_ge))
                link(v.tensor_scalar(tmp, tmp, 2.0, -1.0, ALU.mult, ALU.add))
                for k in range(2):
                    t4 = cols_tmp[:, k, :].rearrange("p (h k) -> p h k", h=H)
                    link(v.tensor_tensor(t4, t4, alpha[:, k, :].unsqueeze(2).to_broadcast([P, H, DT_]), ALU.mult))
                link(v.tensor_tensor(tmp, tmp, w, ALU.subtract))
                link(v.tensor_tensor(w, tmp, w, ALU.add))
                link(v.tensor_tensor(dcol[:], cols[:, 0, :], cols[:, 1, :], ALU.mult))

            def v_bind():
                dve.wait_ge(vb_loaded, 16)
                tmp = e_buf[:]
                link(v.tensor_scalar(tmp, vb[:], 0.0, None, ALU.is_ge))
                link(v.tensor_scalar(tmp, tmp, 2.0, -1.0, ALU.mult, ALU.add))
                for h in range(H):
                    c5 = slice(h * HD, (h + 1) * HD)
                    link(v.scalar_tensor_tensor(tmp[:, c5], tmp[:, c5], alpha[:, 2, h:h + 1], vb[:, c5], ALU.mult,
                                                ALU.subtract))
                link(v.tensor_tensor(vb[:], tmp, vb[:], ALU.add))
                dve.sem_inc(vb_ready, 1)

            def wk_split():
                dve.wait_ge(wk_loaded, 16)
                split(wk, w_staged, CT_, -1.0)
                dve.sem_inc(wk_ready, 1)

            def late_split():
                dve.wait_ge(late_loaded, 16 * 7)
                split(wq, w_staged, CT_, -1.0)
                split(ar, ar_staged, NT_)
                link(v.tensor_copy(b2[:], x2[:, 1, :]))
                link(v.tensor_tensor(b2[ER:P, :], x2[ER:P, 1, :], b2[ER:P, :].bitcast(F32), ALU.subtract))
                link(v.tensor_scalar(bo8[:], bo8[:], 1.0 / LH, None, ALU.mult))
                link(v.tensor_scalar(g16[:], g16[:], float(T) ** 0.5, None, ALU.mult))
                dve.sem_inc(weights_ready, 1)

            def xt_split_d(i, h, halves=range(2)):
                dve.wait_ge(*raw_arrived(i, "xt", h))
                for half in halves:
                    if not (isinstance(i, int) and i == 0 and h == 0):
                        if half == 0:
                            dve.wait_ge(qk_half, i * H + h)
                        elif h > 0:
                            dve.wait_ge(*full(i, "qk", h - 1))
                        else:
                            dve.wait_ge(bank_full[bank_of("qk", 3)], use_before(i, "qk", 3))
                    for dt in range(2):
                        src = raw_slot("xt", h)[:, half * 512 + dt * T:half * 512 + (dt + 1) * T]
                        col = h * DT_ + half * 2 + dt
                        v.tensor_scalar(xd_part[:, half, HI, dt, :], src, dcol[:, col:col + 1], None,
                                        ALU.mult).then_inc(xt_dhi, 1)
                    for dt in range(2):
                        src = raw_slot("xt", h)[:, half * 512 + dt * T:half * 512 + (dt + 1) * T]
                        col = h * DT_ + half * 2 + dt
                        dve.wait_ge(xt_dhi, i * 16 + (2 * h + half) * 2 + dt + 1)
                        last = v.scalar_tensor_tensor(xd_part[:, half, LO, dt, :], src, dcol[:, col:col + 1],
                                                      xd_part[:, half, HI, dt, :].bitcast(F32), ALU.mult,
                                                      ALU.subtract)
                    last.then_inc(xt_d, 1)

            def probs(i, h):
                dve.wait_ge(*freed(i, "qk", h))
                v.scalar_tensor_tensor(prob[:], prob[:], 1.0, halfmask[:], ALU.add,
                                       ALU.mult).then_inc(prob_step, 1)
                dve.wait_ge(prob_step, i * 2 * H + 2 * h + 1)
                if h > 0:
                    dve.wait_ge(*full(i, "av", h - 1, 1))
                v.tensor_copy(prob_part[:, HI, :, :], prob[:]).then_inc(prob_step, 1)
                dve.wait_ge(prob_step, i * 2 * H + 2 * h + 2)
                v.tensor_tensor(prob_part[:, LO, :, :], prob[:], prob_part[:, HI, :, :].bitcast(F32),
                                ALU.subtract).then_inc(prob_ready, 1)

            def x2t_lo_parts(i, j):
                dve.wait_ge(x2t_hi, (i - 1) * 8 + j + 1)
                v.tensor_tensor(t_part[:, j % 2, LO, :], bank("x2t", j)[:, :],
                                t_part[:, j % 2, HI, :].bitcast(F32),
                                ALU.subtract).then_inc(bank_free[bank_of("x2t", j)], 1)

            def key_min(i, h, c):
                dve.wait_ge(*full(i, "k", h, c))
                v.tensor_reduce(kmax4[:, c:c + 1], bank("k", h, c)[:, :], AX.X, ALU.min).then_inc(kmax_step, 1)
                if c == KEY_ORDER[h][-1]:
                    dve.wait_ge(kmax_step, i * 16 + h * 4 + 4)
                    v.tensor_reduce(knmax[:], kmax4[:], AX.X, ALU.min).then_inc(kmax_ready, 1)

            def key_sum(i, h):
                dve.wait_ge(*freed(i, "k", h, 3))
                if h > 0:
                    dve.wait_ge(*freed(i, "g", h - 1))
                v.tensor_reduce(kden[:], kden4[:], AX.X, ALU.add).then_inc(kden_step, 1)
                dve.wait_ge(kden_step, i * 8 + h * 2 + 1)
                v.reciprocal(krden[:], kden[:]).then_inc(kden_step, 1)
                dve.wait_ge(kden_step, i * 8 + h * 2 + 2)
                v.tensor_scalar(krden[:], krden[:], LD ** -0.5, None, ALU.mult).then_inc(krden_ready, 1)

            def et_lo_parts(i, h, c):
                dve.wait_ge(et_hi, i * 16 + h * 4 + c + 1)
                v.tensor_tensor(t_part[:, c % 2, LO, :], bank("et", h, c)[:, :],
                                t_part[:, c % 2, HI, :].bitcast(F32),
                                ALU.subtract).then_inc(bank_free[bank_of("et", h, c)], 1)

            def cx_mask(i, h):
                dve.wait_ge(*full(i, "mt", h, 1))
                v.tensor_tensor(cx[:], bank("mt", h, 1)[:, 0:P], pairmask[:],
                                ALU.mult).then_inc(bank_free[bank_of("mt", h)], 1)

            def m_add(i, h):
                dve.wait_ge(*full(i, "mt", h, 2))
                v.tensor_tensor(msum, bank("mt", h, 2)[:, 0:T], bo8[:],
                                ALU.add).then_inc(bank_free[bank_of("mt", h)], 1)

            def m_lo_part(i, h):
                dve.wait_ge(m_hi, i * OT_ + h + 1)
                v.tensor_tensor(m_part[:, h, LO, :], msum, m_part[:, h, HI, :].bitcast(F32),
                                ALU.subtract).then_inc(m_lo, 1)

            def residual(i, h, tiles=range(CT_)):
                cols = slice(h * HD, (h + 1) * HD)
                for t in tiles:
                    dve.wait_ge(*full(i, "av", h, t))
                    v.tensor_tensor(xa[:, t, cols], xa[:, t, cols], bank("av", h, t)[:, :],
                                    ALU.add).then_inc(bank_free[bank_of("av", h, t)], 1)

            def residual_stats(i, h):
                for t in range(CT_):
                    dve.wait_ge(*freed(i, "av", h, t))
                    v.bn_stats(stats[:, 0, t, h, :], xa[:, t, h * HD:(h + 1) * HD]).then_inc(ln_stats[0], 1)

            def ln_prepare(r, w):
                dve.wait_ge(ln_stats[w], r * 10 + 8)
                v.memset(ln_gate[:], 0.0)
                for t in range(CT_):
                    v.bn_aggr(mv[:, w, t, :], stats[:, w, t, :, :].rearrange("p c s -> p (c s)")).then_inc(
                        ln_stats[w], 1)
                dve.wait_ge(ln_stats[w], r * 10 + 10)
                v.tensor_scalar(ve[:, w, :], mv[:, w, :, 1], LN_EPS, None, ALU.add).then_inc(ln_var[w], 1)

            def ln_finish(r, w):
                dve.wait_ge(ln_rstd[w], r + 1)
                v.scalar_tensor_tensor(nmr[:, w, :], mv[:, w, :, 0], -1.0, rstd[:, w, :], ALU.mult,
                                       ALU.mult).then_inc(ln_nmr[w], 1)
                dve.wait_ge(ln_nmr[w], r + 1)

            def ln_apply(buf, w, t, cols):
                v.tensor_scalar(buf[:, t, cols], buf[:, t, cols], rstd[:, w, t:t + 1], nmr[:, w, t:t + 1],
                                ALU.mult, ALU.add).then_inc(ln_done[w], 1)

            def gates(i):
                r = i - 1
                n = [0]

                def step(ins):
                    n[0] += 1
                    ins.then_inc(gate_step, 1)
                    dve.wait_ge(gate_step, r * 8 + n[0])

                dve.wait_ge(*freed(i, "midt"))
                logits = md[:, :, ER:ARW]
                step(v.tensor_reduce(gmax[:], logits, AX.X, ALU.max))
                v.tensor_tensor(gdif[:], logits, gmax[:].unsqueeze(2).to_broadcast([P, CT_, E]),
                                ALU.subtract).then_inc(gate_diff, 1)
                other = logits.unsqueeze(2).to_broadcast([P, CT_, E, E])
                own = logits.unsqueeze(3).to_broadcast([P, CT_, E, E])
                step(v.tensor_tensor(geq[:], other, own, ALU.is_equal))
                for t in range(CT_):
                    v.tensor_tensor(geq[:, t, :, :], geq[:, t, :, :], before[:], ALU.mult).then_inc(gate_order, 1)
                dve.wait_ge(gate_order, r * 2 + 2)
                step(v.tensor_tensor(ggt[:], other, own, ALU.is_gt))
                step(v.tensor_tensor(ggt[:], ggt[:], geq[:], ALU.add))
                step(v.tensor_reduce(grank[:], ggt[:], AX.X, ALU.add))
                dve.wait_ge(gate_exp, i)
                step(v.scalar_tensor_tensor(gexp[:], grank[:], TOP_K - 0.5, gexp[:], ALU.is_lt, ALU.mult))
                step(v.tensor_reduce(gsum[:], gexp[:], AX.X, ALU.add))
                step(v.reciprocal(gsum[:], gsum[:]))
                assert n[0] == 8

            def gate_mid(i):
                r = i - 1
                v.tensor_tensor(gdif[:], gexp[:], gsum[:].unsqueeze(2).to_broadcast([P, CT_, E]),
                                ALU.mult).then_inc(gate_norm, 1)
                dve.wait_ge(gate_norm, r + 1)
                for t in range(CT_):
                    for a in range(2):
                        v.scalar_tensor_tensor(gated[:, t, a, :].rearrange("p (e r) -> p e r", e=E),
                                               md[:, t, 0:ER].rearrange("p (e r) -> p e r", e=E), LORA_SCALE,
                                               gdif[:, t, :].unsqueeze(2).to_broadcast([P, E, R]),
                                               ALU.mult, ALU.mult).then_inc(gated_ready, 1)

            def gated_lo_part(i):
                dve.wait_ge(gated_hi, i)
                v.tensor_tensor(gated_part[:, LO, :, :].rearrange("p t n -> p (t n)"), bank("gated")[:, 0:T],
                                gated_part[:, HI, :, :].rearrange("p t n -> p (t n)").bitcast(F32),
                                ALU.subtract).then_inc(bank_free[bank_of("gated", 0)], 1)

            def ffn_add(i, k):
                t, c = divmod(k, CH)
                cols = slice(c * 512, (c + 1) * 512)
                dve.wait_ge(*full(i, "delta", k))
                v.tensor_tensor(x2[:, t, cols], x2[:, t, cols], bank("delta", k)[:, :],
                                ALU.add).then_inc(bank_free[bank_of("delta", k)], 1)

            def ffn_stats(i, k):
                t, c = divmod(k, CH)
                dve.wait_ge(*freed(i, "delta", k))
                v.bn_stats(stats[:, 2, t, c, :], x2[:, t, c * 512:(c + 1) * 512]).then_inc(ln_stats[2], 1)

            def q_min_sub(i, s, between=None):
                dve.wait_ge(*full(i, "q", s))
                src = bank("q", s)[:, :].rearrange("p (h d) -> p h d", h=LH)
                v.tensor_reduce(qmin[:, s % 2, :], src, AX.X, ALU.min).then_inc(q_min, 1)
                if between is not None:
                    between()
                dve.wait_ge(q_min, i * NT_ + s + 1)
                if s >= 4:
                    dve.wait_ge(*full(i, "qt", s - 4))
                else:
                    dve.wait_ge(*full(i, "et", 3, s))
                v.tensor_tensor(e_buf[:, (s % 4) * 512 + AH * LD:(s % 4 + 1) * 512].rearrange(
                                    "p (h d) -> p h d", h=LH - AH), src[:, AH:LH, :],
                                qmin[:, s % 2, AH:LH].unsqueeze(2).to_broadcast([P, LH - AH, LD]),
                                ALU.subtract).then_inc(q_sub, 1)

            def q_sums(i, n):
                dve.wait_ge(q_exp, i * NT_ + n + 1)
                v.tensor_reduce(qden[:, n % 2, AH:LH],
                                e_buf[:, (n % 4) * 512 + AH * LD:(n % 4 + 1) * 512].rearrange(
                                    "p (h d) -> p h d", h=LH - AH), AX.X, ALU.add).then_inc(q_sum, 1)

            def q_factors(i, n):
                dve.wait_ge(q_sum, i * NT_ + n + 1)
                if n >= 2:
                    dve.wait_ge(q_norm, i * NT_ + n - 1)
                v.reciprocal(qrden[:, n % 2, :], qden[:, n % 2, :]).then_inc(q_rden, 1)

            def x2_norm(i, c):
                ln_apply(x2, 1, 0, slice(c * 512, (c + 1) * 512))

            def linear(i, nxt):
                ahead = {4: lambda: xt_split_d(nxt, 0, [0]), 5: lambda: xt_split_d(nxt, 0, [1])}
                for s in range(3, NT_ + 9):
                    def between():
                        q, a = divmod(s - 6, 2)
                        if a == 0 and 0 <= q < NT_ // 2:
                            dve.wait_ge(y_square, i * NT_ + 2 * q + 2)
                            if q > 0:
                                dve.wait_ge(y_r, i * (NT_ // 2) + q)
                            v.tensor_scalar(yssm[:], yss[:, q % 2, :], 1e-24, None, ALU.max).then_inc(y_guard, 1)
                        if s - 1 < NT_:
                            q_sums(i, s - 1)

                    if s == 3:
                        cx_mask(i, 3)
                    if s < NT_:
                        q_min_sub(i, s, between)
                    else:
                        between()
                    if s - 1 < NT_:
                        q_factors(i, s - 1)
                    if s == 3:
                        m_add(i, 3)
                    n = s - 3
                    if 0 <= n < NT_:
                        dve.wait_ge(qt_hi, i * NT_ + n + 1)
                        v.tensor_tensor(t_part[:, n % 2, LO, :], bank("qt", n)[:, :],
                                        t_part[:, n % 2, HI, :].bitcast(F32),
                                        ALU.subtract).then_inc(bank_free[bank_of("qt", n)], 1)
                    if s == 3:
                        m_lo_part(i, 3)
                    q, a = divmod(s - 10, 2)
                    if a == 0 and 0 <= q < NT_ // 2 and q % 2 == 1:
                        c = q // 2
                        dve.wait_ge(*freed(i, "yt", q))
                        for t in range(CT_):
                            v.bn_stats(stats[:, 1, t, c, :], x2[:, t, c * 512:(c + 1) * 512]).then_inc(
                                ln_stats[1], 1)
                    q, a = divmod(s - 9, 2)
                    if q == NT_ // 2 - 1 and a == 0 and nxt is not None:
                        xt_split_d(nxt, 1)
                        probs(nxt, 0)
                    if a == 0 and 0 <= q < NT_ // 2:
                        cols = slice(q * T, (q + 1) * T)
                        dve.wait_ge(*full(i, "yt", q))
                        v.scalar_tensor_tensor(x2[:, 0, cols], bank("yt", q)[:, 0:T], g16[:, 0:1], xa[:, 0, cols],
                                               ALU.mult, ALU.add)
                        v.scalar_tensor_tensor(x2[:, 1, cols], bank("yt", q)[:, T:2 * T], g16[:, 1:2],
                                               xa[:, 1, cols], ALU.mult,
                                               ALU.add).then_inc(bank_free[bank_of("yt", q)], 1)
                    if nxt is not None and s in ahead:
                        ahead[s]()
                ln_prepare(i, 1)

            def heads(i, ffn):
                key_min(i, 0, 0)
                if ffn:
                    ln_finish(i - 1, 1)
                    x2_norm(i, 0)
                residual(i, 0)
                if ffn:
                    x2_norm(i, 1)
                    x2t_lo_parts(i, 0)
                    x2_norm(i, 2)
                    x2t_lo_parts(i, 1)
                    x2_norm(i, 3)
                if ffn:
                    x2t_lo_parts(i, 2)
                    x2t_lo_parts(i, 3)
                key_min(i, 0, 1)
                if ffn:
                    x2t_lo_parts(i, 4)
                key_min(i, 0, 2)
                if ffn:
                    x2t_lo_parts(i, 5)
                key_min(i, 0, 3)
                if ffn:
                    x2t_lo_parts(i, 6)
                    x2t_lo_parts(i, 7)
                residual_stats(i, 0)
                key_sum(i, 0)
                et_lo_parts(i, 0, 0)
                et_lo_parts(i, 0, 1)
                if not ffn:
                    late_split()
                if ffn:
                    gates(i)
                    gate_mid(i)
                et_lo_parts(i, 0, 2)
                et_lo_parts(i, 0, 3)
                probs(i, 1)
                xt_split_d(i, 2)
                key_min(i, 1, 0)
                if ffn:
                    gated_lo_part(i)
                key_min(i, 1, 1)
                cx_mask(i, 0)
                if ffn:
                    ffn_add(i, 0)
                key_min(i, 1, 2)
                m_add(i, 0)
                if ffn:
                    ffn_add(i, 1)
                    ffn_stats(i, 0)
                key_min(i, 1, 3)
                if ffn:
                    ffn_add(i, 2)
                    ffn_add(i, 3)
                m_lo_part(i, 0)
                residual(i, 1)
                et_lo_parts(i, 1, 0)
                et_lo_parts(i, 1, 1)
                key_sum(i, 1)
                residual_stats(i, 1)
                if ffn:
                    ffn_stats(i, 1)
                probs(i, 2)
                et_lo_parts(i, 1, 2)
                et_lo_parts(i, 1, 3)
                xt_split_d(i, 3)
                if ffn:
                    ffn_stats(i, 2)
                    ffn_stats(i, 3)
                residual(i, 2)
                residual_stats(i, 2)
                probs(i, 3)
                for c in range(CH):
                    key_min(i, 2, c)
                    if c == 1:
                        cx_mask(i, 1)
                    if c == 2:
                        m_add(i, 1)
                    if ffn and c > 0:
                        ffn_add(i, 3 + c)
                        if c < 3:
                            ffn_stats(i, 3 + c)
                if ffn:
                    ffn_add(i, 7)
                m_lo_part(i, 1)
                if ffn:
                    ffn_stats(i, 6)
                    ffn_stats(i, 7)
                    ln_prepare(i - 1, 2)
                et_lo_parts(i, 2, 0)
                et_lo_parts(i, 2, 1)
                key_sum(i, 2)
                residual(i, 3)
                key_min(i, 3, 0)
                residual_stats(i, 3)
                key_min(i, 3, 2)
                key_min(i, 3, 3)
                ln_prepare(i, 0)
                key_min(i, 3, 1)
                et_lo_parts(i, 2, 2)
                if ffn:
                    ln_finish(i - 1, 2)
                ln_finish(i, 0)
                for c in range(CH):
                    for t in range(CT_):
                        ln_apply(xa, 0, t, slice(c * 512, (c + 1) * 512))
                    if c == 0:
                        et_lo_parts(i, 2, 3)
                    elif c == 2:
                        et_lo_parts(i, 3, 0)
                key_sum(i, 3)
                et_lo_parts(i, 3, 1)
                et_lo_parts(i, 3, 2)
                q_min_sub(i, 0)
                cx_mask(i, 2)
                q_sums(i, 0)
                et_lo_parts(i, 3, 3)
                q_factors(i, 0)
                q_min_sub(i, 1)
                m_add(i, 2)
                q_sums(i, 1)
                m_lo_part(i, 2)
                q_factors(i, 1)
                q_min_sub(i, 2)
                if ffn:
                    dve.wait_ge(stored, i * 16 * CT_)

            def first():
                alpha_and_dcol()
                xt_split_d(0, 0)
                wk_split()
                v_bind()
                xt_split_d(0, 1)
                probs(0, 0)

            def rest(i):
                ln_finish(i - 1, 1)
                for c in range(CH):
                    x2_norm(i, c)
                for j in range(8):
                    x2t_lo_parts(i, j)
                gates(i)
                gate_mid(i)
                gated_lo_part(i)
                for k in range(8):
                    ffn_add(i, k)
                    if k > 0:
                        ffn_stats(i, k - 1)
                ffn_stats(i, 7)
                ln_prepare(i - 1, 2)
                ln_finish(i - 1, 2)

            dve.wait_ge(ident_made, 2)
            rounds(mybir.EngineType.DVE, first, heads, linear, rest)


def kernel(x, ctx_4096, L0_attn_bv_q, L0_attn_bv_k, L0_attn_bv_v, L0_xattn_Wq, L0_xattn_Wk, L0_xattn_Wv,
           L0_xattn_Wo, L0_xattn_bo, L0_xattn_g, L0_ffn_router_w, L0_ffn_A, L0_ffn_B):
    import concourse.bacc as bacc
    from concourse.bass_utils import run_bass_kernel_spmd

    def rows(v):
        return np.broadcast_to(np.asarray(v).reshape(1, -1), (P, np.asarray(v).size))

    def tiles(w, n):
        return np.asarray(w).reshape(n, P, -1).transpose(1, 0, 2).reshape(P, -1)

    def chunks(a):
        return np.asarray(a).reshape(B, CT_, P, CH, 512).transpose(0, 3, 2, 1, 4).reshape(B, CH, P, CT_ * 512)

    def turned(a):
        return np.asarray(a).transpose(0, 2, 1).reshape(B, CH, 4, P, T).transpose(0, 1, 3, 2, 4).reshape(
            B, CH, P, 4 * T)

    a_rows = np.concatenate([np.asarray(L0_ffn_A).reshape(ER, D), np.asarray(L0_ffn_router_w)], 0)
    b_rows = np.asarray(L0_ffn_B).transpose(0, 2, 1).reshape(ER, D)
    arrays = {
        "x": chunks(x), "xt": turned(x), "ctx": chunks(ctx_4096), "ctxt": turned(ctx_4096),
        "bv_v": rows(L0_attn_bv_v), "b_cols": np.concatenate(
            [np.asarray(b).reshape(NT_, P).T for b in (L0_attn_bv_q, L0_attn_bv_k, L0_attn_bv_v)], 1),
        "wqt": tiles(np.asarray(L0_xattn_Wq).T, CT_), "wkt": tiles(np.asarray(L0_xattn_Wk).T, CT_),
        "wvt": tiles(np.asarray(L0_xattn_Wv).T, CT_), "wot": tiles(np.asarray(L0_xattn_Wo).T, OT_),
        "bo": rows(L0_xattn_bo), "g": np.asarray(L0_xattn_g).reshape(CT_, P).T,
        "art": tiles(a_rows.T, NT_), "bt": np.concatenate([b_rows, b_rows], 0),
    }
    arrays = {f"in_{k}": np.ascontiguousarray(a) for k, a in arrays.items()}
    nc = bacc.Bacc("TRN2", target_bir_lowering=False, num_devices=1, dynamic_dma_scratch_size=1024)
    args = [nc.dram_tensor(k, a.shape, mybir.dt.from_np(a.dtype), kind="ExternalInput").ap()
            for k, a in arrays.items()]
    args.append(nc.dram_tensor("out", (B, CT_, P, D), F32, kind="ExternalOutput").ap())
    build(nc, *args)
    done = run_bass_kernel_spmd(nc, [arrays], core_ids=[0])
    return done.results[0]["out"].reshape(B, T, D)
```
